# Optimizing a Trainium2 kernel written in Bass

```python
import numpy as np
import jax
import jax.numpy as jnp

def _softmax(x, axis=-1):
    return jax.nn.softmax(x, axis=axis)

def _gelu(x):
    return jax.nn.gelu(x, approximate=True)

def _silu(x):
    return jax.nn.silu(x)

def _sigmoid(x):
    return jax.nn.sigmoid(x)

def _layernorm(x, axis=-1, eps=1e-05):
    m = jnp.mean(x, axis=axis, keepdims=True)
    v = jnp.var(x, axis=axis, keepdims=True)
    return (x - m) / jnp.sqrt(v + eps)

def _scatter_add(tgt, idx, src, axis=0):
    return tgt.at[idx].add(src)

def _segment_sum(src, seg, n):
    return jax.ops.segment_sum(src, seg, n)
kernel_name = 'mk_gnn_ffn_d2_gnn_r8_407905'

def setup_inputs(seed: int=0):
    np.random.seed(seed)
    _w = jnp.asarray

    def _rec_inputs():
        import jax
        import jax.numpy as jnp
        _gk = jax.random.key(seed)
        x = -0.0002928 + 1 * jax.random.normal(jax.random.fold_in(_gk, 1), (1024, 512), jnp.float32)
        src = jax.random.randint(jax.random.fold_in(_gk, 2), (32768,), 0, 1024, jnp.int32)
        dst = jax.random.randint(jax.random.fold_in(_gk, 3), (32768,), 0, 1024, jnp.int32)
        _o = jnp.argsort(dst, stable=True)
        src = src[_o]
        dst = dst[_o]
        return (x, src, dst)
    x, src, dst = _rec_inputs()

    def _L0_gnn_setup():
        import jax, jax.numpy as jnp
        import numpy as np
        N_NODES = 1024
        N_EDGES = 32768
        D_IN = 512
        D_OUT = 512
        key = jax.random.key(seed)
        k1, k2, k3 = jax.random.split(key, 3)
        x = jax.random.normal(k1, (N_NODES, D_IN), dtype=jnp.float32)
        edge_index = jax.random.randint(k2, (2, N_EDGES), 0, N_NODES, dtype=jnp.int64)
        weight = jax.random.normal(k3, (D_IN, D_OUT), dtype=jnp.float32)
        bias = jnp.zeros((D_OUT,), dtype=jnp.float32)
        return {'x': x, 'edge_index': edge_index, 'weight': weight, 'bias': bias}
    _L0_gnn_all = _L0_gnn_setup()
    _L0_gnn_in = {k: v for k, v in _L0_gnn_all.items() if k in ('weight', 'bias')}
    del _L0_gnn_all

    def _L0_ffn_setup():
        import jax, jax.numpy as jnp
        import numpy as np
        S, B, D, F, E, K = (1024, 2, 512, 256, 8, 2)
        key = jax.random.key(seed)
        ks = jax.random.split(key, 12)
        s = lambda *sh: 1.0 / np.sqrt(sh[0])
        inp = {'x': jax.random.normal(ks[0], (S, B, D), dtype=jnp.float32), 'Wg': jax.random.normal(ks[1], (D, E), dtype=jnp.float32) * s(D), 'bg': jnp.zeros((E,), dtype=jnp.float32), 'W1': jax.random.normal(ks[2], (E, D, F), dtype=jnp.float32) * s(D), 'b1': jnp.zeros((E, F), dtype=jnp.float32), 'W2': jax.random.normal(ks[3], (E, F, D), dtype=jnp.float32) * s(F), 'b2': jnp.zeros((E, D), dtype=jnp.float32), 'Ws1': jax.random.normal(ks[4], (D, F), dtype=jnp.float32) * s(D), 'bs1': jnp.zeros((F,), dtype=jnp.float32), 'Ws2': jax.random.normal(ks[5], (F, D), dtype=jnp.float32) * s(F), 'bs2': jnp.zeros((D,), dtype=jnp.float32)}
        return inp
    _L0_ffn_all = _L0_ffn_setup()
    _L0_ffn_in = {k: v for k, v in _L0_ffn_all.items() if k in ('Wg', 'bg', 'W1', 'b1', 'W2', 'b2', 'Ws1', 'bs1', 'Ws2', 'bs2')}
    del _L0_ffn_all

    def _L1_gnn_setup():
        import jax, jax.numpy as jnp
        import numpy as np
        N_NODES = 2500
        N_EDGES = 18750
        IN_C = 512
        OUT_C = 512
        K_INIT = 7

        def _spmm(row, col, lap, x, num_nodes):
            msgs = lap[:, None] * x[col]
            return jax.ops.segment_sum(msgs, row, num_segments=num_nodes)
        key = jax.random.key(seed)
        k1, k2, k3, k4 = jax.random.split(key, 4)
        x = jax.random.normal(k1, (N_NODES, IN_C), dtype=jnp.float32)
        edge_index = jax.random.randint(k2, (2, N_EDGES), 0, N_NODES, dtype=jnp.int32)
        bound = 1.0 / np.sqrt(IN_C * (K_INIT + 1))
        weight = jax.random.uniform(k3, (K_INIT + 1, IN_C, OUT_C), dtype=jnp.float32, minval=-bound, maxval=bound)
        bias = jax.random.uniform(k4, (OUT_C,), dtype=jnp.float32, minval=-bound, maxval=bound)
        return {'x': x, 'edge_index': edge_index, 'weight': weight, 'bias': bias}
    _L1_gnn_all = _L1_gnn_setup()
    _L1_gnn_in = {k: v for k, v in _L1_gnn_all.items() if k in ('weight', 'bias')}
    del _L1_gnn_all

    def _L1_ffn_setup():
        import jax, jax.numpy as jnp
        import numpy as np
        FP8_MAX = 448.0
        K, N = (512, 512)
        key = jax.random.key(seed)
        kx, kw = jax.random.split(key)
        x = jax.random.normal(kx, (8, 1024, K), dtype=jnp.float32)
        weight = jax.random.normal(kw, (K, N), dtype=jnp.float32) * 0.02
        return {'x': x, 'weight': weight}
    _L1_ffn_all = _L1_ffn_setup()
    _L1_ffn_in = {k: v for k, v in _L1_ffn_all.items() if k in ('weight',)}
    del _L1_ffn_all
    return {'x': x, 'src': src, 'dst': dst, 'L0_gnn_weight': _L0_gnn_in['weight'], 'L0_gnn_bias': _L0_gnn_in['bias'], 'L0_ffn_Wg': _L0_ffn_in['Wg'], 'L0_ffn_bg': _L0_ffn_in['bg'], 'L0_ffn_W1': _L0_ffn_in['W1'], 'L0_ffn_b1': _L0_ffn_in['b1'], 'L0_ffn_W2': _L0_ffn_in['W2'], 'L0_ffn_b2': _L0_ffn_in['b2'], 'L0_ffn_Ws1': _L0_ffn_in['Ws1'], 'L0_ffn_bs1': _L0_ffn_in['bs1'], 'L0_ffn_Ws2': _L0_ffn_in['Ws2'], 'L0_ffn_bs2': _L0_ffn_in['bs2'], 'L1_gnn_weight': _L1_gnn_in['weight'], 'L1_gnn_bias': _L1_gnn_in['bias'], 'L1_ffn_weight': _L1_ffn_in['weight']}

def reference(x, src, dst, L0_gnn_weight, L0_gnn_bias, L0_ffn_Wg, L0_ffn_bg, L0_ffn_W1, L0_ffn_b1, L0_ffn_W2, L0_ffn_b2, L0_ffn_Ws1, L0_ffn_bs1, L0_ffn_Ws2, L0_ffn_bs2, L1_gnn_weight, L1_gnn_bias, L1_ffn_weight):
    import jax
    import jax.numpy as jnp

    def _L0_gnn_ref(x, edge_index, weight, bias):
        import jax, jax.numpy as jnp
        import numpy as np
        N_NODES = 1024
        N_EDGES = 32768
        D_IN = 512
        D_OUT = 512
        n = x.shape[0]
        adj = jnp.zeros((n, n), dtype=x.dtype)
        adj = adj.at[edge_index[0], edge_index[1]].set(1.0)
        adj = adj.at[edge_index[1], edge_index[0]].set(1.0)
        adj = adj + jnp.eye(n, dtype=x.dtype)
        deg = jnp.sum(adj, axis=1)
        dinv = 1.0 / jnp.sqrt(deg)
        adj = adj * dinv[:, None] * dinv[None, :]
        return adj @ (x @ weight) + bias

    def _L0_ffn_ref(x, Wg, bg, W1, b1, W2, b2, Ws1, bs1, Ws2, bs2):
        import jax, jax.numpy as jnp
        import numpy as np
        S, B, D, F, E, K = (1024, 2, 512, 256, 8, 2)
        gate_logits = jnp.einsum('sbd,de->sbe', x, Wg) + bg
        weights, selected = jax.lax.top_k(gate_logits, K)
        weights = jax.nn.softmax(weights.astype(jnp.float32), axis=-1)
        onehot = jax.nn.one_hot(selected, E, dtype=weights.dtype)
        comb = jnp.einsum('sbk,sbke->sbe', weights, onehot)
        h = jax.nn.relu(jnp.einsum('sbd,edf->sbef', x, W1) + b1)
        y = jnp.einsum('sbef,efd->sbed', h, W2) + b2
        out = jnp.einsum('sbe,sbed->sbd', comb, y)
        hs = jax.nn.relu(jnp.einsum('sbd,df->sbf', x, Ws1) + bs1)
        shared = jnp.einsum('sbf,fd->sbd', hs, Ws2) + bs2
        out = out + 1.0 / K * shared
        return out

    def _L1_gnn_ref(x, edge_index, weight, bias):
        import jax, jax.numpy as jnp
        import numpy as np
        N_NODES = 2500
        N_EDGES = 18750
        IN_C = 512
        OUT_C = 512
        K_INIT = 7

        def _spmm(row, col, lap, x, num_nodes):
            msgs = lap[:, None] * x[col]
            return jax.ops.segment_sum(msgs, row, num_segments=num_nodes)
        row, col = (edge_index[0], edge_index[1])
        num_nodes = x.shape[0]
        Kw = weight.shape[0]
        deg = jax.ops.segment_sum(jnp.ones_like(row, dtype=x.dtype), row, num_segments=num_nodes)
        dinv = jnp.where(deg > 0, jax.lax.rsqrt(jnp.maximum(deg, 1e-30)), 0.0)
        lap = -dinv[row] * dinv[col]
        Tx_0 = x
        out = Tx_0 @ weight[0]
        Tx_1 = _spmm(row, col, lap, x, num_nodes)
        out = out + Tx_1 @ weight[1]
        for k in range(2, Kw):
            Tx_2 = 2.0 * _spmm(row, col, lap, Tx_1, num_nodes) - Tx_0
            out = out + Tx_2 @ weight[k]
            Tx_0, Tx_1 = (Tx_1, Tx_2)
        return out + bias

    def _L1_ffn_ref(x, weight):
        import jax, jax.numpy as jnp
        import numpy as np
        FP8_MAX = 448.0
        K, N = (512, 512)
        B, S, _ = x.shape
        x2d = x.reshape(-1, K)
        x_amax = jnp.max(jnp.abs(x2d))
        x_scale = FP8_MAX / jnp.maximum(x_amax, 1e-12)
        x_fp8 = jnp.clip(x2d * x_scale, -FP8_MAX, FP8_MAX).astype(jnp.float8_e4m3fn)
        w_amax = jnp.max(jnp.abs(weight))
        w_scale = FP8_MAX / jnp.maximum(w_amax, 1e-12)
        w_fp8 = jnp.clip(weight.T * w_scale, -FP8_MAX, FP8_MAX).astype(jnp.float8_e4m3fn)
        res = jnp.matmul(x_fp8.astype(jnp.float32), w_fp8.astype(jnp.float32).T)
        out = res * (1.0 / x_scale * (1.0 / w_scale))
        return out.reshape(B, S, N).astype(x.dtype)
    edge_index = jnp.stack([src, dst])
    x = x + _L0_gnn_ref(_layernorm(x, axis=-1), edge_index, L0_gnn_weight, L0_gnn_bias)
    x = x + _L0_ffn_ref(_layernorm(x, axis=-1)[None], L0_ffn_Wg, L0_ffn_bg, L0_ffn_W1, L0_ffn_b1, L0_ffn_W2, L0_ffn_b2, L0_ffn_Ws1, L0_ffn_bs1, L0_ffn_Ws2, L0_ffn_bs2)[0]
    x = x + _L1_gnn_ref(_layernorm(x, axis=-1), edge_index, L1_gnn_weight, L1_gnn_bias)
    x = x + _L1_ffn_ref(_layernorm(x, axis=-1)[None], L1_ffn_weight)[0]
    return x

_drawn_inputs = setup_inputs


def setup_inputs(seed=0):
    import zlib

    import numpy as np

    out = dict(_drawn_inputs(seed))
    spreads = {'L0_gnn_bias': (0.0, 0.1),
     'L0_ffn_bg': (0.0, 0.1),
     'L0_ffn_b1': (0.0, 0.463),
     'L0_ffn_b2': (0.0, 0.321),
     'L0_ffn_bs1': (0.0, 0.676),
     'L0_ffn_bs2': (0.0, 0.468)}
    factors = {'L1_gnn_bias': 8.0}
    for name, (base, spread) in spreads.items():
        noise = np.random.default_rng([zlib.crc32(name.encode()), seed]).standard_normal(out[name].shape)
        drawn = base * np.exp(spread * noise) if base else spread * noise
        out[name] = jnp.asarray(drawn.astype(out[name].dtype))
    for name, factor in factors.items():
        out[name] = (out[name] * factor).astype(out[name].dtype)
    return out
```

```python
from contextlib import ExitStack

import concourse.bass as bass
from concourse import mybir

F32 = mybir.dt.float32
F32R = mybir.dt.float32r
BF16 = mybir.dt.bfloat16
I32 = mybir.dt.int32
U32 = mybir.dt.uint32
ALU = mybir.AluOpType
ACT = mybir.ActivationFunctionType
AX_X = mybir.AxisListType.X
ABSMAX = bass.bass_isa.ReduceOp.absmax
MAX = bass.bass_isa.ReduceOp.max

P = 128
N = 1024
D = 512
NB = N // P
KD = D // P
E = 32768
PAIRS = E // (2 * P)
WD = 32
NW = N // WD
SH = P // WD
SL = N // SH
RING = 4
NE = 9
F = 256
FB = F // P
KC = 8
EPS = 1e-5
FP8_MAX = 448.0
EXACT = 4096
HALVES = N // 512

KB = 1024


def build(nc, x_in, src_in, dst_in, w0_in, bias0_in, wg_in, bg_in, w1_in, b1_in, w2_in, b2_in,
          wc_in, bias1_in, wf_in, out):
    ctx = ExitStack()
    with ctx:
        base = (nc.sbuf_base + 31) // 32 * 32

        def at(name, shape, dt, offset):
            return nc.alloc_sbuf_tensor_at(name, shape, dt, offset=base + int(offset * KB))

        def sem(name):
            return ctx.enter_context(nc.semaphore(name))

        AT = at("AT", [P, NB, N], F32R, 0)
        xT_hi = at("xT_hi", [P, KD, N], F32R, 32)
        xT_lo = at("xT_lo", [P, KD, N], F32R, 48)
        x = at("x", [P, NB, D], F32, 64)
        U = 80
        xh = at("xh", [P, 2, D], F32, 200)
        ident = at("ident", [P, P], F32, 204)
        identb = at("identb", [P, P], BF16, 204.5)
        stats = at("stats", [P, NB, 6], F32, 204.75)
        meanvar = at("meanvar", [P, 4, NB, 2], F32, 205)
        veps = at("veps", [P, 4, NB], F32, 205.25)
        rstd = at("rstd", [P, 4, NB], F32, 205.375)
        nhalf = at("nhalf", [P, NB], F32, 205.5)
        comb = at("comb", [P, NB, NE], F32, 205.5625)
        degs = at("degs", [P, 8, NB], F32, 205.875)
        rowsum, deg0, dinv0, deg1, dinv1, m2dinv1, ndinv1, degpos = (degs[:, i, :] for i in range(8))
        b1T = at("b1T", [P, NE * FB], F32, 206.125)
        few = at("few", [P, 32], F32, 206.25)
        bigflag = at("bigflag", [1, 1], I32, 206.375)
        wg_hilo = at("wg_hilo", [P, KD, 16], F32R, 206.5)
        wg_raw = at("wg_raw", [P, KD, 8], F32, 206.75)
        bgb = at("bgb", [P, 8], F32, 206.875)
        onecol = at("onecol", [P, 1], F32, 206.9375)
        b1cur = at("b1cur", [P, 2, FB], F32, 206.96875)
        iota8 = at("iota8", [P, 8], F32, 206.90625)

        S = at("S", [P, NB, N], F32R, U + 0)
        B = at("B", [P, NB, N], BF16, U + 32)
        y = at("y", [P, NB, D], F32, U + 48)
        y_hi = at("y_hi", [P, NB, D], F32R, U + 64)
        y_lo = at("y_lo", [P, NB, D], F32R, U + 80)
        w0_raw = at("w0_raw", [P, KD, D], F32, U + 96)
        w0_hi = at("w0_hi", [P, KD, D], F32R, U + 104)
        w0_lo = at("w0_lo", [P, KD, D], F32R, U + 112)
        src_i = at("src_i", [P, 2 * P], I32, U + 0)
        dst_i = at("dst_i", [P, 2 * P], I32, U + 1)
        shi_i = at("shi_i", [P, 2 * P], I32, U + 2)
        slo_i = at("slo_i", [P, 2 * P], I32, U + 3)
        joint = at("joint", [P, 2 * P], F32, U + 4)
        slo = at("slo", [P, 2 * P], F32, U + 5)
        idxT = at("idxT", [P, 4, PAIRS], F32, U + 6)
        stage = at("stage", [P, 4, SL], F32, U + 8)
        oh_row = at("oh_row", [P, RING, 2, P], BF16, U + 12)
        oh_col = at("oh_col", [P, RING, 2, SL], BF16, U + 14)
        iotab = at("iotab", [P, SL], BF16, U + 18)
        zerob = at("zerob", [P, P], BF16, U + 18.5)
        diag = at("diag", [P, 2, P], F32, U + 19)
        pairmm = at("pairmm", [P, 2], F32, U + 20)
        wstart = at("wstart", [NW, 2], F32, U + 20.0625)
        ones32 = at("ones32", [P, NW], F32, U + 20.125)
        tri = at("tri", [NW, NW + 1], F32, U + 20.25)
        iotap = at("iotap", [NW, 2, PAIRS], F32, U + 20.5)
        wmask = at("wmask", [NW, 2, PAIRS], F32, U + 21.5)
        wsel = at("wsel", [NW, 2, PAIRS], F32, U + 22.5)
        wcol = at("wcol", [NW, 4], F32, U + 23.5)
        tabf = at("tabf", [1, NW + 1], F32, U + 23.5625)
        tab = at("tab", [1, 3 * NW], I32, U + 23.75)
        wbase = at("wbase", [P, NW], F32, U + 24.25)
        bias0 = at("bias0", [P, D], F32, U + 26)
        w_hi = [[at(f"w{k + 1}_hi{i}", [P, KD, F] if k == 0 else [P, FB, D], F32R, U + (32, 16)[i] + 4 * k)
                 for k in range(2)] for i in range(2)]
        w_lo = [[at(f"w{k + 1}_lo{i}", [P, KD, F] if k == 0 else [P, FB, D], F32R, U + (32, 16)[i] + 8 + 4 * k)
                 for k in range(2)] for i in range(2)]
        w_raw = [[at(f"w{k + 1}_raw{i}", [P, KD, F] if k == 0 else [P, FB, D], F32, U + 96 + 8 * i + 4 * k)
                  for k in range(2)] for i in range(2)]
        h_hi = [at(f"h_hi{i}", [P, FB, N], F32R, U + 48 + 16 * i) for i in range(2)]
        h_lo = [at(f"h_lo{i}", [P, FB, N], F32R, U + 56 + 16 * i) for i in range(2)]
        hrelu = at("hrelu", [P, 2, 512], F32, U + 80)
        combT = at("combT", [NE, N], F32, U + 84)
        b2all = at("b2all", [NE, D], F32, U + 88)
        gate = at("gate", [P, NB, 8], F32, U + 90)
        top8 = at("top8", [P, NB, 8], F32, U + 90.25)
        top8i = at("top8i", [P, NB, 8], U32, U + 90.5)
        topi = at("topi", [P, NB, 2], F32, U + 90.75)
        sel1 = at("sel1", [P, NB, 8], F32, U + 91)
        sel2 = at("sel2", [P, NB, 8], F32, U + 91.25)
        pair = at("pair", [P, 5, NB], F32, U + 91.5)
        wc_hi = [at(f"wc_hi{i}", [P, KD, D], F32R, U + (0, 96)[i]) for i in range(2)]
        wc_lo = [at(f"wc_lo{i}", [P, KD, D], F32R, U + (8, 104)[i]) for i in range(2)]
        wc_raw = at("wc_raw", [P, KD, D], F32, U + 112)
        b = [at(f"b{i}", [P, NB, D], F32, U + 16 + 16 * i) for i in range(2)]
        c_hi = [at("c_hi0", [P, NB, D], F32R, U + 48), at("c_hi1", [P, NB, D], F32R, 64)]
        c_lo = [at("c_lo0", [P, NB, D], F32R, U + 64), at("c_lo1", [P, NB, D], F32R, U + 80)]
        xr = at("xr", [P, NB, D], F32, 64)
        bias1 = at("bias1", [P, D], F32, U + 80)
        xhT = at("xhT", [P, KD, N], F32, U + 16)
        xq = at("xq", [P, KD, N], BF16, U + 84)
        wq = at("wq", [P, KD, D], BF16, U + 0)
        qexp = at("qexp", [P, D], I32, U + 48)
        qmag = at("qmag", [P, D], F32, U + 50)
        qsum = at("qsum", [P, D], F32, U + 52)
        qexpw = at("qexpw", [P, D], I32, U + 92)
        qmagw = at("qmagw", [P, D], F32, U + 94)
        qsumw = at("qsumw", [P, D], F32, U + 4)

        bank = [ctx.enter_context(nc.psum_tensor(f"bank{i}", [P, 512], F32)) for i in range(8)]

        x_spill = nc.dram_tensor("x_spill", [P, NB, D], F32, kind="Internal").ap()

        edges_in = sem("edges_in")
        x_ld = [sem(f"x_ld{m}") for m in range(NB)]
        w0_ld = sem("w0_ld")
        small_ld = sem("small_ld")
        bias0_ld = sem("bias0_ld")
        consts = sem("consts")
        w0_split = sem("w0_split")
        wg_split = sem("wg_split")
        wg_hi_done = sem("wg_hi_done")
        idx_rows = sem("idx_rows")
        idx_turned = sem("idx_turned")
        idx_kept = sem("idx_kept")
        diag_ready = sem("diag_ready")
        pair_rows = sem("pair_rows")
        wcol_ready = sem("wcol_ready")
        tab_rows = sem("tab_rows")
        tab_ready = sem("tab_ready")
        oh_ready = sem("oh_ready")
        oh_used = sem("oh_used")
        win_done = sem("win_done")
        win_staged = sem("win_staged")
        win_placed = [sem(f"win_placed{q}") for q in range(4)]
        b_ready = sem("b_ready")
        bt_done = sem("bt_done")
        s_rows = sem("s_rows")
        s_ready = sem("s_ready")
        y_done = sem("y_done")
        y_kept = sem("y_kept")
        dinv0_ready = sem("dinv0_ready")
        y_hi_ready = sem("y_hi_ready")
        y_lo_ready = sem("y_lo_ready")
        xb_ready = sem("xb_ready")
        gcn_done = sem("gcn_done")
        gcn_kept = sem("gcn_kept")
        ln_var = [sem(f"ln_var{i}") for i in range(4)]
        ln_rstd = [sem(f"ln_rstd{i}") for i in range(4)]
        ln_norm = [sem(f"ln_norm{i}") for i in range(4)]
        ln_turned = [sem(f"ln_turned{i}") for i in range(4)]
        ln_hi = [sem(f"ln_hi{i}") for i in range(4)]
        ln_lo = [sem(f"ln_lo{i}") for i in range(4)]
        gate_done = sem("gate_done")
        topdiff = sem("topdiff")
        topexp = sem("topexp")
        comb_ready = sem("comb_ready")
        combT_done = sem("combT_done")
        combT_kept = sem("combT_kept")
        raw_ld = [[sem(f"w{k + 1}_raw_ld{i}") for i in range(2)] for k in range(2)]
        whi_done = [sem(f"w{k + 1}_hi_done") for k in range(2)]
        wlo_done = [sem(f"w{k + 1}_lo_done") for k in range(2)]
        h_done = sem("h_done")
        relu_done = sem("relu_done")
        b1_kept = sem("b1_kept")
        hhi_done = sem("hhi_done")
        hlo_done = sem("hlo_done")
        moe_done = sem("moe_done")
        moe_added = sem("moe_added")
        spilled = sem("spilled")
        degmax_ready = sem("degmax_ready")
        big_all = sem("big_all")
        big_ready = sem("big_ready")
        deg1_done = sem("deg1_done")
        deg1_kept = sem("deg1_kept")
        deg1_pow = sem("deg1_pow")
        dinv1_ready = sem("dinv1_ready")
        b_zero = sem("b_zero")
        wc_ld = sem("wc_ld")
        wchi_done = sem("wchi_done")
        wclo_done = sem("wclo_done")
        xw_done = sem("xw_done")
        xw_taken = sem("xw_taken")
        prop_done = sem("prop_done")
        b_done = sem("b_done")
        chi_done = sem("chi_done")
        clo_done = sem("clo_done")
        x_back = sem("x_back")
        bias1_ld = sem("bias1_ld")
        xr_ready = sem("xr_ready")
        x3_ready = sem("x3_ready")
        wamax = sem("wamax")
        wamax_all = sem("wamax_all")
        wq_ready = sem("wq_ready")
        xamax = sem("xamax")
        xamax_all = sem("xamax_all")
        xT_kept = sem("xT_kept")
        xq_ready = sem("xq_ready")
        fp8_done = sem("fp8_done")
        out_ready = sem("out_ready")
        stored = sem("stored")
        pool_step = sem("pool_step")
        dve_step = sem("dve_step")

        block = ctx.enter_context(nc.Block())

        @block.sync
        def _(sp):
            sp.dma_start(dst_i[:, :], dst_in).then_inc(edges_in, 16)
            sp.dma_start(src_i[:, :], src_in).then_inc(edges_in, 16)
            for m in range(NB):
                sp.dma_start(x[:, m, :], x_in[m * P:(m + 1) * P, :]).then_inc(x_ld[m], 16)
            sp.dma_start(w0_raw[:, :, :], w0_in.rearrange("(k p) n -> p k n", p=P)).then_inc(w0_ld, 16)
            sp.dma_start(bias0[:, :], bias0_in.partition_broadcast(P)).then_inc(bias0_ld, 16)
            sp.dma_start(wg_raw[:, :, :], wg_in.rearrange("(k p) n -> p k n", p=P)).then_inc(small_ld, 16)
            sp.dma_start(bgb[:, :], bg_in.partition_broadcast(P)).then_inc(small_ld, 16)
            sp.dma_start(b1T[:, :], b1_in).then_inc(small_ld, 16)

            for w in range(NW):
                kt, q = w // 4, w % 4
                sp.wait_ge(win_staged, w + 1)
                sp.dma_start(AT[q * WD:(q + 1) * WD, kt, :].bitcast(F32).rearrange("p (a n) -> p a n", a=SH),
                             stage[:, q, :]).then_inc(win_placed[q], 16)

            def load_expert(k, e, i):
                w = (w1_in, w2_in)[k]
                src = w[e] if isinstance(e, int) else w[bass.ds(e, 1), :, :].rearrange("e a b -> (e a) b")
                sp.dma_start(w_raw[i][k][:, :, :], src.rearrange("(k p) n -> p k n", p=P)).then_inc(raw_ld[k][i], 16)

            sp.wait_ge(y_done, NB)
            for e in range(2):
                for k in range(2):
                    load_expert(k, e, e)
            sp.wait_ge(gcn_done, NB)
            sp.dma_start(b2all[:, :], b2_in).then_inc(small_ld, 16)

            def refill(e, i):
                for k in range(2):
                    sp.wait_ge(whi_done[k], e + 1)
                    sp.wait_ge(wlo_done[k], e + 1)
                    load_expert(k, e + 2, i)

            with sp.Fori(0, 3) as t:
                for i in range(2):
                    refill(2 * t + i, i)
            refill(6, 0)

            sp.dma_start(wc_raw[:, :, :], wc_in[0].rearrange("(k p) n -> p k n", p=P)).then_inc(wc_ld, 16)
            for m in range(NB):
                sp.wait_ge(moe_added, NE * NB + m + 1)
                sp.dma_start(x_spill[:, m, :], x[:, m, :]).then_inc(spilled, 16)

            with sp.Fori(1, KC) as s:
                sp.wait_ge(wchi_done, s)
                sp.wait_ge(wclo_done, s)
                sp.dma_start(wc_raw[:, :, :], wc_in[bass.ds(s, 1), :, :].rearrange("e (k p) n -> p (e k) n", p=P)).then_inc(wc_ld, 16)
            sp.wait_ge(wchi_done, KC)
            sp.wait_ge(wclo_done, KC)
            sp.dma_start(wc_raw[:, :, :], wf_in.rearrange("(k p) n -> p k n", p=P)).then_inc(wc_ld, 16)
            sp.wait_ge(spilled, 16 * NB)
            sp.wait_ge(prop_done, (KC - 2) * NB)
            sp.dma_start(xr[:, :, :], x_spill).then_inc(x_back, 16)
            sp.dma_start(bias1[:, :], bias1_in.partition_broadcast(P)).then_inc(bias1_ld, 16)
            for m in range(NB):
                sp.wait_ge(out_ready, m + 1)
                sp.dma_start(out[m * P:(m + 1) * P, :], b[1][:, m, :]).then_inc(stored, 16)
            sp.wait_ge(stored, 16 * NB)

        @block.gpsimd
        def _(pool):
            steps = [0]

            def link(ins):
                steps[0] += 1
                ins.then_inc(pool_step, 1)
                pool.wait_ge(pool_step, steps[0])

            pool.sem_inc(oh_used, RING)
            link(nc.gpsimd.memset(ident[:, :], 0.0))
            nc.gpsimd.affine_select(out=ident[:, :], in_=ident[:, :], compare_op=ALU.not_equal, fill=1.0, base=0,
                                    pattern=[[-1, P]], channel_multiplier=1).then_inc(consts, 1)
            nc.gpsimd.memset(ones32[:, :], 1.0).then_inc(consts, 1)
            nc.gpsimd.iota(wstart[:, 0:1], [[0, 1]], base=0, channel_multiplier=WD,
                           allow_small_or_imprecise_dtypes=True).then_inc(consts, 1)
            nc.gpsimd.iota(wstart[:, 1:2], [[0, 1]], base=WD, channel_multiplier=WD,
                           allow_small_or_imprecise_dtypes=True).then_inc(consts, 1)
            nc.gpsimd.iota(iotap[:, 0, :], [[1, PAIRS]], base=PAIRS, channel_multiplier=0,
                           allow_small_or_imprecise_dtypes=True).then_inc(consts, 1)
            nc.gpsimd.iota(iotap[:, 1, :], [[1, PAIRS]], base=1, channel_multiplier=0,
                           allow_small_or_imprecise_dtypes=True).then_inc(consts, 1)
            link(nc.gpsimd.memset(tri[:, :], 1.0))
            nc.gpsimd.affine_select(out=tri[:, :], in_=tri[:, :], compare_op=ALU.is_ge, fill=0.0, base=-1,
                                    pattern=[[1, NW + 1]], channel_multiplier=-1).then_inc(consts, 1)
            nc.gpsimd.iota(iotab[:, :], [[1, SL]], base=0, channel_multiplier=0,
                           allow_small_or_imprecise_dtypes=True).then_inc(consts, 1)
            nc.gpsimd.iota(wbase[:, :], [[P, NW]], base=0, channel_multiplier=0,
                           allow_small_or_imprecise_dtypes=True).then_inc(consts, 1)
            nc.gpsimd.memset(zerob[:, :], 0.0).then_inc(consts, 1)
            nc.gpsimd.memset(nhalf[:, :], -0.5).then_inc(consts, 1)
            nc.gpsimd.iota(iota8[:, :], [[1, 8]], base=0, channel_multiplier=0,
                           allow_small_or_imprecise_dtypes=True).then_inc(consts, 1)
            nc.gpsimd.memset(comb[:, :, NE - 1], 0.5).then_inc(consts, 1)
            nc.gpsimd.memset(onecol[:, :], 1.0).then_inc(consts, 1)
            pool.wait_ge(consts, 14)
            nc.gpsimd.tensor_copy(identb[:, :], ident[:, :]).then_inc(consts, 1)

            def ln_rows(i, m):
                pool.wait_ge(ln_var[i], m + 1)
                link(nc.gpsimd.tensor_scalar(veps[:, i, m:m + 1], meanvar[:, i, m, 1:2], EPS, None, ALU.add))
                nc.gpsimd.tensor_tensor(rstd[:, i, m:m + 1], veps[:, i, m:m + 1], nhalf[:, 0:1], ALU.pow)\
                    .then_inc(ln_rstd[i], 1)

            def split_lo(out_lo, raw, hi, done):
                nc.gpsimd.tensor_tensor(out_lo, raw, hi.bitcast(F32), ALU.subtract).then_inc(done, 1)

            pool.wait_ge(wg_hi_done, 1)
            split_lo(wg_hilo[:, :, 8:16], wg_raw[:, :, :], wg_hilo[:, :, 0:8], wg_split)
            pool.wait_ge(w0_split, 1)
            split_lo(w0_lo[:, :, :], w0_raw[:, :, :], w0_hi[:, :, :], w0_split)
            def x_biased(m):
                pool.wait_ge(ln_norm[0], m + 1)
                nc.gpsimd.tensor_tensor(x[:, m, :], x[:, m, :], bias0[:, :], ALU.add).then_inc(xb_ready, 1)

            pool.wait_ge(bias0_ld, 16)
            for m in range(NB):
                ln_rows(0, m)
                if m:
                    x_biased(m - 1)
                if m:
                    for q in range(4):
                        pool.wait_ge(win_placed[q], 16 * m)
                    nc.gpsimd.tensor_scalar(B[:, m - 1, :], AT[:, m - 1, :].bitcast(F32), 1.0, None, ALU.min).then_inc(b_ready, 1)
            x_biased(NB - 1)
            for q in range(4):
                pool.wait_ge(win_placed[q], 16 * NB)
            nc.gpsimd.tensor_scalar(B[:, NB - 1, :], AT[:, NB - 1, :].bitcast(F32), 1.0, None, ALU.min).then_inc(b_ready, 1)
            for m in range(NB):
                pool.wait_ge(s_rows, m + 1)
                d = S[:, m, m * P:(m + 1) * P]
                nc.gpsimd.tensor_tensor(d, d.bitcast(F32), ident[:, :], ALU.add).then_inc(s_ready, 1)
            link(nc.gpsimd.tensor_scalar(deg0, rowsum, 1.0, None, ALU.add))
            nc.gpsimd.tensor_tensor(dinv0, deg0, nhalf[:, :], ALU.pow).then_inc(dinv0_ready, 1)

            def expert_lo(k, e, i):
                pool.wait_ge(whi_done[k], e + 1)
                split_lo(w_lo[i][k][:, :, :], w_raw[i][k][:, :, :], w_hi[i][k][:, :, :], wlo_done[k])

            for m in range(NB):
                ln_rows(1, m)
            pool.wait_ge(gcn_done, NB)
            for e in range(2):
                for k in range(2):
                    expert_lo(k, e, e)

            def hidden_lo(n, i, j):
                pool.wait_ge(hhi_done, n + 1)
                f, half = j // HALVES, j % HALVES
                cols = slice(half * 512, half * 512 + 512)
                split_lo(h_lo[i][:, f, cols], hrelu[:, j % 2, :], h_hi[i][:, f, cols], hlo_done)

            for j in range(4):
                hidden_lo(j, 0, j)

            pool.wait_ge(deg1_kept, 1)
            nc.gpsimd.tensor_tensor(dinv1, deg1, nhalf[:, :], ALU.pow).then_inc(deg1_pow, 1)
            pool.wait_ge(degmax_ready, 1)
            nc.gpsimd.partition_all_reduce(few[:, 1:2], few[:, 0:1], P, MAX).then_inc(big_all, 1)

            def moe_step(e, i, hidden=True, refill=True):
                if hidden:
                    for j in range(4):
                        hidden_lo(4 * (e + 1) + j, 1 - i, j)
                if refill:
                    expert_lo(0, e + 2, i)
                    expert_lo(1, e + 2, i)

            with pool.Fori(0, 3) as t:
                for i in range(2):
                    moe_step(2 * t + i, i)
            moe_step(6, 0)
            moe_step(7, 1, refill=False)

            def cheb_lo(s, i):
                pool.wait_ge(wchi_done, s + 1)
                split_lo(wc_lo[i][:, :, :], wc_raw[:, :, :], wc_hi[i][:, :, :], wclo_done)

            cheb_lo(0, 0)
            for m in range(NB):
                ln_rows(2, m)
            pool.wait_ge(moe_added, (NE + 1) * NB)
            nc.gpsimd.memset(b[0][:, :, :], 0.0).then_inc(b_zero, 1)
            nc.gpsimd.memset(b[1][:, :, :], 0.0).then_inc(b_zero, 1)
            cheb_lo(1, 1)
            with pool.Fori(0, 3) as t:
                for i in range(2):
                    cheb_lo(2 * t + i + 2, i)
            pool.wait_ge(x_back, 16)
            pool.wait_ge(bias1_ld, 16)
            for m in range(NB):
                nc.gpsimd.tensor_tensor(xr[:, m, :], xr[:, m, :], bias1[:, :], ALU.add).then_inc(xr_ready, 1)
            pool.wait_ge(wamax, 1)
            nc.gpsimd.partition_all_reduce(few[:, 3:4], few[:, 2:3], P, ABSMAX).then_inc(wamax_all, 1)
            for m in range(NB):
                ln_rows(3, m)
            pool.wait_ge(xamax, 1)
            nc.gpsimd.partition_all_reduce(few[:, 7:8], few[:, 6:7], P, ABSMAX).then_inc(xamax_all, 1)

        @block.scalar
        def _(act):
            def copy(out_ap, in_ap, done, scale=1.0):
                nc.scalar.activation(out_ap, in_ap, ACT.Copy, scale=scale).then_inc(done, 1)

            def turn_hi(i, m):
                act.wait_ge(ln_turned[i], m + 1)
                copy(xT_hi[:, :, m * P:(m + 1) * P],
                     bank[6 + m % 2][:, :].rearrange("p (k n) -> p k n", k=KD), ln_hi[i])

            act.wait_ge(small_ld, 48)
            copy(wg_hilo[:, :, 0:8], wg_raw[:, :, :], wg_hi_done)
            act.wait_ge(w0_ld, 16)
            copy(w0_hi[:, :, :], w0_raw[:, :, :], w0_split)
            for kt in range(NB):
                turn_hi(0, kt)
                for q in range(4):
                    w = 4 * kt + q
                    act.wait_ge(win_done, w + 1)
                    if kt:
                        act.wait_ge(win_placed[q], 16 * kt)
                    copy(stage[:, q, :], bank[q][:, 0:SL], win_staged)
                if kt:
                    act.wait_ge(y_done, kt)
                    copy(y[:, kt - 1, :], bank[4 + (kt - 1) % 2][:, :], y_kept)
            act.wait_ge(y_done, NB)
            copy(y[:, NB - 1, :], bank[4 + (NB - 1) % 2][:, :], y_kept)
            act.wait_ge(dinv0_ready, 1)
            act.wait_ge(y_kept, NB)
            for m in range(NB):
                copy(y_hi[:, m, :], y[:, m, :], y_hi_ready, scale=degs[:, 2, m:m + 1])
            for m in range(NB):
                turn_hi(1, m)

            def expert_hi(k, e, i, e_half):
                act.wait_ge(raw_ld[k][i], 16 * (e_half + 1))
                copy(w_hi[i][k][:, :, :], w_raw[i][k][:, :, :], whi_done[k])

            act.wait_ge(gcn_done, NB)
            for e in range(2):
                for k in range(2):
                    expert_hi(k, e, e, 0)

            def hidden(e, i, j):
                n = 4 * e + j
                act.wait_ge(h_done, n + 1)
                if not (isinstance(n, int) and n < 2):
                    act.wait_ge(hlo_done, n - 1)
                f = j // HALVES
                nc.scalar.activation(hrelu[:, j % 2, :], bank[j][:, :], ACT.Relu, bias=b1cur[:, i, f:f + 1]).then_inc(relu_done, 1)

            def hidden_bias(e, i):
                copy(b1cur[:, i, :], b1T[:, bass.ds(e * FB, FB)], b1_kept)
                act.wait_ge(b1_kept, e + 1)

            hidden_bias(0, 0)
            for j in range(4):
                hidden(0, 0, j)
            act.wait_ge(topdiff, 1)
            nc.scalar.activation(pair[:, 1, :], pair[:, 0, :], ACT.Exp).then_inc(topexp, 1)

            def moe_step(e, i, t, nxt=True, refill=True):
                if nxt:
                    hidden_bias(e + 1, 1 - i)
                    for j in range(4):
                        hidden(e + 1, 1 - i, j)
                if refill:
                    act.wait_ge(h_done, 4 * (e + 1))
                    expert_hi(0, e + 2, i, t + 1)
                    act.wait_ge(moe_done, NB * (e + 2))
                    expert_hi(1, e + 2, i, t + 1)

            with act.Fori(0, 3) as t:
                for i in range(2):
                    moe_step(2 * t + i, i, t)
            moe_step(6, 0, 3)
            moe_step(7, 1, 3, refill=False)

            def cheb_hi(s, i):
                act.wait_ge(wc_ld, 16 * (s + 1))
                if not isinstance(s, int) or s >= 2:
                    act.wait_ge(xw_done, NB * (s - 1))
                copy(wc_hi[i][:, :, :], wc_raw[:, :, :], wchi_done)

            cheb_hi(0, 0)
            for m in range(NB):
                turn_hi(2, m)
            act.wait_ge(moe_added, (NE + 1) * NB)
            cheb_hi(1, 1)

            def scaled_hi(s, m, i):
                act.wait_ge(b_done, NB * s + m + 1)
                copy(c_hi[i][:, m, :], b[i][:, m, :], chi_done, scale=degs[:, 4, m:m + 1])

            act.wait_ge(dinv1_ready, 1)
            act.wait_ge(spilled, 16 * NB)
            for m in range(NB):
                scaled_hi(0, m, 0)
            with act.Fori(0, 3) as t:
                for j in range(2):
                    s = 2 * t + 1 + j
                    for m in range(NB):
                        scaled_hi(s, m, 1 - j)
                        if m == 0:
                            cheb_hi(s + 1, j)
            for m in range(NB):
                act.wait_ge(ln_turned[3], m + 1)
                copy(xhT[:, :, m * P:(m + 1) * P],
                     bank[6 + m % 2][:, :].rearrange("p (k n) -> p k n", k=KD), xT_kept)

        @block.vector
        def _(dve):
            steps = [0]

            def link(ins):
                steps[0] += 1
                ins.then_inc(dve_step, 1)
                dve.wait_ge(dve_step, steps[0])

            def ln_stats(i, m, rows):
                link(nc.vector.bn_stats(stats[:, m, :], rows))
                nc.vector.bn_aggr(meanvar[:, i, m, :], stats[:, m, :]).then_inc(ln_var[i], 1)

            def ln_norm_block(i, m, rows):
                dve.wait_ge(ln_rstd[i], m + 1)
                if m >= 2:
                    dve.wait_ge(ln_turned[i], m - 1)
                nc.vector.tensor_scalar(xh[:, m % 2, :], rows, meanvar[:, i, m, 0:1], rstd[:, i, m:m + 1],
                                        ALU.subtract, ALU.mult).then_inc(ln_norm[i], 1)

            def turn_lo(i, m):
                dve.wait_ge(ln_hi[i], m + 1)
                cols = slice(m * P, (m + 1) * P)
                nc.vector.tensor_tensor(xT_lo[:, :, cols], bank[6 + m % 2][:, :].rearrange("p (k n) -> p k n", k=KD),
                                        xT_hi[:, :, cols].bitcast(F32), ALU.subtract).then_inc(ln_lo[i], 1)

            dve.wait_ge(edges_in, 32)
            nc.vector.tensor_reduce(pairmm[:, 0:1], dst_i[:, :], AX_X, ALU.min)
            nc.vector.tensor_scalar(shi_i[:, :], src_i[:, :], 8, None, ALU.logical_shift_right)
            link(nc.vector.tensor_reduce(pairmm[:, 1:2], dst_i[:, :], AX_X, ALU.max))
            link(nc.vector.tensor_scalar(slo_i[:, :], src_i[:, :], SL - 1, None, ALU.bitwise_and))
            dve.wait_ge(consts, 15)
            for c in range(2):
                nc.vector.tensor_scalar(diag[:, c, :], ident[:, :], pairmm[:, c:c + 1], None, ALU.mult).then_inc(diag_ready, 1)
            nc.vector.scalar_tensor_tensor(joint[:, :], dst_i[:, :], float(SH), shi_i[:, :], ALU.mult, ALU.add).then_inc(idx_rows, 1)
            nc.vector.tensor_copy(slo[:, :], slo_i[:, :]).then_inc(idx_rows, 1)
            dve.wait_ge(pair_rows, 1)
            link(nc.vector.tensor_scalar(wmask[:, 0, :], bank[3][0:NW, 0:PAIRS], wstart[:, 1:2], None, ALU.is_lt))
            link(nc.vector.scalar_tensor_tensor(wmask[:, 1, :], bank[3][0:NW, PAIRS:2 * PAIRS], wstart[:, 0:1],
                                                wmask[:, 0, :], ALU.is_ge, ALU.mult))
            nc.vector.scalar_tensor_tensor(wsel[:, 0, :], wmask[:, 1, :], -float(PAIRS), iotap[:, 0, :], ALU.mult, ALU.add)
            link(nc.vector.tensor_tensor(wsel[:, 1, :], wmask[:, 1, :], iotap[:, 1, :], ALU.mult))
            nc.vector.tensor_reduce(wcol[:, 0:1], wsel[:, 0, :], AX_X, ALU.min)
            link(nc.vector.tensor_reduce(wcol[:, 1:2], wsel[:, 1, :], AX_X, ALU.max))
            link(nc.vector.tensor_scalar(wcol[:, 2:3], wcol[:, 0:1], float(PAIRS - 1), None, ALU.min))
            link(nc.vector.tensor_tensor(wcol[:, 3:4], wcol[:, 1:2], wcol[:, 2:3], ALU.subtract))
            nc.vector.tensor_scalar(wcol[:, 3:4], wcol[:, 3:4], 1.0, None, ALU.max).then_inc(wcol_ready, 1)
            dve.wait_ge(idx_turned, 1)
            nc.vector.tensor_copy(idxT[:, :, :], bank[2][:, :].rearrange("p (c n) -> p c n", c=4)).then_inc(idx_kept, 1)
            dve.wait_ge(tab_rows, 1)
            link(nc.vector.tensor_copy(tabf[:, :], bank[3][0:1, 0:NW + 1]))
            nc.vector.tensor_copy(tab[:, 0:NW + 1], tabf[:, :]).then_inc(tab_ready, 1)
            nc.vector.tensor_tensor(tab[:, 2 * NW:3 * NW], bank[3][0:1, 64:64 + NW], tabf[:, 0:NW], ALU.subtract).then_inc(tab_ready, 1)

            dve.wait_ge(tab_ready, 2)
            dve.wait_ge(idx_kept, 1)
            for kt in range(NB):
                dve.wait_ge(x_ld[kt], 16)
                ln_stats(0, kt, x[:, kt, :])
                if kt:
                    turn_lo(0, kt - 1)
                for q in range(4):
                    w = 4 * kt + q
                    first = dve.value_load(tab[0:1, w:w + 1], min_val=0, max_val=NW * PAIRS)
                    after = dve.value_load(tab[0:1, w + 1:w + 2], min_val=1, max_val=NW * PAIRS)
                    shift = dve.value_load(tab[0:1, 2 * NW + w:2 * NW + w + 1])
                    with dve.Fori(first, after) as v:
                        dve.wait_ge(oh_used, v + 1)
                        slot = v & (RING - 1)
                        for h in range(2):
                            nc.vector.tensor_scalar(oh_row[:, bass.ds(slot, 1), h, :], iotab[:, 0:P].rearrange("p (a n) -> p a n", a=1),
                                                    wbase[:, w:w + 1], idxT[:, h, bass.ds(v + shift, 1)], ALU.add, ALU.is_equal)
                            last = nc.vector.tensor_scalar(oh_col[:, bass.ds(slot, 1), h, :], iotab[:, :].rearrange("p (a n) -> p a n", a=1),
                                                           idxT[:, 2 + h, bass.ds(v + shift, 1)], None, ALU.is_equal)
                        last.then_inc(oh_ready, 1)
                ln_norm_block(0, kt, x[:, kt, :])
            turn_lo(0, NB - 1)

            dve.wait_ge(xb_ready, NB)
            for m in range(NB):
                dve.wait_ge(bt_done, m + 1)
                nc.vector.scalar_tensor_tensor(S[:, m, :], B[:, m, :], 1.0, bank[2 + m % 2][:, :].bitcast(BF16), ALU.mult, ALU.max,
                                               accum_out=degs[:, 0, m:m + 1]).then_inc(s_rows, 1)
            for m in range(NB):
                dve.wait_ge(y_hi_ready, m + 1)
                nc.vector.scalar_tensor_tensor(y_lo[:, m, :], y[:, m, :], degs[:, 2, m:m + 1], y_hi[:, m, :].bitcast(F32),
                                               ALU.mult, ALU.subtract).then_inc(y_lo_ready, 1)
            for m in range(NB + 2):
                if m < NB:
                    dve.wait_ge(gcn_done, m + 1)
                    dve.wait_ge(xb_ready, m + 1)
                    nc.vector.scalar_tensor_tensor(x[:, m, :], bank[4 + m % 2][:, :], degs[:, 2, m:m + 1], x[:, m, :],
                                                   ALU.mult, ALU.add).then_inc(gcn_kept, 1)
                    dve.wait_ge(gcn_kept, m + 1)
                    ln_stats(1, m, x[:, m, :])
                if 1 <= m < NB + 1:
                    ln_norm_block(1, m - 1, x[:, m - 1, :])
                if m >= 2:
                    turn_lo(1, m - 2)

            def hidden_hi(n, i, j):
                dve.wait_ge(relu_done, n + 1)
                f, half = j // HALVES, j % HALVES
                nc.vector.tensor_copy(h_hi[i][:, f, half * 512:half * 512 + 512], hrelu[:, j % 2, :]).then_inc(hhi_done, 1)

            for j in range(4):
                hidden_hi(j, 0, j)

            dve.wait_ge(gate_done, 1)
            for m in range(NB):
                last = nc.vector.tensor_tensor(gate[:, m, :], bank[4][:, 8 * m:8 * m + 8], bgb[:, :], ALU.add)
            link(last)
            for m in range(NB):
                last = nc.vector.max(top8[:, m, :], gate[:, m, :])
            link(last)
            for m in range(NB):
                last = nc.vector.max_index(top8i[:, m, :], top8[:, m, :], gate[:, m, :])
            nc.vector.tensor_tensor(pair[:, 0, :], top8[:, :, 1], top8[:, :, 0], ALU.subtract).then_inc(topdiff, 1)
            link(nc.vector.engine_nop())
            nc.vector.tensor_copy(topi[:, :, :], top8i[:, :, 0:2])
            dve.wait_ge(topexp, 1)
            link(nc.vector.tensor_scalar(pair[:, 2, :], pair[:, 1, :], 1.0, None, ALU.add))
            link(nc.vector.reciprocal(pair[:, 3, :], pair[:, 2, :]))
            link(nc.vector.tensor_tensor(pair[:, 4, :], pair[:, 1, :], pair[:, 3, :], ALU.mult))
            for m in range(NB):
                nc.vector.tensor_scalar(sel1[:, m, :], iota8[:, :], topi[:, m, 0:1], pair[:, 3, m:m + 1], ALU.is_equal, ALU.mult)
                last = nc.vector.tensor_scalar(sel2[:, m, :], iota8[:, :], topi[:, m, 1:2], pair[:, 4, m:m + 1], ALU.is_equal, ALU.mult)
            link(last)
            nc.vector.tensor_tensor(comb[:, :, 0:8], sel1[:, :, :], sel2[:, :, :], ALU.add).then_inc(comb_ready, 1)
            for g in range(2):
                dve.wait_ge(combT_done, g + 1)
                nc.vector.tensor_copy(combT[:, g * 512:(g + 1) * 512], bank[6 + g][0:NE, :]).then_inc(combT_kept, 1)

            dve.wait_ge(deg1_done, 1)
            nc.vector.tensor_scalar(degs[:, 7, :], bank[5][:, 0:NB], 0.0, None, ALU.is_gt)
            nc.vector.tensor_scalar(degs[:, 3, :], bank[5][:, 0:NB], 1e-30, None, ALU.max).then_inc(deg1_kept, 1)
            nc.vector.tensor_reduce(few[:, 0:1], AT[:, :, :].bitcast(F32).rearrange("p k n -> p (k n)"), AX_X, ALU.max).then_inc(degmax_ready, 1)
            dve.wait_ge(deg1_pow, 1)
            link(nc.vector.tensor_tensor(degs[:, 4, :], degs[:, 4, :], degs[:, 7, :], ALU.mult))
            nc.vector.tensor_scalar(degs[:, 5, :], degs[:, 4, :], -2.0, None, ALU.mult)
            nc.vector.tensor_scalar(degs[:, 6, :], degs[:, 4, :], -1.0, None, ALU.mult).then_inc(dinv1_ready, 1)
            dve.wait_ge(big_all, 1)
            nc.vector.tensor_scalar(bigflag[0:1, 0:1], few[0:1, 1:2], float(EXACT), None, ALU.is_gt).then_inc(big_ready, 1)

            def biases_added(m):
                dve.wait_ge(moe_done, m + 1)
                nc.vector.scalar_tensor_tensor(x[:, m, :], bank[4 + m % 2][:, :], 1.0, x[:, m, :], ALU.mult, ALU.add).then_inc(moe_added, 1)

            for m in range(NB):
                biases_added(m)

            def expert_added(e, m):
                dve.wait_ge(moe_done, NB * (e + 1) + m + 1)
                if isinstance(e, int):
                    weight = comb[:, m, e:e + 1]
                else:
                    weight = comb[:, m, bass.ds(e, 1)]
                nc.vector.scalar_tensor_tensor(x[:, m, :], bank[4 + m % 2][:, :], weight, x[:, m, :], ALU.mult, ALU.add).then_inc(moe_added, 1)

            def moe_step(e, i, nxt=True):
                if nxt:
                    for j in range(4):
                        hidden_hi(4 * (e + 1) + j, 1 - i, j)
                for m in range(NB):
                    expert_added(e, m)

            with dve.Fori(0, 3) as t:
                for i in range(2):
                    moe_step(2 * t + i, i)
            moe_step(6, 0)
            moe_step(7, 1)
            for m in range(NB + 2):
                if m < NB:
                    expert_added(NE - 1, m)
                    dve.wait_ge(moe_added, NE * NB + m + 1)
                    ln_stats(2, m, x[:, m, :])
                if 1 <= m < NB + 1:
                    ln_norm_block(2, m - 1, x[:, m - 1, :])
                if m >= 2:
                    turn_lo(2, m - 2)

            def take_xw(s, m, i):
                dve.wait_ge(xw_done, NB * s + m + 1)
                nc.vector.tensor_tensor(b[i][:, m, :], bank[m % 4][:, :], b[i][:, m, :], ALU.subtract).then_inc(xw_taken, 1)

            def propagate(s, m, i, factor, banks=4):
                dve.wait_ge(prop_done, NB * (s - 1) + m + 1)
                dve.wait_ge(xw_taken, NB * s + m + 1)
                return nc.vector.scalar_tensor_tensor(b[i][:, m, :], bank[4 + m % banks][:, :], degs[:, factor, m:m + 1], b[i][:, m, :],
                                                      ALU.mult, ALU.add).then_inc(b_done, 1)

            def scaled_lo(s, m, i):
                dve.wait_ge(chi_done, NB * s + m + 1)
                nc.vector.scalar_tensor_tensor(c_lo[i][:, m, :], b[i][:, m, :], degs[:, 4, m:m + 1], c_hi[i][:, m, :].bitcast(F32),
                                               ALU.mult, ALU.subtract).then_inc(clo_done, 1)

            dve.wait_ge(b_zero, 2)
            for m in range(NB + 1):
                if m < NB:
                    dve.wait_ge(xw_done, m + 1)
                    nc.vector.tensor_tensor(b[0][:, m, :], bank[m % 4][:, :], b[0][:, m, :], ALU.subtract).then_inc(b_done, 1)
                if m:
                    scaled_lo(0, m - 1, 0)
            for m in range(NB):
                last = nc.vector.engine_nop().then_inc(xw_taken, 1)

            def cheb_step(s, i):
                take_xw(s, 0, i)
                take_xw(s, 1, i)
                for m in range(NB):
                    propagate(s, m, i, 5)
                    if m + 2 < NB:
                        take_xw(s, m + 2, i)
                    if m:
                        scaled_lo(s, m - 1, i)
                scaled_lo(s, NB - 1, i)

            with dve.Fori(0, 3) as t:
                for j in range(2):
                    cheb_step(2 * t + 1 + j, 1 - j)

            def round_fp8(q_out, v, scale, e_s, mag_s, sum_s):
                link(nc.vector.tensor_scalar(v, v, scale, FP8_MAX, ALU.mult, ALU.min))
                link(nc.vector.tensor_scalar(e_s, v.bitcast(I32), 0x7F800000, None, ALU.bitwise_and))
                link(nc.vector.tensor_scalar(mag_s, e_s.bitcast(F32), 2.0 ** -6, 1.5 * 2.0 ** 20, ALU.max, ALU.mult))
                link(nc.vector.scalar_tensor_tensor(sum_s, v, -FP8_MAX, mag_s, ALU.max, ALU.add))
                return nc.vector.tensor_tensor(q_out, sum_s, mag_s, ALU.subtract)

            def scale_of(amax_all, scale, inverse):
                link(nc.vector.tensor_scalar(inverse, amax_all, 1e-12, None, ALU.max))
                link(nc.vector.reciprocal(scale, inverse))
                link(nc.vector.tensor_scalar(scale, scale, FP8_MAX, None, ALU.mult))
                link(nc.vector.reciprocal(inverse, scale))

            S7 = KC - 1
            take_xw(S7, 0, 1)
            take_xw(S7, 1, 1)
            dve.wait_ge(wc_ld, 16 * (KC + 1))
            nc.vector.tensor_reduce(few[:, 2:3], wc_raw[:, :, :].rearrange("p k n -> p (k n)"), AX_X, ALU.max,
                                    apply_absolute_value=True).then_inc(wamax, 1)
            for m in range(NB + 3):
                if m < NB:
                    propagate(S7, m, 1, 6, banks=2)
                    if m + 2 < NB:
                        take_xw(S7, m + 2, 1)
                    dve.wait_ge(b_done, NB * S7 + m + 1)
                    dve.wait_ge(xr_ready, m + 1)
                    nc.vector.tensor_tensor(b[1][:, m, :], b[1][:, m, :], xr[:, m, :], ALU.add).then_inc(x3_ready, 1)
                    dve.wait_ge(x3_ready, m + 1)
                    ln_stats(3, m, b[1][:, m, :])
                if 1 <= m < NB + 1:
                    ln_norm_block(3, m - 1, b[1][:, m - 1, :])
                    dve.wait_ge(ln_norm[3], m)
                    link(nc.vector.tensor_reduce(few[:, 8 + m - 1:8 + m], xh[:, (m - 1) % 2, :], AX_X, ALU.max,
                                                 apply_absolute_value=True))
            nc.vector.tensor_reduce(few[:, 6:7], few[:, 8:8 + NB], AX_X, ALU.max).then_inc(xamax, 1)
            dve.wait_ge(wamax_all, 1)
            scale_of(few[:, 3:4], few[:, 4:5], few[:, 5:6])
            for k in range(KD):
                round_fp8(wq[:, k, :], wc_raw[:, k, :], few[:, 4:5], qexpw[:, :], qmagw[:, :], qsumw[:, :]).then_inc(wq_ready, 1)
                dve.wait_ge(wq_ready, k + 1)
            dve.wait_ge(xamax_all, 1)
            scale_of(few[:, 7:8], few[:, 16:17], few[:, 17:18])
            link(nc.vector.tensor_tensor(few[:, 18:19], few[:, 17:18], few[:, 5:6], ALU.mult))
            dve.wait_ge(xT_kept, NB)
            for half in range(HALVES):
                for k in range(KD):
                    cols = slice(half * 512, half * 512 + 512)
                    round_fp8(xq[:, k, cols], xhT[:, k, cols], few[:, 16:17], qexp[:, :], qmag[:, :], qsum[:, :]).then_inc(xq_ready, 1)
                    dve.wait_ge(xq_ready, KD * half + k + 1)
            for m in range(NB):
                dve.wait_ge(fp8_done, m + 1)
                nc.vector.scalar_tensor_tensor(b[1][:, m, :], bank[m % 4][:, :], few[:, 18:19], b[1][:, m, :],
                                               ALU.mult, ALU.add).then_inc(out_ready, 1)

        @block.tensor
        def _(pe):
            def mm(out_ap, lhsT, rhs, start, stop):
                return nc.tensor.matmul(out_ap, lhsT, rhs, start=start, stop=stop)

            def product(out_ap, terms):
                for n, (a, c) in enumerate(terms):
                    last = mm(out_ap, a, c, n == 0, n == len(terms) - 1)
                return last

            def turn(i, m):
                pe.wait_ge(ln_norm[i], m + 1)
                if m >= 2:
                    pe.wait_ge(ln_lo[i] if i < 3 else xT_kept, m - 1)
                for k in range(KD):
                    last = nc.tensor.transpose(bank[6 + m % 2][:, k * P:(k + 1) * P], xh[:, m % 2, k * P:(k + 1) * P], ident[:, :])
                last.then_inc(ln_turned[i], 1)

            def x_times(w_hi_ap, w_lo_ap, m):
                rows = slice(m * P, (m + 1) * P)
                t = []
                for k in range(KD):
                    t.append((xT_hi[:, k, rows], w_hi_ap[:, k, :]))
                    t.append((xT_hi[:, k, rows], w_lo_ap[:, k, :]))
                    t.append((xT_lo[:, k, rows], w_hi_ap[:, k, :]))
                return t

            pe.wait_ge(consts, 15)
            pe.wait_ge(diag_ready, 2)
            mm(bank[3][0:NW, 0:2 * PAIRS], ones32[:, :], diag[:, :, :], True, True).then_inc(pair_rows, 1)
            pe.wait_ge(idx_rows, 2)
            for c, rows in enumerate((joint, slo)):
                for h in range(2):
                    last = nc.tensor.transpose(bank[2][:, (2 * c + h) * P:(2 * c + h + 1) * P], rows[:, h * P:(h + 1) * P], ident[:, :])
            last.then_inc(idx_turned, 1)
            pe.wait_ge(wcol_ready, 1)
            mm(bank[3][0:1, 0:NW + 1], wcol[:, 3:4], tri[:, :], True, True)
            mm(bank[3][0:1, 64:64 + NW], wcol[:, 2:3], ident[0:NW, 0:NW], True, True).then_inc(tab_rows, 1)

            def y_block(m):
                pe.wait_ge(ln_lo[0], m + 1)
                pe.wait_ge(ln_hi[0], m + 1)
                if m == 0:
                    pe.wait_ge(w0_split, 2)
                if m >= 2:
                    pe.wait_ge(y_kept, m - 1)
                product(bank[4 + m % 2][:, :], x_times(w0_hi, w0_lo, m)).then_inc(y_done, 1)

            pe.wait_ge(tab_ready, 2)
            pe.wait_ge(idx_kept, 1)
            for kt in range(NB):
                for q in range(4):
                    w = 4 * kt + q
                    sums = bank[q][:, 0:SL]
                    if kt:
                        pe.wait_ge(win_staged, w - 3)
                    mm(sums, zerob[:, :], iotab[:, :], True, False)
                    first = pe.value_load(tab[0:1, w:w + 1], min_val=0, max_val=NW * PAIRS)
                    after = pe.value_load(tab[0:1, w + 1:w + 2], min_val=1, max_val=NW * PAIRS)
                    with pe.Fori(first, after) as v:
                        pe.wait_ge(oh_ready, v + 1)
                        slot = v & (RING - 1)
                        for h in range(2):
                            last = mm(sums, oh_row[:, bass.ds(slot, 1), h, :], oh_col[:, bass.ds(slot, 1), h, :], False, False)
                        last.then_inc(oh_used, 1)
                    mm(sums, zerob[:, :], iotab[:, :], False, True).then_inc(win_done, 1)
                turn(0, kt)
                if kt:
                    y_block(kt - 1)
            y_block(NB - 1)

            pe.wait_ge(b_ready, NB)
            pe.wait_ge(idx_kept, 1)
            for m in range(NB):
                if m >= 2:
                    pe.wait_ge(s_rows, m - 1)
                for j in range(NB):
                    last = nc.tensor.transpose(bank[2 + m % 2][:, :].bitcast(BF16)[:, j * P:(j + 1) * P], B[:, j, m * P:(m + 1) * P], identb[:, :])
                last.then_inc(bt_done, 1)

            pe.wait_ge(s_ready, NB)
            pe.wait_ge(y_lo_ready, NB)
            pe.wait_ge(y_hi_ready, NB)
            for m in range(NB + 2):
                if m < NB:
                    if m >= 2:
                        pe.wait_ge(gcn_kept, m - 1)
                    else:
                        pe.wait_ge(y_kept, NB)
                    rows = slice(m * P, (m + 1) * P)
                    t = [(S[:, k, rows], part[:, k, :]) for k in range(NB) for part in (y_hi, y_lo)]
                    product(bank[4 + m % 2][:, :], t).then_inc(gcn_done, 1)
                if m >= 2:
                    turn(1, m - 2)

            pe.wait_ge(ln_lo[1], NB)

            def hidden(e, i):
                pe.wait_ge(whi_done[0], e + 1)
                pe.wait_ge(wlo_done[0], e + 1)
                for j in range(4):
                    if not (isinstance(e, int) and e == 0):
                        pe.wait_ge(relu_done, 4 * (e - 1) + j + 1)
                    f, half = j // HALVES, j % HALVES
                    cols, fs = slice(half * 512, half * 512 + 512), slice(f * P, (f + 1) * P)
                    t = []
                    for k in range(KD):
                        t.append((w_hi[i][0][:, k, fs], xT_hi[:, k, cols]))
                        t.append((w_hi[i][0][:, k, fs], xT_lo[:, k, cols]))
                        t.append((w_lo[i][0][:, k, fs], xT_hi[:, k, cols]))
                    product(bank[j][:, :], t).then_inc(h_done, 1)

            def expert_out(e, i, last=False):
                pe.wait_ge(whi_done[1], e + 1)
                pe.wait_ge(wlo_done[1], e + 1)
                pe.wait_ge(hlo_done, 4 * (e + 1))
                for m in range(NB):
                    pe.wait_ge(moe_added, NB * (e + 1) + m - 1)
                    rows = slice(m * P, (m + 1) * P)
                    t = []
                    for f in range(FB):
                        t.append((h_hi[i][:, f, rows], w_hi[i][1][:, f, :]))
                        t.append((h_hi[i][:, f, rows], w_lo[i][1][:, f, :]))
                        t.append((h_lo[i][:, f, rows], w_hi[i][1][:, f, :]))
                    product(bank[4 + m % 2][:, :], t).then_inc(moe_done, 1)
                    if last and m >= 2:
                        turn(2, m - 2)

            hidden(0, 0)
            pe.wait_ge(wg_split, 1)
            pe.wait_ge(gcn_kept, NB)
            for m in range(NB):
                rows, g = slice(m * P, (m + 1) * P), bank[4][:, 8 * m:8 * m + 8]
                t = []
                for k in range(KD):
                    t.append((xT_hi[:, k, rows], wg_hilo[:, k, 0:8]))
                    t.append((xT_hi[:, k, rows], wg_hilo[:, k, 8:16]))
                    t.append((xT_lo[:, k, rows], wg_hilo[:, k, 0:8]))
                last = product(g, t)
            last.then_inc(gate_done, 1)
            for m in range(NB):
                rows = slice(m * P, (m + 1) * P)
                last = product(bank[5][:, m:m + 1], [(AT[:, k, rows].bitcast(F32), onecol[:, :]) for k in range(NB)])
            last.then_inc(deg1_done, 1)
            pe.wait_ge(comb_ready, 1)
            for g in range(2):
                for m in range(4 * g, 4 * g + 4):
                    last = nc.tensor.transpose(bank[6 + g][0:NE, (m % 4) * P:(m % 4 + 1) * P], comb[:, m, :], ident[:, :])
                last.then_inc(combT_done, 1)
            pe.wait_ge(combT_kept, 2)
            pe.wait_ge(deg1_kept, 1)
            pe.wait_ge(small_ld, 64)
            for m in range(NB):
                if m >= 2:
                    pe.wait_ge(moe_added, m - 1)
                mm(bank[4 + m % 2][:, :], combT[:, m * P:(m + 1) * P], b2all[:, :], True, True).then_inc(moe_done, 1)

            with pe.Fori(0, 3) as t:
                for i in range(2):
                    hidden(2 * t + i + 1, 1 - i)
                    expert_out(2 * t + i, i)
            hidden(7, 1)
            expert_out(6, 0)
            hidden(8, 0)
            expert_out(7, 1)
            expert_out(8, 0, last=True)
            turn(2, NB - 2)
            turn(2, NB - 1)
            pe.wait_ge(ln_lo[2], NB)
            pe.wait_ge(moe_added, (NE + 1) * NB)

            def xw(s, m, i):
                if m == 0:
                    pe.wait_ge(wchi_done, s + 1)
                    pe.wait_ge(wclo_done, s + 1)
                if isinstance(s, int) and s == 0:
                    if m >= 4:
                        pe.wait_ge(b_done, m - 3)
                else:
                    pe.wait_ge(xw_taken, NB * s + m - 3)
                product(bank[m % 4][:, :], x_times(wc_hi[i], wc_lo[i], m)).then_inc(xw_done, 1)

            def prop(s, m, i, cast, banks):
                pe.wait_ge(clo_done, NB * s)
                if m >= banks:
                    pe.wait_ge(b_done, NB * s + m - banks + 1)
                rows = slice(m * P, (m + 1) * P)
                t = [(cast(AT[:, k, rows]), cast(part[:, k, :])) for k in range(NB) for part in (c_hi[i], c_lo[i])]
                product(bank[4 + m % banks][:, :], t).then_inc(prop_done, 1)

            def cheb(cast):
                def step(s, i, final=False):
                    xw(s, 0, i)
                    xw(s, 1, i)
                    for m in range(NB):
                        prop(s, m, 1 - i, cast, 2 if final else 4)
                        if m + 2 < NB:
                            xw(s, m + 2, i)
                        if final and m >= 2:
                            turn(3, m - 2)

                with pe.Fori(0, 3) as t:
                    for j in range(2):
                        step(2 * t + 1 + j, 1 - j)
                step(KC - 1, 1, final=True)

            for m in range(NB):
                xw(0, m, 0)
            pe.wait_ge(big_ready, 1)
            big = pe.value_load(bigflag[0:1, 0:1], min_val=0, max_val=1)
            with pe.If(big > 0):
                cheb(lambda ap: ap.bitcast(F32))
            with pe.Else():
                cheb(lambda ap: ap)

            turn(3, NB - 2)
            turn(3, NB - 1)
            pe.wait_ge(wq_ready, KD)
            for m in range(NB):
                pe.wait_ge(xq_ready, KD * (m // 4 + 1))
                if m >= 4:
                    pe.wait_ge(out_ready, m - 3)
                rows = slice(m * P, (m + 1) * P)
                product(bank[m % 4][:, :], [(xq[:, k, rows], wq[:, k, :]) for k in range(KD)]).then_inc(fp8_done, 1)


def kernel(x, src, dst, L0_gnn_weight, L0_gnn_bias, L0_ffn_Wg, L0_ffn_bg, L0_ffn_W1, L0_ffn_b1,
           L0_ffn_W2, L0_ffn_b2, L0_ffn_Ws1, L0_ffn_bs1, L0_ffn_Ws2, L0_ffn_bs2,
           L1_gnn_weight, L1_gnn_bias, L1_ffn_weight):
    import numpy as np
    import concourse.bacc as bacc
    from concourse.bass_utils import run_bass_kernel_spmd

    rows = lambda a: np.asarray(a)
    arrays = {
        "x_in": rows(x),
        "src_in": rows(src).reshape(PAIRS, 2 * P),
        "dst_in": rows(dst).reshape(PAIRS, 2 * P),
        "w0_in": rows(L0_gnn_weight),
        "bias0_in": rows(L0_gnn_bias),
        "wg_in": rows(L0_ffn_Wg),
        "bg_in": rows(L0_ffn_bg),
        "w1_in": np.concatenate([rows(L0_ffn_W1), rows(L0_ffn_Ws1)[None]]),
        "b1_in": np.concatenate([rows(L0_ffn_b1), rows(L0_ffn_bs1)[None]]).reshape(NE * FB, P).T,
        "w2_in": np.concatenate([rows(L0_ffn_W2), rows(L0_ffn_Ws2)[None]]),
        "b2_in": np.concatenate([rows(L0_ffn_b2), rows(L0_ffn_bs2)[None]]),
        "wc_in": rows(L1_gnn_weight)[::-1],
        "bias1_in": rows(L1_gnn_bias),
        "wf_in": rows(L1_ffn_weight),
    }
    arrays = {n: np.ascontiguousarray(a) for n, a in arrays.items()}
    nc = bacc.Bacc("TRN2", target_bir_lowering=False, num_devices=1)
    aps = [nc.dram_tensor(n, a.shape, mybir.dt.from_np(a.dtype), kind="ExternalInput").ap() for n, a in arrays.items()]
    out = nc.dram_tensor("out", [N, D], F32, kind="ExternalOutput").ap()
    build(nc, *aps, out)
    r = run_bass_kernel_spmd(nc, [arrays], core_ids=[0])
    return r.results[0]["out"]
```

```python
from contextlib import ExitStack

import concourse.bass as bass
from concourse import mybir

F32 = mybir.dt.float32
F32R = mybir.dt.float32r
BF16 = mybir.dt.bfloat16
I32 = mybir.dt.int32
U32 = mybir.dt.uint32
ALU = mybir.AluOpType
ACT = mybir.ActivationFunctionType
AX_X = mybir.AxisListType.X
ABSMAX = bass.bass_isa.ReduceOp.absmax
MAX = bass.bass_isa.ReduceOp.max

P = 128
N = 1024
D = 512
NB = N // P
KD = D // P
E = 32768
PAIRS = E // (2 * P)
TILES = E // P
WD = 16
NW = N // WD
SH = P // WD
SL = N // SH
WG = 512 // SL
NG = NW // WG
TPW = TILES // NW
BEFORE = 3
VIS = TPW + 2 * BEFORE
CHUNK = TPW * WG
RING = 4
NE = 9
F = 256
FB = F // P
KC = 8
EPS = 1e-5
FP8_MAX = 448.0
EXACT = 4096
HALVES = N // 512

KB = 1024


def build(nc, x_in, src_in, dst_in, w0_in, bias0_in, wg_in, bg_in, w1_in, b1_in, w2_in, b2_in,
          wc_in, bias1_in, wf_in, out):
    ctx = ExitStack()
    with ctx:
        base = (nc.sbuf_base + 31) // 32 * 32

        def at(name, shape, dt, offset):
            return nc.alloc_sbuf_tensor_at(name, shape, dt, offset=base + int(offset * KB))

        def sem(name):
            return ctx.enter_context(nc.semaphore(name))

        AT = at("AT", [P, NB, N], F32R, 0)
        xT_hi = at("xT_hi", [P, KD, N], F32R, 32)
        xT_lo = at("xT_lo", [P, KD, N], F32R, 48)
        x = at("x", [P, NB, D], F32, 64)
        U = 80
        xh = at("xh", [P, 2, D], F32, 200)
        ident = at("ident", [P, P], F32, 204)
        identb = at("identb", [P, P], BF16, 204.5)
        stats = at("stats", [P, NB, 6], F32, 204.75)
        meanvar = at("meanvar", [P, 4, NB, 2], F32, 205)
        veps = at("veps", [P, 4, NB], F32, 205.25)
        rstd = at("rstd", [P, 4, NB], F32, 205.375)
        nhalf = at("nhalf", [P, NB], F32, 205.5)
        comb = at("comb", [P, NB, NE], F32, 205.5625)
        degs = at("degs", [P, 8, NB], F32, 205.875)
        rowsum, deg0, dinv0, deg1, dinv1, m2dinv1, ndinv1, degpos = (degs[:, i, :] for i in range(8))
        b1T = at("b1T", [P, NE * FB], F32, 206.125)
        few = at("few", [P, 32], F32, 206.25)
        bigflag = at("bigflag", [1, 1], I32, 206.375)
        wg_hilo = at("wg_hilo", [P, KD, 16], F32R, 206.5)
        wg_raw = at("wg_raw", [P, KD, 8], F32, 206.75)
        bgb = at("bgb", [P, 8], F32, 206.875)
        onecol = at("onecol", [P, 1], F32, 206.9375)
        b1cur = at("b1cur", [P, 2, FB], F32, 206.96875)
        iota8 = at("iota8", [P, 8], F32, 206.90625)

        S = at("S", [P, NB, N], F32R, U + 0)
        B = at("B", [P, NB, N], BF16, U + 32)
        y = at("y", [P, NB, D], F32, U + 48)
        y_hi = at("y_hi", [P, NB, D], F32R, U + 64)
        y_lo = at("y_lo", [P, NB, D], F32R, U + 80)
        w0_raw = at("w0_raw", [P, KD, D], F32, U + 96)
        w0_hi = at("w0_hi", [P, KD, D], F32R, U + 104)
        w0_lo = at("w0_lo", [P, KD, D], F32R, U + 112)
        src_i = at("src_i", [P, 2 * P], I32, U + 0)
        dst_i = at("dst_i", [P, 2 * P], I32, U + 1)
        shi_i = at("shi_i", [P, 2 * P], I32, U + 2)
        slo_i = at("slo_i", [P, 2 * P], I32, U + 3)
        joint = at("joint", [P, 2 * P], F32, U + 4)
        slo = at("slo", [P, 2 * P], F32, U + 5)
        stage = at("stage", [P, 4, WG, SL], F32, U + 6)
        rel = at("rel", [P, NW, VIS], BF16, U + 14)
        jT = at("jT", [P, BEFORE + TILES + VIS], F32, U + 15.5)
        sT = at("sT", [P, TILES], BF16, U + 16.75)
        jconst = at("jconst", [P, P, 2], BF16, U + 17.25)
        wbase = at("wbase", [P, NW], F32, U + 17.75)
        tilemm_i = at("tilemm_i", [P, 2, 2], I32, U + 18)
        tilemm = at("tilemm", [P, 2, 2], F32, U + 18.0625)
        tilewin = at("tilewin", [P, 2, 2], I32, U + 18.125)
        tileno = at("tileno", [P, 2, 2], F32, U + 18.1875)
        off = at("off", [P, 4], F32, U + 18.25)
        offall = at("offall", [1, 1], F32, U + 18.3125)
        unsorted = at("unsorted", [1, 1], I32, U + 18.375)
        bias0 = at("bias0", [P, D], F32, U + 28)
        oh_rows = [at(f"oh_rows{i}", [P, WG * VIS // 2, P, 2], BF16, U + 64 + 10 * i) for i in range(2)]
        oh_cols = [at(f"oh_cols{i}", [P, CHUNK // 2, SL, 2], BF16, U + (84, 88, 92, 20, 24)[i]) for i in range(5)]
        sF = at("sF", [P, TILES], F32, U + 76)
        oh_row = at("oh_row", [P, RING, 2, P], BF16, U + 64)
        oh_col = at("oh_col", [P, RING, 2, SL], BF16, U + 66)
        iotab = at("iotab", [P, P], BF16, U + 68)
        zerob = at("zerob", [P, P], BF16, U + 68.5)
        diag = at("diag", [P, 2, P], F32, U + 69)
        pairmm = at("pairmm", [P, 2], F32, U + 70)
        wstart = at("wstart", [NW, 2], F32, U + 70.0625)
        ones_w = at("ones_w", [P, NW], F32, U + 70.125)
        tri = at("tri", [NW, NW + 1], F32, U + 70.5)
        iotap = at("iotap", [NW, 2, PAIRS], F32, U + 71)
        wmask = at("wmask", [NW, 2, PAIRS], F32, U + 72)
        wsel = at("wsel", [NW, 2, PAIRS], F32, U + 73)
        wcol = at("wcol", [NW, 4], F32, U + 74)
        tabf = at("tabf", [1, NW + 1], F32, U + 74.25)
        tab = at("tab", [1, 2 * NW + 1], I32, U + 75)
        w_hi = [[at(f"w{k + 1}_hi{i}", [P, KD, F] if k == 0 else [P, FB, D], F32R, U + (32, 16)[i] + 4 * k)
                 for k in range(2)] for i in range(2)]
        w_lo = [[at(f"w{k + 1}_lo{i}", [P, KD, F] if k == 0 else [P, FB, D], F32R, U + (32, 16)[i] + 8 + 4 * k)
                 for k in range(2)] for i in range(2)]
        w_raw = [[at(f"w{k + 1}_raw{i}", [P, KD, F] if k == 0 else [P, FB, D], F32, U + 96 + 8 * i + 4 * k)
                  for k in range(2)] for i in range(2)]
        h_hi = [at(f"h_hi{i}", [P, FB, N], F32R, U + 48 + 16 * i) for i in range(2)]
        h_lo = [at(f"h_lo{i}", [P, FB, N], F32R, U + 56 + 16 * i) for i in range(2)]
        hrelu = at("hrelu", [P, 2, 512], F32, U + 80)
        combT = at("combT", [NE, N], F32, U + 84)
        b2all = at("b2all", [NE, D], F32, U + 88)
        gate = at("gate", [P, NB, 8], F32, U + 90)
        top8 = at("top8", [P, NB, 8], F32, U + 90.25)
        top8i = at("top8i", [P, NB, 8], U32, U + 90.5)
        topi = at("topi", [P, NB, 2], F32, U + 90.75)
        sel1 = at("sel1", [P, NB, 8], F32, U + 91)
        sel2 = at("sel2", [P, NB, 8], F32, U + 91.25)
        pair = at("pair", [P, 5, NB], F32, U + 91.5)
        wc_hi = [at(f"wc_hi{i}", [P, KD, D], F32R, U + (0, 96)[i]) for i in range(2)]
        wc_lo = [at(f"wc_lo{i}", [P, KD, D], F32R, U + (8, 104)[i]) for i in range(2)]
        wc_raw = at("wc_raw", [P, KD, D], F32, U + 112)
        b = [at(f"b{i}", [P, NB, D], F32, U + 16 + 16 * i) for i in range(2)]
        c_hi = [at("c_hi0", [P, NB, D], F32R, U + 48), at("c_hi1", [P, NB, D], F32R, 64)]
        c_lo = [at("c_lo0", [P, NB, D], F32R, U + 64), at("c_lo1", [P, NB, D], F32R, U + 80)]
        xr = at("xr", [P, NB, D], F32, 64)
        bias1 = at("bias1", [P, D], F32, U + 80)
        xhT = at("xhT", [P, KD, N], F32, U + 16)
        xq = at("xq", [P, KD, N], BF16, U + 84)
        wq = at("wq", [P, KD, D], BF16, U + 0)
        qexp = at("qexp", [P, D], I32, U + 48)
        qmag = at("qmag", [P, D], F32, U + 50)
        qsum = at("qsum", [P, D], F32, U + 52)
        qexpw = at("qexpw", [P, D], I32, U + 92)
        qmagw = at("qmagw", [P, D], F32, U + 94)
        qsumw = at("qsumw", [P, D], F32, U + 4)

        bank = [ctx.enter_context(nc.psum_tensor(f"bank{i}", [P, 512], F32)) for i in range(8)]

        x_spill = nc.dram_tensor("x_spill", [P, NB, D], F32, kind="Internal").ap()

        edges_in = sem("edges_in")
        x_ld = [sem(f"x_ld{m}") for m in range(NB)]
        w0_ld = sem("w0_ld")
        small_ld = sem("small_ld")
        bias0_ld = sem("bias0_ld")
        consts = sem("consts")
        w0_split = sem("w0_split")
        wg_split = sem("wg_split")
        wg_hi_done = sem("wg_hi_done")
        idx_rows = sem("idx_rows")
        idx_turned = sem("idx_turned")
        idx_kept = sem("idx_kept")
        off_ready = sem("off_ready")
        off_row = sem("off_row")
        path_ready = sem("path_ready")
        slow_consts = sem("slow_consts")
        diag_ready = sem("diag_ready")
        pair_rows = sem("pair_rows")
        wcol_ready = sem("wcol_ready")
        tab_rows = sem("tab_rows")
        tab_ready = sem("tab_ready")
        oh_ready = sem("oh_ready")
        oh_used = sem("oh_used")
        win_done = sem("win_done")
        win_staged = sem("win_staged")
        win_placed = [sem(f"win_placed{i}") for i in range(4)]
        b_ready = sem("b_ready")
        bt_done = sem("bt_done")
        s_rows = sem("s_rows")
        s_ready = sem("s_ready")
        y_done = sem("y_done")
        y_kept = sem("y_kept")
        dinv0_ready = sem("dinv0_ready")
        y_hi_ready = sem("y_hi_ready")
        y_lo_ready = sem("y_lo_ready")
        xb_ready = sem("xb_ready")
        gcn_done = sem("gcn_done")
        gcn_kept = sem("gcn_kept")
        ln_var = [sem(f"ln_var{i}") for i in range(4)]
        ln_rstd = [sem(f"ln_rstd{i}") for i in range(4)]
        ln_norm = [sem(f"ln_norm{i}") for i in range(4)]
        ln_turned = [sem(f"ln_turned{i}") for i in range(4)]
        ln_hi = [sem(f"ln_hi{i}") for i in range(4)]
        ln_lo = [sem(f"ln_lo{i}") for i in range(4)]
        gate_done = sem("gate_done")
        topdiff = sem("topdiff")
        topexp = sem("topexp")
        comb_ready = sem("comb_ready")
        combT_done = sem("combT_done")
        combT_kept = sem("combT_kept")
        raw_ld = [[sem(f"w{k + 1}_raw_ld{i}") for i in range(2)] for k in range(2)]
        whi_done = [sem(f"w{k + 1}_hi_done") for k in range(2)]
        wlo_done = [sem(f"w{k + 1}_lo_done") for k in range(2)]
        h_done = sem("h_done")
        relu_done = sem("relu_done")
        b1_kept = sem("b1_kept")
        hhi_done = sem("hhi_done")
        hlo_done = sem("hlo_done")
        moe_done = sem("moe_done")
        moe_added = sem("moe_added")
        spilled = sem("spilled")
        degmax_ready = sem("degmax_ready")
        big_all = sem("big_all")
        big_ready = sem("big_ready")
        deg1_done = sem("deg1_done")
        deg1_kept = sem("deg1_kept")
        deg1_pow = sem("deg1_pow")
        dinv1_ready = sem("dinv1_ready")
        b_zero = sem("b_zero")
        wc_ld = sem("wc_ld")
        wchi_done = sem("wchi_done")
        wclo_done = sem("wclo_done")
        xw_done = sem("xw_done")
        xw_taken = sem("xw_taken")
        prop_done = sem("prop_done")
        b_done = sem("b_done")
        chi_done = sem("chi_done")
        clo_done = sem("clo_done")
        x_back = sem("x_back")
        bias1_ld = sem("bias1_ld")
        xr_ready = sem("xr_ready")
        x3_ready = sem("x3_ready")
        wamax = sem("wamax")
        wamax_all = sem("wamax_all")
        wq_ready = sem("wq_ready")
        xamax = sem("xamax")
        xamax_all = sem("xamax_all")
        xT_kept = sem("xT_kept")
        xq_ready = sem("xq_ready")
        fp8_done = sem("fp8_done")
        out_ready = sem("out_ready")
        stored = sem("stored")
        pool_step = sem("pool_step")
        dve_step = [sem(f"dve_step{i}") for i in range(4)]
        slow_step = sem("slow_step")

        block = ctx.enter_context(nc.Block())

        @block.sync
        def _(sp):
            sp.dma_start(dst_i[:, :], dst_in).then_inc(edges_in, 16)
            sp.dma_start(src_i[:, :], src_in).then_inc(edges_in, 16)
            for m in range(NB):
                sp.dma_start(x[:, m, :], x_in[m * P:(m + 1) * P, :]).then_inc(x_ld[m], 16)
            sp.dma_start(w0_raw[:, :, :], w0_in.rearrange("(k p) n -> p k n", p=P)).then_inc(w0_ld, 16)
            sp.dma_start(bias0[:, :], bias0_in.partition_broadcast(P)).then_inc(bias0_ld, 16)
            sp.dma_start(wg_raw[:, :, :], wg_in.rearrange("(k p) n -> p k n", p=P)).then_inc(small_ld, 16)
            sp.dma_start(bgb[:, :], bg_in.partition_broadcast(P)).then_inc(small_ld, 16)
            sp.dma_start(b1T[:, :], b1_in).then_inc(small_ld, 16)

            for g in range(NG):
                sp.wait_ge(win_staged, g + 1)
                for q in range(WG):
                    row = (g * WG + q) * WD
                    sp.dma_start(AT[row % P:row % P + WD, row // P, :].bitcast(F32).rearrange("p (a n) -> p a n", a=SH),
                                 stage[:, g % 4, q, :]).then_inc(win_placed[g % 4], 16)

            def load_expert(k, e, i):
                w = (w1_in, w2_in)[k]
                src = w[e] if isinstance(e, int) else w[bass.ds(e, 1), :, :].rearrange("e a b -> (e a) b")
                sp.dma_start(w_raw[i][k][:, :, :], src.rearrange("(k p) n -> p k n", p=P)).then_inc(raw_ld[k][i], 16)

            sp.wait_ge(y_done, NB)
            for e in range(2):
                for k in range(2):
                    load_expert(k, e, e)
            sp.wait_ge(gcn_done, NB)
            sp.dma_start(b2all[:, :], b2_in).then_inc(small_ld, 16)

            def refill(e, i):
                for k in range(2):
                    sp.wait_ge(whi_done[k], e + 1)
                    sp.wait_ge(wlo_done[k], e + 1)
                    load_expert(k, e + 2, i)

            refill(0, 0)
            with sp.Fori(0, 3) as t:
                refill(2 * t + 1, 1)
                refill(2 * t + 2, 0)

            sp.dma_start(wc_raw[:, :, :], wc_in[0].rearrange("(k p) n -> p k n", p=P)).then_inc(wc_ld, 16)
            for m in range(NB):
                sp.wait_ge(moe_added, NE * NB + m + 1)
                sp.dma_start(x_spill[:, m, :], x[:, m, :]).then_inc(spilled, 16)

            with sp.Fori(1, KC) as s:
                sp.wait_ge(wchi_done, s)
                sp.wait_ge(wclo_done, s)
                sp.dma_start(wc_raw[:, :, :], wc_in[bass.ds(s, 1), :, :].rearrange("e (k p) n -> p (e k) n", p=P)).then_inc(wc_ld, 16)
            sp.wait_ge(wchi_done, KC)
            sp.wait_ge(wclo_done, KC)
            sp.dma_start(wc_raw[:, :, :], wf_in.rearrange("(k p) n -> p k n", p=P)).then_inc(wc_ld, 16)
            sp.wait_ge(spilled, 16 * NB)
            sp.wait_ge(prop_done, (KC - 2) * NB)
            sp.dma_start(xr[:, :, :], x_spill).then_inc(x_back, 16)
            sp.dma_start(bias1[:, :], bias1_in.partition_broadcast(P)).then_inc(bias1_ld, 16)
            for m in range(NB):
                sp.wait_ge(out_ready, m + 1)
                sp.dma_start(out[m * P:(m + 1) * P, :], b[1][:, m, :]).then_inc(stored, 16)
            sp.wait_ge(stored, 16 * NB)

        @block.gpsimd
        def _(pool):
            steps = [0]

            def link(ins):
                steps[0] += 1
                ins.then_inc(pool_step, 1)
                pool.wait_ge(pool_step, steps[0])

            def iota(out_ap, pattern, base, channel, done):
                nc.gpsimd.iota(out_ap, pattern, base=base, channel_multiplier=channel,
                               allow_small_or_imprecise_dtypes=True).then_inc(done, 1)

            iota(tileno[:, :, :], [[0, 2], [1, 2]], 0, 2, consts)
            link(nc.gpsimd.memset(ident[:, :], 0.0))
            nc.gpsimd.affine_select(out=ident[:, :], in_=ident[:, :], compare_op=ALU.not_equal, fill=1.0, base=0,
                                    pattern=[[-1, P]], channel_multiplier=1).then_inc(consts, 1)
            iota(jconst[:, :, :], [[1, P], [0, 2]], 0, 0, consts)
            iota(wbase[:, :], [[P, NW]], 0, 0, consts)
            nc.gpsimd.memset(jT[:, 0:BEFORE], -1.0).then_inc(consts, 1)
            nc.gpsimd.memset(jT[:, BEFORE + TILES:], -1.0).then_inc(consts, 1)
            nc.gpsimd.memset(nhalf[:, :], -0.5).then_inc(consts, 1)
            iota(iota8[:, :], [[1, 8]], 0, 0, consts)
            nc.gpsimd.memset(comb[:, :, NE - 1], 0.5).then_inc(consts, 1)
            nc.gpsimd.memset(onecol[:, :], 1.0).then_inc(consts, 1)
            pool.wait_ge(consts, 10)
            nc.gpsimd.tensor_copy(identb[:, :], ident[:, :]).then_inc(consts, 1)

            pool.wait_ge(path_ready, 1)
            other = pool.value_load(unsorted[0:1, 0:1], min_val=0, max_val=1)
            with pool.If(other > 0):
                pool.sem_inc(oh_used, RING)
                iota(iotab[:, :], [[1, P]], 0, 0, slow_consts)
                nc.gpsimd.memset(zerob[:, :], 0.0).then_inc(slow_consts, 1)
                iota(wstart[:, 0:1], [[0, 1]], 0, WD, slow_consts)
                iota(wstart[:, 1:2], [[0, 1]], WD, WD, slow_consts)
                nc.gpsimd.memset(ones_w[:, :], 1.0).then_inc(slow_consts, 1)
                iota(iotap[:, 0, :], [[1, PAIRS]], PAIRS, 0, slow_consts)
                iota(iotap[:, 1, :], [[1, PAIRS]], 1, 0, slow_consts)
                nc.gpsimd.memset(tri[:, :], 1.0).then_inc(slow_step, 1)
                pool.wait_ge(slow_step, 1)
                nc.gpsimd.affine_select(out=tri[:, :], in_=tri[:, :], compare_op=ALU.is_ge, fill=0.0, base=-1,
                                        pattern=[[1, NW + 1]], channel_multiplier=-1).then_inc(slow_consts, 1)

            def ln_rows(i, m):
                pool.wait_ge(ln_var[i], m + 1)
                link(nc.gpsimd.tensor_scalar(veps[:, i, m:m + 1], meanvar[:, i, m, 1:2], EPS, None, ALU.add))
                nc.gpsimd.tensor_tensor(rstd[:, i, m:m + 1], veps[:, i, m:m + 1], nhalf[:, 0:1], ALU.pow)\
                    .then_inc(ln_rstd[i], 1)

            def split_lo(out_lo, raw, hi, done):
                nc.gpsimd.tensor_tensor(out_lo, raw, hi.bitcast(F32), ALU.subtract).then_inc(done, 1)

            pool.wait_ge(wg_hi_done, 1)
            split_lo(wg_hilo[:, :, 8:16], wg_raw[:, :, :], wg_hilo[:, :, 0:8], wg_split)
            pool.wait_ge(w0_split, 1)
            split_lo(w0_lo[:, :, :], w0_raw[:, :, :], w0_hi[:, :, :], w0_split)
            def x_biased(m):
                pool.wait_ge(ln_norm[0], m + 1)
                nc.gpsimd.tensor_tensor(x[:, m, :], x[:, m, :], bias0[:, :], ALU.add).then_inc(xb_ready, 1)

            def binary(m):
                for g in (2 * m, 2 * m + 1):
                    pool.wait_ge(win_placed[g % 4], 16 * WG * (g // 4 + 1))
                nc.gpsimd.tensor_scalar(B[:, m, :], AT[:, m, :].bitcast(F32), 1.0, None, ALU.min).then_inc(b_ready, 1)

            pool.wait_ge(bias0_ld, 16)
            for m in range(NB):
                ln_rows(0, m)
                if m:
                    x_biased(m - 1)
                    binary(m - 1)
            x_biased(NB - 1)
            binary(NB - 1)
            for m in range(NB):
                pool.wait_ge(s_rows, m + 1)
                d = S[:, m, m * P:(m + 1) * P]
                link(nc.gpsimd.tensor_scalar(degs[:, 1, m:m + 1], degs[:, 0, m:m + 1], 1.0, None, ALU.add))
                nc.gpsimd.tensor_tensor(degs[:, 2, m:m + 1], degs[:, 1, m:m + 1], nhalf[:, 0:1], ALU.pow).then_inc(dinv0_ready, 1)
                nc.gpsimd.tensor_tensor(d, d.bitcast(F32), ident[:, :], ALU.add).then_inc(s_ready, 1)

            def expert_lo(k, e, i):
                pool.wait_ge(whi_done[k], e + 1)
                split_lo(w_lo[i][k][:, :, :], w_raw[i][k][:, :, :], w_hi[i][k][:, :, :], wlo_done[k])

            for k in range(2):
                expert_lo(k, 0, 0)
            for m in range(NB):
                ln_rows(1, m)
            for k in range(2):
                expert_lo(k, 1, 1)

            def hidden_lo(n, i, j):
                pool.wait_ge(hhi_done, n + 1)
                f, half = j // HALVES, j % HALVES
                cols = slice(half * 512, half * 512 + 512)
                split_lo(h_lo[i][:, f, cols], hrelu[:, j % 2, :], h_hi[i][:, f, cols], hlo_done)

            for j in range(4):
                hidden_lo(j, 0, j)

            pool.wait_ge(deg1_kept, 1)
            nc.gpsimd.tensor_tensor(dinv1, deg1, nhalf[:, :], ALU.pow).then_inc(deg1_pow, 1)
            pool.wait_ge(degmax_ready, 1)
            nc.gpsimd.partition_all_reduce(few[:, 1:2], few[:, 0:1], P, MAX).then_inc(big_all, 1)

            def moe_step(e, i, hidden=True, refill=True):
                if hidden:
                    for j in range(4):
                        hidden_lo(4 * (e + 1) + j, 1 - i, j)
                if refill:
                    expert_lo(0, e + 2, i)
                    expert_lo(1, e + 2, i)

            moe_step(0, 0)
            with pool.Fori(0, 3) as t:
                moe_step(2 * t + 1, 1)
                moe_step(2 * t + 2, 0)
            moe_step(7, 1, refill=False)

            def cheb_lo(s, i):
                pool.wait_ge(wchi_done, s + 1)
                split_lo(wc_lo[i][:, :, :], wc_raw[:, :, :], wc_hi[i][:, :, :], wclo_done)

            cheb_lo(0, 0)
            for m in range(NB):
                ln_rows(2, m)
            pool.wait_ge(moe_added, (NE + 1) * NB)
            nc.gpsimd.memset(b[0][:, :, :], 0.0).then_inc(b_zero, 1)
            nc.gpsimd.memset(b[1][:, :, :], 0.0).then_inc(b_zero, 1)
            cheb_lo(1, 1)
            with pool.Fori(0, 3) as t:
                for i in range(2):
                    cheb_lo(2 * t + i + 2, i)
            pool.wait_ge(x_back, 16)
            pool.wait_ge(bias1_ld, 16)
            for m in range(NB):
                nc.gpsimd.tensor_tensor(xr[:, m, :], xr[:, m, :], bias1[:, :], ALU.add).then_inc(xr_ready, 1)
            pool.wait_ge(wamax, 1)
            nc.gpsimd.partition_all_reduce(few[:, 3:4], few[:, 2:3], P, ABSMAX).then_inc(wamax_all, 1)
            for m in range(NB):
                ln_rows(3, m)
            pool.wait_ge(xamax, 1)
            nc.gpsimd.partition_all_reduce(few[:, 7:8], few[:, 6:7], P, ABSMAX).then_inc(xamax_all, 1)

        @block.scalar
        def _(act):
            def copy(out_ap, in_ap, done, scale=1.0):
                nc.scalar.activation(out_ap, in_ap, ACT.Copy, scale=scale).then_inc(done, 1)

            def turn_hi(i, m):
                act.wait_ge(ln_turned[i], m + 1)
                copy(xT_hi[:, :, m * P:(m + 1) * P],
                     bank[6 + m % 2][:, :].rearrange("p (k n) -> p k n", k=KD), ln_hi[i])

            act.wait_ge(small_ld, 48)
            copy(wg_hilo[:, :, 0:8], wg_raw[:, :, :], wg_hi_done)
            act.wait_ge(w0_ld, 16)
            copy(w0_hi[:, :, :], w0_raw[:, :, :], w0_split)
            for kt in range(NB):
                turn_hi(0, kt)
                for g in (2 * kt, 2 * kt + 1):
                    act.wait_ge(win_done, g + 1)
                    if g >= 4:
                        act.wait_ge(win_placed[g % 4], 16 * WG * (g // 4))
                    copy(stage[:, g % 4, :, :], bank[g % 4][:, :].rearrange("p (q n) -> p q n", q=WG), win_staged)
                if kt:
                    act.wait_ge(y_done, kt)
                    copy(y[:, kt - 1, :], bank[4 + (kt - 1) % 2][:, :], y_kept)
            act.wait_ge(y_done, NB)
            copy(y[:, NB - 1, :], bank[4 + (NB - 1) % 2][:, :], y_kept)
            act.wait_ge(y_kept, NB)
            for m in range(NB):
                act.wait_ge(dinv0_ready, m + 1)
                copy(y_hi[:, m, :], y[:, m, :], y_hi_ready, scale=degs[:, 2, m:m + 1])

            def expert_hi(k, e, i, e_half):
                act.wait_ge(raw_ld[k][i], 16 * (e_half + 1))
                copy(w_hi[i][k][:, :, :], w_raw[i][k][:, :, :], whi_done[k])

            for k in range(2):
                expert_hi(k, 0, 0, 0)
            for m in range(NB):
                turn_hi(1, m)
            for k in range(2):
                expert_hi(k, 1, 1, 0)

            def hidden(e, i, j):
                n = 4 * e + j
                act.wait_ge(h_done, n + 1)
                if not (isinstance(n, int) and n < 2):
                    act.wait_ge(hlo_done, n - 1)
                f = j // HALVES
                nc.scalar.activation(hrelu[:, j % 2, :], bank[j][:, :], ACT.Relu, bias=b1cur[:, i, f:f + 1]).then_inc(relu_done, 1)

            def hidden_bias(e, i):
                copy(b1cur[:, i, :], b1T[:, bass.ds(e * FB, FB)], b1_kept)
                act.wait_ge(b1_kept, e + 1)

            hidden_bias(0, 0)
            for j in range(4):
                hidden(0, 0, j)
            act.wait_ge(topdiff, 1)
            nc.scalar.activation(pair[:, 1, :], pair[:, 0, :], ACT.Exp).then_inc(topexp, 1)

            def moe_step(e, i, t, nxt=True, refill=True):
                if nxt:
                    hidden_bias(e + 1, 1 - i)
                    for j in range(4):
                        hidden(e + 1, 1 - i, j)
                if refill:
                    act.wait_ge(h_done, 4 * (e + 1))
                    expert_hi(0, e + 2, i, t + 1)
                    act.wait_ge(moe_done, NB * (e + 2))
                    expert_hi(1, e + 2, i, t + 1)

            moe_step(0, 0, 0)
            with act.Fori(0, 3) as t:
                moe_step(2 * t + 1, 1, t)
                moe_step(2 * t + 2, 0, t + 1)
            moe_step(7, 1, 3, refill=False)

            def cheb_hi(s, i):
                act.wait_ge(wc_ld, 16 * (s + 1))
                if not isinstance(s, int) or s >= 2:
                    act.wait_ge(xw_done, NB * (s - 1))
                copy(wc_hi[i][:, :, :], wc_raw[:, :, :], wchi_done)

            cheb_hi(0, 0)
            for m in range(NB):
                turn_hi(2, m)
            act.wait_ge(moe_added, (NE + 1) * NB)
            cheb_hi(1, 1)

            def scaled_hi(s, m, i):
                act.wait_ge(b_done, NB * s + m + 1)
                copy(c_hi[i][:, m, :], b[i][:, m, :], chi_done, scale=degs[:, 4, m:m + 1])

            act.wait_ge(dinv1_ready, 1)
            act.wait_ge(spilled, 16 * NB)
            for m in range(NB):
                scaled_hi(0, m, 0)
            with act.Fori(0, 3) as t:
                for j in range(2):
                    s = 2 * t + 1 + j
                    for m in range(NB):
                        scaled_hi(s, m, 1 - j)
                        if m == 0:
                            cheb_hi(s + 1, j)
            for m in range(NB):
                act.wait_ge(ln_turned[3], m + 1)
                copy(xhT[:, :, m * P:(m + 1) * P],
                     bank[6 + m % 2][:, :].rearrange("p (k n) -> p k n", k=KD), xT_kept)

        @block.vector
        def _(dve):
            chain = [0, 0]

            def new_chain():
                chain[:] = [chain[0] + 1, 0]

            def link(ins):
                chain[1] += 1
                ins.then_inc(dve_step[chain[0]], 1)
                dve.wait_ge(dve_step[chain[0]], chain[1])

            def ln_stats(i, m, rows):
                link(nc.vector.bn_stats(stats[:, m, :], rows))
                nc.vector.bn_aggr(meanvar[:, i, m, :], stats[:, m, :]).then_inc(ln_var[i], 1)

            def ln_norm_block(i, m, rows):
                dve.wait_ge(ln_rstd[i], m + 1)
                if m >= 2:
                    dve.wait_ge(ln_turned[i], m - 1)
                nc.vector.tensor_scalar(xh[:, m % 2, :], rows, meanvar[:, i, m, 0:1], rstd[:, i, m:m + 1],
                                        ALU.subtract, ALU.mult).then_inc(ln_norm[i], 1)

            def turn_lo(i, m):
                dve.wait_ge(ln_hi[i], m + 1)
                cols = slice(m * P, (m + 1) * P)
                nc.vector.tensor_tensor(xT_lo[:, :, cols], bank[6 + m % 2][:, :].rearrange("p (k n) -> p k n", k=KD),
                                        xT_hi[:, :, cols].bitcast(F32), ALU.subtract).then_inc(ln_lo[i], 1)

            dve.wait_ge(edges_in, 32)
            halves = dst_i[:, :].rearrange("p (h n) -> p h n", h=2)
            nc.vector.tensor_reduce(tilemm_i[:, 0, :], halves, AX_X, ALU.min)
            nc.vector.tensor_scalar(shi_i[:, :], src_i[:, :], SL.bit_length() - 1, None, ALU.logical_shift_right)
            nc.vector.tensor_scalar(slo_i[:, :], src_i[:, :], SL - 1, None, ALU.bitwise_and)
            link(nc.vector.tensor_reduce(tilemm_i[:, 1, :], halves, AX_X, ALU.max))
            nc.vector.scalar_tensor_tensor(joint[:, :], dst_i[:, :], float(SH), shi_i[:, :], ALU.mult, ALU.add).then_inc(idx_rows, 1)
            nc.vector.tensor_copy(slo[:, :], slo_i[:, :]).then_inc(idx_rows, 1)
            link(nc.vector.tensor_scalar(tilewin[:, :, :], tilemm_i[:, :, :], N - WD, None, ALU.bitwise_and))
            dve.wait_ge(consts, 11)
            link(nc.vector.scalar_tensor_tensor(tilemm[:, :, :], tilewin[:, :, :], float(TPW) / WD, tileno[:, :, :],
                                                ALU.mult, ALU.subtract))
            nc.vector.tensor_reduce(off[:, 0:1], tilemm[:, 1, :], AX_X, ALU.max)
            link(nc.vector.tensor_reduce(off[:, 1:2], tilemm[:, 0, :], AX_X, ALU.min))
            nc.vector.tensor_scalar(off[:, 2:3], off[:, 0:1], float(BEFORE), None, ALU.subtract)
            link(nc.vector.tensor_scalar(off[:, 3:4], off[:, 1:2], -1.0, -float(VIS - 1 - BEFORE), ALU.mult, ALU.add))
            nc.vector.tensor_tensor(off[:, 0:1], off[:, 2:3], off[:, 3:4], ALU.max).then_inc(off_ready, 1)
            dve.wait_ge(idx_turned, 1)
            turned = bank[2][:, :].rearrange("p (c h t) -> p c t h", c=2, h=2)
            nc.vector.tensor_copy(jT[:, BEFORE:BEFORE + TILES].rearrange("p (t h) -> p t h", h=2), turned[:, 0, :, :]).then_inc(idx_kept, 1)
            nc.vector.tensor_copy(sT[:, :].rearrange("p (t h) -> p t h", h=2), turned[:, 1, :, :]).then_inc(idx_kept, 1)
            dve.wait_ge(off_row, 1)
            link(nc.vector.tensor_reduce(offall[:, :], bank[3][0:1, 0:P], AX_X, ALU.max))
            nc.vector.tensor_scalar(unsorted[:, :], offall[:, :], 0.0, None, ALU.is_gt).then_inc(path_ready, 1)
            dve.wait_ge(idx_kept, 2)

            def cols_of(c):
                shape = [P, CHUNK // 2, SL, 2]
                idx = sT[:, c * CHUNK:(c + 1) * CHUNK].rearrange("p (t o h) -> p t o h", o=1, h=2).broadcast_to(shape)
                j = jconst[:, 0:SL, :].rearrange("p (o n) h -> p o n h", o=1).broadcast_to(shape)
                return nc.vector.tensor_tensor(oh_cols[c % 5][:, :, :, :], idx, j, ALU.is_equal)

            def rows_of(g):
                shape = [P, WG * VIS // 2, P, 2]
                idx = rel[:, g * WG:(g + 1) * WG, :].rearrange("p w (t o h) -> p (w t) o h", o=1, h=2).broadcast_to(shape)
                j = jconst[:, :, :].rearrange("p (o n) h -> p o n h", o=1).broadcast_to(shape)
                return nc.vector.tensor_tensor(oh_rows[g % 2][:, :, :, :], idx, j, ALU.is_equal)

            def sorted_path():
                for a in range(0, VIS, TPW):
                    n = min(TPW, VIS - a)
                    tiles = jT[:, a:a + TILES].rearrange("p (w f) -> p w f", f=TPW)[:, :, 0:n]
                    base_w = wbase[:, :].rearrange("p (w o) -> p w o", o=1).broadcast_to([P, NW, n])
                    last = nc.vector.tensor_tensor(rel[:, :, a:a + n], tiles, base_w, ALU.subtract)
                cols_of(0)
                link(last)
                for kt in range(NB):
                    for g in (2 * kt, 2 * kt + 1):
                        if g >= 2:
                            dve.wait_ge(win_done, g - 1)
                        if g + 1 < NG:
                            cols_of(g + 1)
                        rows_of(g).then_inc(oh_ready, 1)
                    first_norm(kt)

            def first_norm(kt):
                dve.wait_ge(x_ld[kt], 16)
                ln_stats(0, kt, x[:, kt, :])
                if kt:
                    turn_lo(0, kt - 1)
                ln_norm_block(0, kt, x[:, kt, :])

            def general_path():
                dve.wait_ge(slow_consts, 8)
                nc.vector.tensor_copy(sF[:, :], sT[:, :])
                nc.vector.tensor_reduce(pairmm[:, 0:1], dst_i[:, :], AX_X, ALU.min)
                link(nc.vector.tensor_reduce(pairmm[:, 1:2], dst_i[:, :], AX_X, ALU.max))
                for c in range(2):
                    nc.vector.tensor_scalar(diag[:, c, :], ident[:, :], pairmm[:, c:c + 1], None, ALU.mult).then_inc(diag_ready, 1)
                dve.wait_ge(pair_rows, 1)
                link(nc.vector.tensor_scalar(wmask[:, 0, :], bank[3][0:NW, 0:PAIRS], wstart[:, 1:2], None, ALU.is_lt))
                link(nc.vector.scalar_tensor_tensor(wmask[:, 1, :], bank[3][0:NW, PAIRS:2 * PAIRS], wstart[:, 0:1],
                                                    wmask[:, 0, :], ALU.is_ge, ALU.mult))
                nc.vector.scalar_tensor_tensor(wsel[:, 0, :], wmask[:, 1, :], -float(PAIRS), iotap[:, 0, :], ALU.mult, ALU.add)
                link(nc.vector.tensor_tensor(wsel[:, 1, :], wmask[:, 1, :], iotap[:, 1, :], ALU.mult))
                nc.vector.tensor_reduce(wcol[:, 0:1], wsel[:, 0, :], AX_X, ALU.min)
                link(nc.vector.tensor_reduce(wcol[:, 1:2], wsel[:, 1, :], AX_X, ALU.max))
                link(nc.vector.tensor_scalar(wcol[:, 2:3], wcol[:, 0:1], float(PAIRS - 1), None, ALU.min))
                link(nc.vector.tensor_tensor(wcol[:, 3:4], wcol[:, 1:2], wcol[:, 2:3], ALU.subtract))
                nc.vector.tensor_scalar(wcol[:, 3:4], wcol[:, 3:4], 1.0, None, ALU.max).then_inc(wcol_ready, 1)
                dve.wait_ge(tab_rows, 1)
                link(nc.vector.tensor_copy(tabf[:, :], bank[3][0:1, 0:NW + 1]))
                nc.vector.tensor_copy(tab[:, 0:NW + 1], tabf[:, :]).then_inc(tab_ready, 1)
                nc.vector.tensor_tensor(tab[:, NW + 1:2 * NW + 1], bank[3][0:1, P:P + NW], tabf[:, 0:NW], ALU.subtract).then_inc(tab_ready, 1)
                dve.wait_ge(tab_ready, 2)
                for kt in range(NB):
                    for w in range(2 * WG * kt, 2 * WG * (kt + 1)):
                        first = dve.value_load(tab[0:1, w:w + 1], min_val=0, max_val=NW * PAIRS)
                        after = dve.value_load(tab[0:1, w + 1:w + 2], min_val=1, max_val=NW * PAIRS)
                        shift = dve.value_load(tab[0:1, NW + 1 + w:NW + 2 + w])
                        with dve.Fori(first, after) as v:
                            dve.wait_ge(oh_used, v + 1)
                            slot = v & (RING - 1)
                            for h in range(2):
                                tile = (v + shift) * 2 + h
                                nc.vector.tensor_scalar(oh_row[:, bass.ds(slot, 1), h, :], iotab[:, :].rearrange("p (a n) -> p a n", a=1),
                                                        wbase[:, w:w + 1], jT[:, bass.ds(tile + BEFORE, 1)], ALU.add, ALU.is_equal)
                                last = nc.vector.tensor_scalar(oh_col[:, bass.ds(slot, 1), h, :], iotab[:, :].rearrange("p (a n) -> p a n", a=1),
                                                               sF[:, bass.ds(tile, 1)], None, ALU.is_equal)
                            last.then_inc(oh_ready, 1)
                    first_norm(kt)

            dve.wait_ge(path_ready, 1)
            other = dve.value_load(unsorted[0:1, 0:1], min_val=0, max_val=1)
            with dve.If(other > 0):
                new_chain()
                general_path()
            with dve.Else():
                new_chain()
                sorted_path()
            new_chain()
            turn_lo(0, NB - 1)

            dve.wait_ge(xb_ready, NB)
            for m in range(NB + 1):
                if m < NB:
                    dve.wait_ge(bt_done, m + 1)
                    nc.vector.scalar_tensor_tensor(S[:, m, :], B[:, m, :], 1.0, bank[2 + m % 2][:, :].bitcast(BF16), ALU.mult, ALU.max,
                                                   accum_out=degs[:, 0, m:m + 1]).then_inc(s_rows, 1)
                if m:
                    dve.wait_ge(y_hi_ready, m)
                    nc.vector.scalar_tensor_tensor(y_lo[:, m - 1, :], y[:, m - 1, :], degs[:, 2, m - 1:m], y_hi[:, m - 1, :].bitcast(F32),
                                                   ALU.mult, ALU.subtract).then_inc(y_lo_ready, 1)
            for m in range(NB + 2):
                if m < NB:
                    dve.wait_ge(gcn_done, m + 1)
                    dve.wait_ge(xb_ready, m + 1)
                    nc.vector.scalar_tensor_tensor(x[:, m, :], bank[4 + m % 2][:, :], degs[:, 2, m:m + 1], x[:, m, :],
                                                   ALU.mult, ALU.add).then_inc(gcn_kept, 1)
                    dve.wait_ge(gcn_kept, m + 1)
                    ln_stats(1, m, x[:, m, :])
                if 1 <= m < NB + 1:
                    ln_norm_block(1, m - 1, x[:, m - 1, :])
                if m >= 2:
                    turn_lo(1, m - 2)

            def hidden_hi(n, i, j):
                dve.wait_ge(relu_done, n + 1)
                f, half = j // HALVES, j % HALVES
                nc.vector.tensor_copy(h_hi[i][:, f, half * 512:half * 512 + 512], hrelu[:, j % 2, :]).then_inc(hhi_done, 1)

            for j in range(4):
                hidden_hi(j, 0, j)

            dve.wait_ge(gate_done, 1)
            for m in range(NB):
                last = nc.vector.tensor_tensor(gate[:, m, :], bank[4][:, 8 * m:8 * m + 8], bgb[:, :], ALU.add)
            link(last)
            for m in range(NB):
                last = nc.vector.max(top8[:, m, :], gate[:, m, :])
            link(last)
            for m in range(NB):
                last = nc.vector.max_index(top8i[:, m, :], top8[:, m, :], gate[:, m, :])
            nc.vector.tensor_tensor(pair[:, 0, :], top8[:, :, 1], top8[:, :, 0], ALU.subtract).then_inc(topdiff, 1)
            link(nc.vector.engine_nop())
            nc.vector.tensor_copy(topi[:, :, :], top8i[:, :, 0:2])
            dve.wait_ge(topexp, 1)
            link(nc.vector.tensor_scalar(pair[:, 2, :], pair[:, 1, :], 1.0, None, ALU.add))
            link(nc.vector.reciprocal(pair[:, 3, :], pair[:, 2, :]))
            link(nc.vector.tensor_tensor(pair[:, 4, :], pair[:, 1, :], pair[:, 3, :], ALU.mult))
            for m in range(NB):
                nc.vector.tensor_scalar(sel1[:, m, :], iota8[:, :], topi[:, m, 0:1], pair[:, 3, m:m + 1], ALU.is_equal, ALU.mult)
                last = nc.vector.tensor_scalar(sel2[:, m, :], iota8[:, :], topi[:, m, 1:2], pair[:, 4, m:m + 1], ALU.is_equal, ALU.mult)
            link(last)
            nc.vector.tensor_tensor(comb[:, :, 0:8], sel1[:, :, :], sel2[:, :, :], ALU.add).then_inc(comb_ready, 1)
            for g in range(2):
                dve.wait_ge(combT_done, g + 1)
                nc.vector.tensor_copy(combT[:, g * 512:(g + 1) * 512], bank[6 + g][0:NE, :]).then_inc(combT_kept, 1)

            dve.wait_ge(deg1_done, 1)
            nc.vector.tensor_scalar(degs[:, 7, :], bank[5][:, 0:NB], 0.0, None, ALU.is_gt)
            nc.vector.tensor_scalar(degs[:, 3, :], bank[5][:, 0:NB], 1e-30, None, ALU.max).then_inc(deg1_kept, 1)
            nc.vector.tensor_reduce(few[:, 0:1], AT[:, :, :].bitcast(F32).rearrange("p k n -> p (k n)"), AX_X, ALU.max).then_inc(degmax_ready, 1)
            dve.wait_ge(deg1_pow, 1)
            link(nc.vector.tensor_tensor(degs[:, 4, :], degs[:, 4, :], degs[:, 7, :], ALU.mult))
            nc.vector.tensor_scalar(degs[:, 5, :], degs[:, 4, :], -2.0, None, ALU.mult)
            nc.vector.tensor_scalar(degs[:, 6, :], degs[:, 4, :], -1.0, None, ALU.mult).then_inc(dinv1_ready, 1)
            dve.wait_ge(big_all, 1)
            nc.vector.tensor_scalar(bigflag[0:1, 0:1], few[0:1, 1:2], float(EXACT), None, ALU.is_gt).then_inc(big_ready, 1)

            def biases_added(m):
                dve.wait_ge(moe_done, m + 1)
                nc.vector.scalar_tensor_tensor(x[:, m, :], bank[4 + m % 2][:, :], 1.0, x[:, m, :], ALU.mult, ALU.add).then_inc(moe_added, 1)

            for j in range(4):
                hidden_hi(4 + j, 1, j)
            for m in range(NB):
                biases_added(m)

            def expert_added(e, m):
                dve.wait_ge(moe_done, NB * (e + 1) + m + 1)
                if isinstance(e, int):
                    weight = comb[:, m, e:e + 1]
                else:
                    weight = comb[:, m, bass.ds(e, 1)]
                nc.vector.scalar_tensor_tensor(x[:, m, :], bank[4 + m % 2][:, :], weight, x[:, m, :], ALU.mult, ALU.add).then_inc(moe_added, 1)

            def moe_step(e, i, nxt=True):
                if nxt:
                    for j in range(4):
                        hidden_hi(4 * (e + 1) + j, 1 - i, j)
                for m in range(NB):
                    expert_added(e, m)

            for m in range(NB):
                expert_added(0, m)
            with dve.Fori(0, 3) as t:
                moe_step(2 * t + 1, 1)
                moe_step(2 * t + 2, 0)
            moe_step(7, 1)
            for m in range(NB + 2):
                if m < NB:
                    expert_added(NE - 1, m)
                    dve.wait_ge(moe_added, NE * NB + m + 1)
                    ln_stats(2, m, x[:, m, :])
                if 1 <= m < NB + 1:
                    ln_norm_block(2, m - 1, x[:, m - 1, :])
                if m >= 2:
                    turn_lo(2, m - 2)

            def take_xw(s, m, i):
                dve.wait_ge(xw_done, NB * s + m + 1)
                nc.vector.tensor_tensor(b[i][:, m, :], bank[m % 4][:, :], b[i][:, m, :], ALU.subtract).then_inc(xw_taken, 1)

            def propagate(s, m, i, factor, banks=4):
                dve.wait_ge(prop_done, NB * (s - 1) + m + 1)
                dve.wait_ge(xw_taken, NB * s + m + 1)
                return nc.vector.scalar_tensor_tensor(b[i][:, m, :], bank[4 + m % banks][:, :], degs[:, factor, m:m + 1], b[i][:, m, :],
                                                      ALU.mult, ALU.add).then_inc(b_done, 1)

            def scaled_lo(s, m, i):
                dve.wait_ge(chi_done, NB * s + m + 1)
                nc.vector.scalar_tensor_tensor(c_lo[i][:, m, :], b[i][:, m, :], degs[:, 4, m:m + 1], c_hi[i][:, m, :].bitcast(F32),
                                               ALU.mult, ALU.subtract).then_inc(clo_done, 1)

            dve.wait_ge(b_zero, 2)
            for m in range(NB + 1):
                if m < NB:
                    dve.wait_ge(xw_done, m + 1)
                    nc.vector.tensor_tensor(b[0][:, m, :], bank[m % 4][:, :], b[0][:, m, :], ALU.subtract).then_inc(b_done, 1)
                if m:
                    scaled_lo(0, m - 1, 0)
            for m in range(NB):
                last = nc.vector.engine_nop().then_inc(xw_taken, 1)

            def cheb_step(s, i):
                take_xw(s, 0, i)
                take_xw(s, 1, i)
                for m in range(NB):
                    propagate(s, m, i, 5)
                    if m + 2 < NB:
                        take_xw(s, m + 2, i)
                    if m:
                        scaled_lo(s, m - 1, i)
                scaled_lo(s, NB - 1, i)

            with dve.Fori(0, 3) as t:
                for j in range(2):
                    cheb_step(2 * t + 1 + j, 1 - j)

            def round_fp8(q_out, v, scale, e_s, mag_s, sum_s):
                link(nc.vector.tensor_scalar(v, v, scale, FP8_MAX, ALU.mult, ALU.min))
                link(nc.vector.tensor_scalar(e_s, v.bitcast(I32), 0x7F800000, None, ALU.bitwise_and))
                link(nc.vector.tensor_scalar(mag_s, e_s.bitcast(F32), 2.0 ** -6, 1.5 * 2.0 ** 20, ALU.max, ALU.mult))
                link(nc.vector.scalar_tensor_tensor(sum_s, v, -FP8_MAX, mag_s, ALU.max, ALU.add))
                return nc.vector.tensor_tensor(q_out, sum_s, mag_s, ALU.subtract)

            def scale_of(amax_all, scale, inverse):
                link(nc.vector.tensor_scalar(inverse, amax_all, 1e-12, None, ALU.max))
                link(nc.vector.reciprocal(scale, inverse))
                link(nc.vector.tensor_scalar(scale, scale, FP8_MAX, None, ALU.mult))
                link(nc.vector.reciprocal(inverse, scale))

            S7 = KC - 1
            take_xw(S7, 0, 1)
            take_xw(S7, 1, 1)
            dve.wait_ge(wc_ld, 16 * (KC + 1))
            nc.vector.tensor_reduce(few[:, 2:3], wc_raw[:, :, :].rearrange("p k n -> p (k n)"), AX_X, ALU.max,
                                    apply_absolute_value=True).then_inc(wamax, 1)
            for m in range(NB + 3):
                if m < NB:
                    propagate(S7, m, 1, 6, banks=2)
                    if m + 2 < NB:
                        take_xw(S7, m + 2, 1)
                    dve.wait_ge(b_done, NB * S7 + m + 1)
                    dve.wait_ge(xr_ready, m + 1)
                    nc.vector.tensor_tensor(b[1][:, m, :], b[1][:, m, :], xr[:, m, :], ALU.add).then_inc(x3_ready, 1)
                    dve.wait_ge(x3_ready, m + 1)
                    ln_stats(3, m, b[1][:, m, :])
                if 1 <= m < NB + 1:
                    ln_norm_block(3, m - 1, b[1][:, m - 1, :])
                    dve.wait_ge(ln_norm[3], m)
                    link(nc.vector.tensor_reduce(few[:, 8 + m - 1:8 + m], xh[:, (m - 1) % 2, :], AX_X, ALU.max,
                                                 apply_absolute_value=True))
            nc.vector.tensor_reduce(few[:, 6:7], few[:, 8:8 + NB], AX_X, ALU.max).then_inc(xamax, 1)
            dve.wait_ge(wamax_all, 1)
            scale_of(few[:, 3:4], few[:, 4:5], few[:, 5:6])
            for k in range(KD):
                round_fp8(wq[:, k, :], wc_raw[:, k, :], few[:, 4:5], qexpw[:, :], qmagw[:, :], qsumw[:, :]).then_inc(wq_ready, 1)
                dve.wait_ge(wq_ready, k + 1)
            dve.wait_ge(xamax_all, 1)
            scale_of(few[:, 7:8], few[:, 16:17], few[:, 17:18])
            link(nc.vector.tensor_tensor(few[:, 18:19], few[:, 17:18], few[:, 5:6], ALU.mult))
            dve.wait_ge(xT_kept, NB)
            for half in range(HALVES):
                for k in range(KD):
                    cols = slice(half * 512, half * 512 + 512)
                    round_fp8(xq[:, k, cols], xhT[:, k, cols], few[:, 16:17], qexp[:, :], qmag[:, :], qsum[:, :]).then_inc(xq_ready, 1)
                    dve.wait_ge(xq_ready, KD * half + k + 1)
            for m in range(NB):
                dve.wait_ge(fp8_done, m + 1)
                nc.vector.scalar_tensor_tensor(b[1][:, m, :], bank[m % 4][:, :], few[:, 18:19], b[1][:, m, :],
                                               ALU.mult, ALU.add).then_inc(out_ready, 1)

        @block.tensor
        def _(pe):
            def mm(out_ap, lhsT, rhs, start, stop):
                return nc.tensor.matmul(out_ap, lhsT, rhs, start=start, stop=stop)

            def product(out_ap, terms):
                for n, (a, c) in enumerate(terms):
                    last = mm(out_ap, a, c, n == 0, n == len(terms) - 1)
                return last

            def turn(i, m):
                pe.wait_ge(ln_norm[i], m + 1)
                if m >= 2:
                    pe.wait_ge(ln_lo[i] if i < 3 else xT_kept, m - 1)
                for k in range(KD):
                    last = nc.tensor.transpose(bank[6 + m % 2][:, k * P:(k + 1) * P], xh[:, m % 2, k * P:(k + 1) * P], ident[:, :])
                last.then_inc(ln_turned[i], 1)

            def x_times(w_hi_ap, w_lo_ap, m):
                rows = slice(m * P, (m + 1) * P)
                t = []
                for k in range(KD):
                    t.append((xT_hi[:, k, rows], w_hi_ap[:, k, :]))
                    t.append((xT_hi[:, k, rows], w_lo_ap[:, k, :]))
                    t.append((xT_lo[:, k, rows], w_hi_ap[:, k, :]))
                return t

            pe.wait_ge(consts, 11)
            pe.wait_ge(idx_rows, 2)
            for c, rows in enumerate((joint, slo)):
                for h in range(2):
                    last = nc.tensor.transpose(bank[2][:, (2 * c + h) * P:(2 * c + h + 1) * P], rows[:, h * P:(h + 1) * P], ident[:, :])
            last.then_inc(idx_turned, 1)
            pe.wait_ge(off_ready, 1)
            nc.tensor.transpose(bank[3][0:1, 0:P], off[:, 0:1], ident[:, :]).then_inc(off_row, 1)

            def y_block(m):
                pe.wait_ge(ln_lo[0], m + 1)
                pe.wait_ge(ln_hi[0], m + 1)
                if m == 0:
                    pe.wait_ge(w0_split, 2)
                if m >= 2:
                    pe.wait_ge(y_kept, m - 1)
                product(bank[4 + m % 2][:, :], x_times(w0_hi, w0_lo, m)).then_inc(y_done, 1)

            def between(kt):
                turn(0, kt)
                if kt:
                    y_block(kt - 1)

            def sorted_path():
                for kt in range(NB):
                    for g in (2 * kt, 2 * kt + 1):
                        if g >= 4:
                            pe.wait_ge(win_staged, g - 3)
                        pe.wait_ge(oh_ready, g + 1)
                        for q in range(WG):
                            w = g * WG + q
                            t = []
                            for i in range(VIS):
                                tile = TPW * w - BEFORE + i
                                if 0 <= tile < TILES:
                                    c, n = tile // CHUNK, tile % CHUNK
                                    t.append((oh_rows[g % 2][:, (q * VIS + i) // 2, :, i % 2],
                                              oh_cols[c % 5][:, n // 2, :, n % 2]))
                            last = product(bank[g % 4][:, q * SL:(q + 1) * SL], t)
                        last.then_inc(win_done, 1)
                    between(kt)

            def general_path():
                pe.wait_ge(slow_consts, 8)
                pe.wait_ge(diag_ready, 2)
                mm(bank[3][0:NW, 0:2 * PAIRS], ones_w[:, :], diag[:, :, :], True, True).then_inc(pair_rows, 1)
                pe.wait_ge(wcol_ready, 1)
                mm(bank[3][0:1, 0:NW + 1], wcol[:, 3:4], tri[:, :], True, True)
                mm(bank[3][0:1, P:P + NW], wcol[:, 2:3], ident[0:NW, 0:NW], True, True).then_inc(tab_rows, 1)
                pe.wait_ge(tab_ready, 2)
                for kt in range(NB):
                    for g in (2 * kt, 2 * kt + 1):
                        if g >= 4:
                            pe.wait_ge(win_staged, g - 3)
                        for q in range(WG):
                            w = g * WG + q
                            sums = bank[g % 4][:, q * SL:(q + 1) * SL]
                            mm(sums, zerob[:, :], iotab[:, :], True, False)
                            first = pe.value_load(tab[0:1, w:w + 1], min_val=0, max_val=NW * PAIRS)
                            after = pe.value_load(tab[0:1, w + 1:w + 2], min_val=1, max_val=NW * PAIRS)
                            with pe.Fori(first, after) as v:
                                pe.wait_ge(oh_ready, v + 1)
                                slot = v & (RING - 1)
                                for h in range(2):
                                    last = mm(sums, oh_row[:, bass.ds(slot, 1), h, :], oh_col[:, bass.ds(slot, 1), h, :], False, False)
                                last.then_inc(oh_used, 1)
                            last = mm(sums, zerob[:, :], iotab[:, :], False, True)
                        last.then_inc(win_done, 1)
                    between(kt)

            pe.wait_ge(idx_kept, 2)
            pe.wait_ge(path_ready, 1)
            other = pe.value_load(unsorted[0:1, 0:1], min_val=0, max_val=1)
            with pe.If(other > 0):
                general_path()
            with pe.Else():
                sorted_path()
            y_block(NB - 1)

            pe.wait_ge(b_ready, NB)
            pe.wait_ge(win_staged, NG)
            for m in range(NB):
                if m >= 2:
                    pe.wait_ge(s_rows, m - 1)
                for j in range(NB):
                    last = nc.tensor.transpose(bank[2 + m % 2][:, :].bitcast(BF16)[:, j * P:(j + 1) * P], B[:, j, m * P:(m + 1) * P], identb[:, :])
                last.then_inc(bt_done, 1)

            for m in range(NB + 2):
                if m < NB:
                    if m >= 2:
                        pe.wait_ge(gcn_kept, m - 1)
                    else:
                        pe.wait_ge(y_kept, NB)
                    rows = slice(m * P, (m + 1) * P)
                    for k in range(NB):
                        if m == 0:
                            pe.wait_ge(s_ready, k + 1)
                            pe.wait_ge(y_hi_ready, k + 1)
                            pe.wait_ge(y_lo_ready, k + 1)
                        mm(bank[4 + m % 2][:, :], S[:, k, rows], y_hi[:, k, :], k == 0, False)
                        last = mm(bank[4 + m % 2][:, :], S[:, k, rows], y_lo[:, k, :], False, k == NB - 1)
                    last.then_inc(gcn_done, 1)
                if m >= 2:
                    turn(1, m - 2)

            pe.wait_ge(ln_lo[1], NB)

            def hidden(e, i):
                pe.wait_ge(whi_done[0], e + 1)
                pe.wait_ge(wlo_done[0], e + 1)
                for j in range(4):
                    if not (isinstance(e, int) and e == 0):
                        pe.wait_ge(relu_done, 4 * (e - 1) + j + 1)
                    f, half = j // HALVES, j % HALVES
                    cols, fs = slice(half * 512, half * 512 + 512), slice(f * P, (f + 1) * P)
                    t = []
                    for k in range(KD):
                        t.append((w_hi[i][0][:, k, fs], xT_hi[:, k, cols]))
                        t.append((w_hi[i][0][:, k, fs], xT_lo[:, k, cols]))
                        t.append((w_lo[i][0][:, k, fs], xT_hi[:, k, cols]))
                    product(bank[j][:, :], t).then_inc(h_done, 1)

            def expert_out(e, i, last=False):
                pe.wait_ge(whi_done[1], e + 1)
                pe.wait_ge(wlo_done[1], e + 1)
                pe.wait_ge(hlo_done, 4 * (e + 1))
                for m in range(NB):
                    pe.wait_ge(moe_added, NB * (e + 1) + m - 1)
                    rows = slice(m * P, (m + 1) * P)
                    t = []
                    for f in range(FB):
                        t.append((h_hi[i][:, f, rows], w_hi[i][1][:, f, :]))
                        t.append((h_hi[i][:, f, rows], w_lo[i][1][:, f, :]))
                        t.append((h_lo[i][:, f, rows], w_hi[i][1][:, f, :]))
                    product(bank[4 + m % 2][:, :], t).then_inc(moe_done, 1)
                    if last and m >= 2:
                        turn(2, m - 2)

            hidden(0, 0)
            pe.wait_ge(wg_split, 1)
            pe.wait_ge(gcn_kept, NB)
            for m in range(NB):
                rows, g = slice(m * P, (m + 1) * P), bank[4][:, 8 * m:8 * m + 8]
                t = []
                for k in range(KD):
                    t.append((xT_hi[:, k, rows], wg_hilo[:, k, 0:8]))
                    t.append((xT_hi[:, k, rows], wg_hilo[:, k, 8:16]))
                    t.append((xT_lo[:, k, rows], wg_hilo[:, k, 0:8]))
                last = product(g, t)
            last.then_inc(gate_done, 1)
            for m in range(NB):
                rows = slice(m * P, (m + 1) * P)
                last = product(bank[5][:, m:m + 1], [(AT[:, k, rows].bitcast(F32), onecol[:, :]) for k in range(NB)])
            last.then_inc(deg1_done, 1)
            hidden(1, 1)
            pe.wait_ge(comb_ready, 1)
            for g in range(2):
                for m in range(4 * g, 4 * g + 4):
                    last = nc.tensor.transpose(bank[6 + g][0:NE, (m % 4) * P:(m % 4 + 1) * P], comb[:, m, :], ident[:, :])
                last.then_inc(combT_done, 1)
            pe.wait_ge(combT_kept, 2)
            pe.wait_ge(deg1_kept, 1)
            pe.wait_ge(small_ld, 64)
            for m in range(NB):
                if m >= 2:
                    pe.wait_ge(moe_added, m - 1)
                mm(bank[4 + m % 2][:, :], combT[:, m * P:(m + 1) * P], b2all[:, :], True, True).then_inc(moe_done, 1)

            expert_out(0, 0)
            with pe.Fori(0, 3) as t:
                hidden(2 * t + 2, 0)
                expert_out(2 * t + 1, 1)
                hidden(2 * t + 3, 1)
                expert_out(2 * t + 2, 0)
            hidden(8, 0)
            expert_out(7, 1)
            expert_out(8, 0, last=True)
            turn(2, NB - 2)
            turn(2, NB - 1)
            pe.wait_ge(ln_lo[2], NB)
            pe.wait_ge(moe_added, (NE + 1) * NB)

            def xw(s, m, i):
                if m == 0:
                    pe.wait_ge(wchi_done, s + 1)
                    pe.wait_ge(wclo_done, s + 1)
                if isinstance(s, int) and s == 0:
                    if m >= 4:
                        pe.wait_ge(b_done, m - 3)
                else:
                    pe.wait_ge(xw_taken, NB * s + m - 3)
                product(bank[m % 4][:, :], x_times(wc_hi[i], wc_lo[i], m)).then_inc(xw_done, 1)

            def prop(s, m, i, cast, banks):
                pe.wait_ge(clo_done, NB * s)
                if m >= banks:
                    pe.wait_ge(b_done, NB * s + m - banks + 1)
                rows = slice(m * P, (m + 1) * P)
                t = [(cast(AT[:, k, rows]), cast(part[:, k, :])) for k in range(NB) for part in (c_hi[i], c_lo[i])]
                product(bank[4 + m % banks][:, :], t).then_inc(prop_done, 1)

            def cheb(cast):
                def step(s, i, final=False):
                    xw(s, 0, i)
                    xw(s, 1, i)
                    for m in range(NB):
                        prop(s, m, 1 - i, cast, 2 if final else 4)
                        if m + 2 < NB:
                            xw(s, m + 2, i)
                        if final and m >= 2:
                            turn(3, m - 2)

                with pe.Fori(0, 3) as t:
                    for j in range(2):
                        step(2 * t + 1 + j, 1 - j)
                step(KC - 1, 1, final=True)

            for m in range(NB):
                xw(0, m, 0)
            pe.wait_ge(big_ready, 1)
            big = pe.value_load(bigflag[0:1, 0:1], min_val=0, max_val=1)
            with pe.If(big > 0):
                cheb(lambda ap: ap.bitcast(F32))
            with pe.Else():
                cheb(lambda ap: ap)

            turn(3, NB - 2)
            turn(3, NB - 1)
            pe.wait_ge(wq_ready, KD)
            for m in range(NB):
                pe.wait_ge(xq_ready, KD * (m // 4 + 1))
                if m >= 4:
                    pe.wait_ge(out_ready, m - 3)
                rows = slice(m * P, (m + 1) * P)
                product(bank[m % 4][:, :], [(xq[:, k, rows], wq[:, k, :]) for k in range(KD)]).then_inc(fp8_done, 1)


def kernel(x, src, dst, L0_gnn_weight, L0_gnn_bias, L0_ffn_Wg, L0_ffn_bg, L0_ffn_W1, L0_ffn_b1,
           L0_ffn_W2, L0_ffn_b2, L0_ffn_Ws1, L0_ffn_bs1, L0_ffn_Ws2, L0_ffn_bs2,
           L1_gnn_weight, L1_gnn_bias, L1_ffn_weight):
    import numpy as np
    import concourse.bacc as bacc
    from concourse.bass_utils import run_bass_kernel_spmd

    rows = lambda a: np.asarray(a)
    arrays = {
        "x_in": rows(x),
        "src_in": rows(src).reshape(PAIRS, 2 * P),
        "dst_in": rows(dst).reshape(PAIRS, 2 * P),
        "w0_in": rows(L0_gnn_weight),
        "bias0_in": rows(L0_gnn_bias),
        "wg_in": rows(L0_ffn_Wg),
        "bg_in": rows(L0_ffn_bg),
        "w1_in": np.concatenate([rows(L0_ffn_W1), rows(L0_ffn_Ws1)[None]]),
        "b1_in": np.concatenate([rows(L0_ffn_b1), rows(L0_ffn_bs1)[None]]).reshape(NE * FB, P).T,
        "w2_in": np.concatenate([rows(L0_ffn_W2), rows(L0_ffn_Ws2)[None]]),
        "b2_in": np.concatenate([rows(L0_ffn_b2), rows(L0_ffn_bs2)[None]]),
        "wc_in": rows(L1_gnn_weight)[::-1],
        "bias1_in": rows(L1_gnn_bias),
        "wf_in": rows(L1_ffn_weight),
    }
    arrays = {n: np.ascontiguousarray(a) for n, a in arrays.items()}
    nc = bacc.Bacc("TRN2", target_bir_lowering=False, num_devices=1)
    aps = [nc.dram_tensor(n, a.shape, mybir.dt.from_np(a.dtype), kind="ExternalInput").ap() for n, a in arrays.items()]
    out = nc.dram_tensor("out", [N, D], F32, kind="ExternalOutput").ap()
    build(nc, *aps, out)
    r = run_bass_kernel_spmd(nc, [arrays], core_ids=[0])
    return r.results[0]["out"]
```

```python
from contextlib import ExitStack

import concourse.bass as bass
from concourse import mybir

F32 = mybir.dt.float32
F32R = mybir.dt.float32r
BF16 = mybir.dt.bfloat16
I32 = mybir.dt.int32
U32 = mybir.dt.uint32
ALU = mybir.AluOpType
ACT = mybir.ActivationFunctionType
AX_X = mybir.AxisListType.X
ABSMAX = bass.bass_isa.ReduceOp.absmax
MAX = bass.bass_isa.ReduceOp.max

P = 128
N = 1024
D = 512
NB = N // P
KD = D // P
E = 32768
PAIRS = E // (2 * P)
TILES = E // P
WD = 16
NW = N // WD
SH = P // WD
SL = N // SH
WG = 512 // SL
NG = NW // WG
TPW = TILES // NW
BEFORE = 3
VIS = TPW + 2 * BEFORE
CHUNK = TPW * WG
ACT_COLS = 6
ACT_FROM = 3
RING = 4
NE = 9
F = 256
FB = F // P
KC = 8
EPS = 1e-5
FP8_MAX = 448.0
EXACT = 4096
HALVES = N // 512
CK = 64 + NE

KB = 1024
ROWSUM, DEG0, DINV0, DEG1, DINV1, M2_DINV1, NEG_DINV1, DEG_POS = range(8)
MAGIC = 1.5 * 2.0 ** 20
GCN_BANKS = (0, 1, 4, 5)
BT_BANKS = (2, 3, 6, 7)


def build(nc, x_in, src_in, dst_in, w0_in, bias0_in, wg_in, bg_in, w1_in, b1_in, w2_in, b2_in,
          wc_in, bias1_in, wf_in, out):
    ctx = ExitStack()
    with ctx:
        base = (nc.sbuf_base + 31) // 32 * 32

        def at(name, shape, dt, offset):
            return nc.alloc_sbuf_tensor_at(name, shape, dt, offset=base + int(offset * KB))

        def sem(name):
            return ctx.enter_context(nc.semaphore(name))

        AT = at("AT", [P, NB, N], F32R, 0)
        xT_hi = at("xT_hi", [P, KD, N], F32R, 32)
        xT_lo = at("xT_lo", [P, KD, N], F32R, 48)
        x = at("x", [P, NB, D], F32, 64)
        U = 80
        xh = at("xh", [P, 2, D], F32, 200)
        ident = at("ident", [P, P], F32, 204)
        identb = at("identb", [P, P], BF16, 204.5)
        stats = at("stats", [P, NB, 6], F32, 204.75)
        meanvar = at("meanvar", [P, 4, NB, 2], F32, 205)
        veps = at("veps", [P, 4, NB], F32, 205.25)
        rstd = at("rstd", [P, 4, NB], F32, 205.375)
        shift = veps
        nhalf = at("nhalf", [P, NB], F32, 205.5)
        comb = at("comb", [P, NB, NE], F32, 205.5625)
        degs = at("degs", [P, 8, NB], F32, 205.875)
        b1T = at("b1T", [P, NE * FB], F32, 206.125)
        few = at("few", [P, 32], F32, 206.25)
        (mult_max, mult_max_all, w_amax, w_amax_all, w_scale, w_unscale, x_amax, x_amax_all) = \
            (few[:, c:c + 1] for c in range(8))
        block_maxs = few[:, 8:8 + NB]
        x_scale, x_unscale, out_scale = (few[:, c:c + 1] for c in (16, 17, 18))
        bigflag = at("bigflag", [1, 1], I32, 206.375)
        wg_hilo = at("wg_hilo", [P, KD, 16], F32R, 206.5)
        wg_raw = at("wg_raw", [P, KD, 8], F32, 206.75)
        bgb = at("bgb", [P, 8], F32, 206.875)
        onecol = at("onecol", [P, 2], F32R, 206.9375)
        b1cur = at("b1cur", [P, 2, FB], F32, 206.96875)
        iota8 = at("iota8", [P, 8], F32, 206.90625)

        S = at("S", [P, NB, N], F32R, U + 0)
        B = at("B", [P, NB, N], BF16, U + 32)
        y = at("y", [P, NB, D], F32, U + 48)
        y_hi = at("y_hi", [P, NB, D], F32R, U + 64)
        y_lo = at("y_lo", [P, NB, D], F32R, U + 80)
        w0_raw = at("w0_raw", [P, KD, D], F32, U + 96)
        w0_hi = at("w0_hi", [P, KD, D], F32R, U + 104)
        w0_lo = at("w0_lo", [P, KD, D], F32R, U + 112)
        src_i = at("src_i", [P, 2 * P], I32, U + 0)
        dst_i = at("dst_i", [P, 2 * P], I32, U + 1)
        shi_i = at("shi_i", [P, 2 * P], I32, U + 2)
        slo_i = at("slo_i", [P, 2 * P], I32, U + 3)
        joint = at("joint", [P, 2 * P], F32, U + 4)
        slo = at("slo", [P, 2 * P], F32, U + 5)
        stage = at("stage", [P, 4, WG, SL], F32, U + 6)
        rel = at("rel", [P, NW, VIS], BF16, U + 14)
        jT = at("jT", [P, BEFORE + TILES + VIS], F32, U + 15.5)
        sT = at("sT", [P, TILES], BF16, U + 16.75)
        jconst = at("jconst", [P, P, 2], BF16, U + 17.25)
        wbase = at("wbase", [P, NW], F32, U + 17.75)
        tilemm_i = at("tilemm_i", [P, 2, 2], I32, U + 18)
        tilemm = at("tilemm", [P, 2, 2], F32, U + 18.0625)
        tilewin = at("tilewin", [P, 2, 2], I32, U + 18.125)
        tileno = at("tileno", [P, 2, 2], F32, U + 18.1875)
        off = at("off", [P, 4], F32, U + 18.25)
        offall = at("offall", [1, 1], F32, U + 18.3125)
        neg_slo = at("neg_slo", [P, TILES], F32, U + 19)
        distance = at("distance", [P, ACT_COLS, SL], BF16, U + 30)
        unsorted = at("unsorted", [1, 1], I32, U + 18.375)
        bias0 = at("bias0", [P, D], F32, U + 28)
        oh_rows = [at(f"oh_rows{i}", [P, WG * VIS // 2, P, 2], BF16, U + 64 + 10 * i) for i in range(2)]
        oh_cols = [at(f"oh_cols{i}", [P, CHUNK // 2, SL, 2], BF16, U + (84, 88, 92, 20, 24)[i]) for i in range(5)]
        sF = at("sF", [P, TILES], F32, U + 76)
        oh_row = at("oh_row", [P, RING, 2, P], BF16, U + 64)
        oh_col = at("oh_col", [P, RING, 2, SL], BF16, U + 66)
        iotab = at("iotab", [P, P], BF16, U + 68)
        zerob = at("zerob", [P, P], BF16, U + 68.5)
        diag = at("diag", [P, 2, P], F32, U + 69)
        pairmm = at("pairmm", [P, 2], F32, U + 70)
        wstart = at("wstart", [NW, 2], F32, U + 70.0625)
        ones_w = at("ones_w", [P, NW], F32, U + 70.125)
        tri = at("tri", [NW, NW + 1], F32, U + 70.5)
        iotap = at("iotap", [NW, 2, PAIRS], F32, U + 71)
        wmask = at("wmask", [NW, 2, PAIRS], F32, U + 72)
        wsel = at("wsel", [NW, 2, PAIRS], F32, U + 73)
        wcol = at("wcol", [NW, 4], F32, U + 74)
        tabf = at("tabf", [1, NW + 1], F32, U + 74.25)
        tab = at("tab", [1, 2 * NW + 1], I32, U + 75)
        w_hi = [[at(f"w{k + 1}_hi{i}", [P, KD, F] if k == 0 else [P, FB, D], F32R, U + (32, 16)[i] + 4 * k)
                 for k in range(2)] for i in range(2)]
        w_lo = [[at(f"w{k + 1}_lo{i}", [P, KD, F] if k == 0 else [P, FB, D], F32R, U + (32, 16)[i] + 8 + 4 * k)
                 for k in range(2)] for i in range(2)]
        w_raw = [[at(f"w{k + 1}_raw{i}", [P, KD, F] if k == 0 else [P, FB, D], F32, U + 96 + 8 * i + 4 * k)
                  for k in range(2)] for i in range(2)]
        h_hi = [at(f"h_hi{i}", [P, FB, N], F32R, U + 48 + 16 * i) for i in range(2)]
        h_lo = [at(f"h_lo{i}", [P, FB, N], F32R, U + 56 + 16 * i) for i in range(2)]
        hrelu = at("hrelu", [P, 2, 512], F32, U + 80)
        combT = at("combT", [P, N], F32R, U + 84)
        b2_parts = at("b2_parts", [P, D], F32R, U + 88)
        gate = at("gate", [P, NB, 8], F32, U + 90)
        top8 = at("top8", [P, NB, 8], F32, U + 90.25)
        top8i = at("top8i", [P, NB, 8], U32, U + 90.5)
        topi = at("topi", [P, NB, 2], F32, U + 90.75)
        sel1 = at("sel1", [P, NB, 8], F32, U + 91)
        sel2 = at("sel2", [P, NB, 8], F32, U + 91.25)
        pair = at("pair", [P, 5, NB], F32, U + 91.5)
        comb2 = at("comb2", [P, NB, NE], F32, U + 91.6875)
        gate_rows = at("gate_rows", [16, N], F32, U + 92)
        comb_parts = at("comb_parts", [P, NB, CK], F32R, U + 0)
        b2_raw = at("b2_raw", [P, D], F32, U + 4)
        wc_hi = [at(f"wc_hi{i}", [P, KD, D], F32R, U + (0, 96)[i]) for i in range(2)]
        wc_lo = [at(f"wc_lo{i}", [P, KD, D], F32R, U + (8, 104)[i]) for i in range(2)]
        wc_raw = at("wc_raw", [P, KD, D], F32, U + 112)
        b = [at(f"b{i}", [P, NB, D], F32, U + 32 - 16 * i) for i in range(2)]
        c_hi = [at("c_hi0", [P, NB, D], F32R, U + 48), at("c_hi1", [P, NB, D], F32R, 64)]
        c_lo = [at("c_lo0", [P, NB, D], F32R, U + 64), at("c_lo1", [P, NB, D], F32R, U + 80)]
        xr = at("xr", [P, NB, D], F32, 64)
        bias1 = at("bias1", [P, D], F32, U + 80)
        deg_row = at("deg_row", [1, N], F32, U + 92)
        xhT = at("xhT", [P, KD, N], F32, U + 32)
        xq = at("xq", [P, KD, N], BF16, U + 84)
        wq = at("wq", [P, KD, D], BF16, U + 0)
        qtmp_w = [[at(f"qtmp_w{c}{n}", [P, 1, D], F32, U + 4 + 6 * c + 2 * n) for n in range(3)] for c in range(2)]
        qtmp_x = [[at(f"qtmp_x{c}{n}", [P, KD, 2 * P], F32, U + (4, 48)[c] + 4 * n) for n in range(3)] for c in range(2)]
        scaled_out = at("scaled_out", [P, 4, D], F32, U + 60)

        bank = [ctx.enter_context(nc.psum_tensor(f"bank{i}", [P, 512], F32)) for i in range(8)]

        x_spill = nc.dram_tensor("x_spill", [P, NB, D], F32, kind="Internal").ap()

        edges_in = sem("edges_in")
        x_ld = [sem(f"x_ld{m}") for m in range(NB)]
        w0_ld = sem("w0_ld")
        small_ld = sem("small_ld")
        bias0_ld = sem("bias0_ld")
        consts = sem("consts")
        w0_split = sem("w0_split")
        wg_split = sem("wg_split")
        wg_hi_done = sem("wg_hi_done")
        idx_rows = sem("idx_rows")
        idx_turned = sem("idx_turned")
        idx_kept = sem("idx_kept")
        off_ready = sem("off_ready")
        off_row = sem("off_row")
        path_ready = sem("path_ready")
        slow_consts = sem("slow_consts")
        diag_ready = sem("diag_ready")
        pair_rows = sem("pair_rows")
        wcol_ready = sem("wcol_ready")
        tab_rows = sem("tab_rows")
        tab_ready = sem("tab_ready")
        rel_ready = sem("rel_ready")
        oh_ready = sem("oh_ready")
        distances = sem("distances")
        act_cols = sem("act_cols")
        oh_used = sem("oh_used")
        win_done = sem("win_done")
        win_staged = sem("win_staged")
        win_placed = [sem(f"win_placed{i}") for i in range(4)]
        b_ready = sem("b_ready")
        bt_done = sem("bt_done")
        s_rows = sem("s_rows")
        s_ready = sem("s_ready")
        y_done = sem("y_done")
        y_kept = sem("y_kept")
        dinv0_ready = sem("dinv0_ready")
        y_hi_ready = sem("y_hi_ready")
        y_lo_ready = sem("y_lo_ready")
        xb_ready = sem("xb_ready")
        gcn_done = sem("gcn_done")
        gcn_kept = sem("gcn_kept")
        ln_var = [sem(f"ln_var{i}") for i in range(4)]
        ln_rstd = [sem(f"ln_rstd{i}") for i in range(4)]
        ln_norm = [sem(f"ln_norm{i}") for i in range(4)]
        ln_turned = [sem(f"ln_turned{i}") for i in range(4)]
        ln_hi = [sem(f"ln_hi{i}") for i in range(4)]
        ln_lo = [sem(f"ln_lo{i}") for i in range(4)]
        gate_done = sem("gate_done")
        gate_kept = sem("gate_kept")
        gate_turned = sem("gate_turned")
        small_zero = sem("small_zero")
        comb_parts_ready = sem("comb_parts_ready")
        b2_ld = sem("b2_ld")
        b2_hi_done = sem("b2_hi_done")
        b2_ready = sem("b2_ready")
        deg_rows = sem("deg_rows")
        deg_rows_kept = sem("deg_rows_kept")
        topdiff = sem("topdiff")
        topexp = sem("topexp")
        comb_ready = sem("comb_ready")
        comb2_ready = sem("comb2_ready")
        combT_done = sem("combT_done")
        combT_kept = sem("combT_kept")
        raw_ld = [[sem(f"w{k + 1}_raw_ld{i}") for i in range(2)] for k in range(2)]
        whi_done = [sem(f"w{k + 1}_hi_done") for k in range(2)]
        wlo_done = [sem(f"w{k + 1}_lo_done") for k in range(2)]
        h_done = sem("h_done")
        relu_done = sem("relu_done")
        b1_kept = sem("b1_kept")
        hhi_done = sem("hhi_done")
        hlo_done = sem("hlo_done")
        moe_done = sem("moe_done")
        moe_added = sem("moe_added")
        spilled = sem("spilled")
        degmax_ready = sem("degmax_ready")
        big_all = sem("big_all")
        big_ready = sem("big_ready")
        deg1_done = sem("deg1_done")
        deg1_kept = sem("deg1_kept")
        deg1_pow = sem("deg1_pow")
        dinv1_ready = sem("dinv1_ready")
        b_zero = sem("b_zero")
        wc_ld = sem("wc_ld")
        wchi_done = sem("wchi_done")
        wclo_done = sem("wclo_done")
        xw_done = sem("xw_done")
        xw_taken = sem("xw_taken")
        prop_done = sem("prop_done")
        b_done = sem("b_done")
        chi_done = sem("chi_done")
        clo_done = sem("clo_done")
        x_back = sem("x_back")
        bias1_ld = sem("bias1_ld")
        xr_ready = sem("xr_ready")
        x_added = sem("x_added")
        wamax = sem("wamax")
        wamax_all = sem("wamax_all")
        wq_ready = sem("wq_ready")
        block_amax = sem("block_amax")
        xamax = sem("xamax")
        xamax_all = sem("xamax_all")
        xT_kept = sem("xT_kept")
        wscale_ready = sem("wscale_ready")
        w_scaled = sem("w_scaled")
        xscale_ready = sem("xscale_ready")
        x_scaled = sem("x_scaled")
        round_step = sem("round_step")
        xq_ready = sem("xq_ready")
        fp8_done = sem("fp8_done")
        fp8_scaled = sem("fp8_scaled")
        out_ready_pool = sem("out_ready_pool")
        out_ready = sem("out_ready")
        stored = sem("stored")
        pool_step = sem("pool_step")
        dve_step = [sem(f"dve_step{i}") for i in range(4)]
        slow_step = sem("slow_step")

        block = ctx.enter_context(nc.Block())

        @block.sync
        def _(sp):
            sp.dma_start(dst_i[:, :], dst_in).then_inc(edges_in, 16)
            sp.dma_start(src_i[:, :], src_in).then_inc(edges_in, 16)
            for m in range(NB):
                sp.dma_start(x[:, m, :], x_in[m * P:(m + 1) * P, :]).then_inc(x_ld[m], 16)
            sp.dma_start(w0_raw[:, :, :], w0_in.rearrange("(k p) n -> p k n", p=P)).then_inc(w0_ld, 16)
            sp.dma_start(bias0[:, :], bias0_in.partition_broadcast(P)).then_inc(bias0_ld, 16)
            sp.dma_start(wg_raw[:, :, :], wg_in.rearrange("(k p) n -> p k n", p=P)).then_inc(small_ld, 16)
            sp.dma_start(bgb[:, :], bg_in.partition_broadcast(P)).then_inc(small_ld, 16)
            sp.dma_start(b1T[:, :], b1_in).then_inc(small_ld, 16)

            for g in range(NG):
                sp.wait_ge(win_staged, g + 1)
                for q in range(WG):
                    row = (g * WG + q) * WD
                    sp.dma_start(AT[row % P:row % P + WD, row // P, :].bitcast(F32).rearrange("p (a n) -> p a n", a=SH),
                                 stage[:, g % 4, q, :]).then_inc(win_placed[g % 4], 16)

            def load_expert(k, e, i):
                w = (w1_in, w2_in)[k]
                src = w[e] if isinstance(e, int) else w[bass.ds(e, 1), :, :].rearrange("e a b -> (e a) b")
                sp.dma_start(w_raw[i][k][:, :, :], src.rearrange("(k p) n -> p k n", p=P)).then_inc(raw_ld[k][i], 16)

            sp.wait_ge(y_done, NB)
            for e in range(2):
                for k in range(2):
                    load_expert(k, e, e)
            def refill(e, i):
                for k in range(2):
                    sp.wait_ge(whi_done[k], e + 1)
                    sp.wait_ge(wlo_done[k], e + 1)
                    load_expert(k, e + 2, i)

            refill(0, 0)
            sp.wait_ge(small_zero, 2)
            for r in range(3):
                sp.dma_start(b2_raw[32 * r:32 * r + NE, :], b2_in).then_inc(b2_ld, 16)
            with sp.Fori(0, 3) as t:
                refill(2 * t + 1, 1)
                refill(2 * t + 2, 0)

            sp.dma_start(wc_raw[:, :, :], wc_in[0].rearrange("(k p) n -> p k n", p=P)).then_inc(wc_ld, 16)
            def load_cheb(s):
                sp.wait_ge(wchi_done, s)
                sp.wait_ge(wclo_done, s)
                src = wc_in[s] if isinstance(s, int) else wc_in[bass.ds(s, 1), :, :].rearrange("e a b -> (e a) b")
                sp.dma_start(wc_raw[:, :, :], src.rearrange("(k p) n -> p k n", p=P)).then_inc(wc_ld, 16)

            load_cheb(1)
            for m in range(NB):
                sp.wait_ge(moe_added, (NE - 1) * NB + m + 1)
                sp.dma_start(x_spill[:, m, :], x[:, m, :]).then_inc(spilled, 16)

            with sp.Fori(2, KC) as s:
                load_cheb(s)
            sp.wait_ge(wchi_done, KC)
            sp.wait_ge(wclo_done, KC)
            sp.dma_start(wc_raw[:, :, :], wf_in.rearrange("(k p) n -> p k n", p=P)).then_inc(wc_ld, 16)
            sp.wait_ge(spilled, 16 * NB)
            sp.wait_ge(prop_done, (KC - 2) * NB)
            sp.dma_start(xr[:, :, :], x_spill).then_inc(x_back, 16)
            sp.dma_start(bias1[:, :], bias1_in.partition_broadcast(P)).then_inc(bias1_ld, 16)
            for m in range(NB):
                if m < 4:
                    sp.wait_ge(out_ready_pool, m + 1)
                else:
                    sp.wait_ge(out_ready, m - 3)
                sp.dma_start(out[m * P:(m + 1) * P, :], b[1][:, m, :]).then_inc(stored, 16)
            sp.wait_ge(stored, 16 * NB)

        @block.gpsimd
        def _(pool):
            steps = [0]

            def link(ins):
                steps[0] += 1
                ins.then_inc(pool_step, 1)
                pool.wait_ge(pool_step, steps[0])

            def iota(out_ap, pattern, base, channel, done):
                nc.gpsimd.iota(out_ap, pattern, base=base, channel_multiplier=channel,
                               allow_small_or_imprecise_dtypes=True).then_inc(done, 1)

            iota(tileno[:, :, :], [[0, 2], [1, 2]], 0, 2, consts)
            link(nc.gpsimd.memset(ident[:, :], 0.0))
            nc.gpsimd.affine_select(out=ident[:, :], in_=ident[:, :], compare_op=ALU.not_equal, fill=1.0, base=0,
                                    pattern=[[-1, P]], channel_multiplier=1).then_inc(consts, 1)
            iota(jconst[:, :, :], [[1, P], [0, 2]], 0, 0, consts)
            iota(wbase[:, :], [[P, NW]], 0, 0, consts)
            nc.gpsimd.memset(jT[:, 0:BEFORE], -1.0).then_inc(consts, 1)
            nc.gpsimd.memset(jT[:, BEFORE + TILES:], -1.0).then_inc(consts, 1)
            nc.gpsimd.memset(nhalf[:, :], -0.5).then_inc(consts, 1)
            iota(iota8[:, :], [[1, 8]], 0, 0, consts)
            nc.gpsimd.memset(comb[:, :, NE - 1], 0.5).then_inc(consts, 1)
            nc.gpsimd.memset(onecol[:, :].bitcast(F32), 1.0).then_inc(consts, 1)
            pool.wait_ge(consts, 10)
            nc.gpsimd.tensor_copy(identb[:, :], ident[:, :]).then_inc(consts, 1)

            pool.wait_ge(path_ready, 1)
            other = pool.value_load(unsorted[0:1, 0:1], min_val=0, max_val=1)
            with pool.If(other > 0):
                pool.sem_inc(oh_used, RING)
                iota(iotab[:, :], [[1, P]], 0, 0, slow_consts)
                nc.gpsimd.memset(zerob[:, :], 0.0).then_inc(slow_consts, 1)
                iota(wstart[:, 0:1], [[0, 1]], 0, WD, slow_consts)
                iota(wstart[:, 1:2], [[0, 1]], WD, WD, slow_consts)
                nc.gpsimd.memset(ones_w[:, :], 1.0).then_inc(slow_consts, 1)
                iota(iotap[:, 0, :], [[1, PAIRS]], PAIRS, 0, slow_consts)
                iota(iotap[:, 1, :], [[1, PAIRS]], 1, 0, slow_consts)
                nc.gpsimd.memset(tri[:, :], 1.0).then_inc(slow_step, 1)
                pool.wait_ge(slow_step, 1)
                nc.gpsimd.affine_select(out=tri[:, :], in_=tri[:, :], compare_op=ALU.is_ge, fill=0.0, base=-1,
                                        pattern=[[1, NW + 1]], channel_multiplier=-1).then_inc(slow_consts, 1)

            def ln_rows(i, m):
                pool.wait_ge(ln_var[i], m + 1)
                link(nc.gpsimd.tensor_scalar(veps[:, i, m:m + 1], meanvar[:, i, m, 1:2], EPS, None, ALU.add))
                link(nc.gpsimd.tensor_tensor(rstd[:, i, m:m + 1], veps[:, i, m:m + 1], nhalf[:, 0:1], ALU.pow))
                nc.gpsimd.tensor_scalar(shift[:, i, m:m + 1], meanvar[:, i, m, 0:1], rstd[:, i, m:m + 1], -1.0,
                                        ALU.mult, ALU.mult).then_inc(ln_rstd[i], 1)

            def split_lo(out_lo, raw, hi, done):
                nc.gpsimd.tensor_tensor(out_lo, raw, hi.bitcast(F32), ALU.subtract).then_inc(done, 1)

            pool.wait_ge(wg_hi_done, 1)
            split_lo(wg_hilo[:, :, 8:16], wg_raw[:, :, :], wg_hilo[:, :, 0:8], wg_split)
            ln_rows(0, 0)
            pool.wait_ge(w0_split, 1)
            split_lo(w0_lo[:, :, :], w0_raw[:, :, :], w0_hi[:, :, :], w0_split)
            def x_biased(m):
                pool.wait_ge(ln_norm[0], m + 1)
                nc.gpsimd.tensor_tensor(x[:, m, :], x[:, m, :], bias0[:, :], ALU.add).then_inc(xb_ready, 1)

            def binary(m):
                for g in (2 * m, 2 * m + 1):
                    pool.wait_ge(win_placed[g % 4], 16 * WG * (g // 4 + 1))
                nc.gpsimd.tensor_scalar(B[:, m, :], AT[:, m, :].bitcast(F32), 1.0, None, ALU.min).then_inc(b_ready, 1)

            pool.wait_ge(bias0_ld, 16)
            for m in range(1, NB):
                ln_rows(0, m)
                x_biased(m - 1)
                binary(m - 1)
            x_biased(NB - 1)
            for m in range(NB):
                pool.wait_ge(s_rows, m + 1)
                d = S[:, m, m * P:(m + 1) * P]
                link(nc.gpsimd.tensor_scalar(degs[:, DEG0, m:m + 1], degs[:, ROWSUM, m:m + 1], 1.0, None, ALU.add))
                nc.gpsimd.tensor_tensor(degs[:, DINV0, m:m + 1], degs[:, DEG0, m:m + 1], nhalf[:, 0:1], ALU.pow).then_inc(dinv0_ready, 1)
                nc.gpsimd.tensor_tensor(d, d.bitcast(F32), ident[:, :], ALU.add).then_inc(s_ready, 1)

            def expert_lo(k, e, i):
                pool.wait_ge(whi_done[k], e + 1)
                split_lo(w_lo[i][k][:, :, :], w_raw[i][k][:, :, :], w_hi[i][k][:, :, :], wlo_done[k])

            for k in range(2):
                expert_lo(k, 0, 0)
            for m in range(NB):
                ln_rows(1, m)
            def hidden_lo(n, i, j):
                pool.wait_ge(hhi_done, n + 1)
                f, half = j % FB, j // FB
                cols = slice(half * 512, half * 512 + 512)
                split_lo(h_lo[i][:, f, cols], hrelu[:, j % 2, :], h_hi[i][:, f, cols], hlo_done)

            expert_lo(0, 1, 1)
            for j in range(4):
                if j == 2:
                    expert_lo(1, 1, 1)
                hidden_lo(j, 0, j)
            nc.gpsimd.memset(b2_raw[:, :], 0.0).then_inc(small_zero, 1)
            nc.gpsimd.memset(comb_parts[:, :, :].bitcast(F32), 0.0).then_inc(small_zero, 1)

            def moe_step(e, i, hidden=True, refill=True):
                if hidden:
                    for j in range(4):
                        hidden_lo(4 * (e + 1) + j, 1 - i, j)
                if refill:
                    expert_lo(0, e + 2, i)
                    expert_lo(1, e + 2, i)

            moe_step(0, 0)
            pool.wait_ge(comb2_ready, 1)
            pool.wait_ge(comb_parts_ready, 2)
            nc.gpsimd.tensor_tensor(comb_parts[:, :, 64:64 + NE], comb2[:, :, :], comb_parts[:, :, 0:NE].bitcast(F32),
                                    ALU.subtract).then_inc(comb_parts_ready, 1)
            pool.wait_ge(b2_hi_done, 1)
            pool.wait_ge(comb_parts_ready, 3)
            nc.gpsimd.tensor_tensor(b2_parts[32:32 + NE, :], b2_raw[32:32 + NE, :], b2_parts[32:32 + NE, :].bitcast(F32),
                                    ALU.subtract).then_inc(b2_ready, 1)
            pool.wait_ge(b2_ready, 1)
            with pool.Fori(0, 3) as t:
                moe_step(2 * t + 1, 1)
                moe_step(2 * t + 2, 0)
            moe_step(7, 1, refill=False)
            pool.wait_ge(degmax_ready, 1)
            nc.gpsimd.partition_all_reduce(mult_max_all, mult_max, P, MAX).then_inc(big_all, 1)

            def cheb_lo(s, i):
                pool.wait_ge(wchi_done, s + 1)
                split_lo(wc_lo[i][:, :, :], wc_raw[:, :, :], wc_hi[i][:, :, :], wclo_done)

            cheb_lo(0, 0)
            for m in range(NB):
                ln_rows(2, m)
            nc.gpsimd.memset(b[1][:, :, :], 0.0).then_inc(b_zero, 1)
            pool.wait_ge(deg1_kept, 1)
            nc.gpsimd.tensor_tensor(degs[:, DINV1, :], degs[:, DEG1, :], nhalf[:, :], ALU.pow).then_inc(deg1_pow, 1)
            cheb_lo(1, 1)
            with pool.Fori(0, 3) as t:
                for i in range(2):
                    cheb_lo(2 * t + i + 2, i)
            pool.wait_ge(x_back, 16)
            pool.wait_ge(bias1_ld, 16)

            def xr_biased(m):
                nc.gpsimd.tensor_tensor(xr[:, m, :], xr[:, m, :], bias1[:, :], ALU.add).then_inc(xr_ready, 1)

            for m in range(3):
                xr_biased(m)
            pool.wait_ge(wamax, 1)
            nc.gpsimd.partition_all_reduce(w_amax_all, w_amax, P, ABSMAX).then_inc(wamax_all, 1)
            for m in range(NB):
                if m + 3 < NB:
                    xr_biased(m + 3)
                ln_rows(3, m)
            pool.wait_ge(xamax, 1)
            nc.gpsimd.partition_all_reduce(x_amax_all, x_amax, P, ABSMAX).then_inc(xamax_all, 1)
            for m in range(4):
                pool.wait_ge(fp8_scaled, m + 1)
                nc.gpsimd.tensor_tensor(b[1][:, m, :], b[1][:, m, :], scaled_out[:, m, :], ALU.add).then_inc(out_ready_pool, 1)

        @block.scalar
        def _(act):
            def copy(out_ap, in_ap, done, scale=1.0):
                nc.scalar.activation(out_ap, in_ap, ACT.Copy, scale=scale).then_inc(done, 1)

            def normalise(i, m, rows):
                act.wait_ge(ln_rstd[i], m + 1)
                if m >= 2:
                    act.wait_ge(ln_turned[i], m - 1)
                    if i == 3:
                        act.wait_ge(block_amax, m - 1)
                nc.scalar.activation(xh[:, m % 2, :], rows, ACT.Identity, bias=shift[:, i, m:m + 1],
                                     scale=rstd[:, i, m:m + 1]).then_inc(ln_norm[i], 1)

            def turn_hi(i, m):
                act.wait_ge(ln_turned[i], m + 1)
                copy(xT_hi[:, :, m * P:(m + 1) * P],
                     bank[6 + m % 2][:, :].rearrange("p (k n) -> p k n", k=KD), ln_hi[i])

            def near(c):
                if c >= 5:
                    act.wait_ge(win_done, c - 3)
                for n in range(ACT_COLS):
                    tile = (c + 1) * CHUNK - ACT_COLS + n
                    last = nc.scalar.activation(distance[:, n, :], jconst[:, 0:SL, 0], ACT.Abs, bias=neg_slo[:, tile:tile + 1])
                last.then_inc(distances, 1)

            def one_hot(c):
                act.wait_ge(distances, c - ACT_FROM + 1)
                nc.scalar.activation(oh_cols[c % 5][:, (CHUNK - ACT_COLS) // 2:, :, :].rearrange("p t n h -> p t h n"),
                                     distance[:, :, :].rearrange("p (t h) n -> p t h n", h=2), ACT.Relu, bias=1.0, scale=-1.0)\
                    .then_inc(act_cols, 1)

            act.wait_ge(consts, 11)
            act.wait_ge(idx_kept, 3)
            act.wait_ge(small_ld, 48)
            copy(wg_hilo[:, :, 0:8], wg_raw[:, :, :], wg_hi_done)
            act.wait_ge(w0_ld, 16)
            copy(w0_hi[:, :, :], w0_raw[:, :, :], w0_split)
            def staged(g):
                act.wait_ge(win_done, g + 1)
                if g >= 4:
                    act.wait_ge(win_placed[g % 4], 16 * WG * (g // 4))
                copy(stage[:, g % 4, :, :], bank[g % 4][:, :].rearrange("p (q n) -> p q n", q=WG), win_staged)

            def next_cols(g):
                if g + 3 < NG:
                    if g:
                        act.wait_ge(act_cols, g + 3 - ACT_FROM)
                    near(g + 3)
                    one_hot(g + 3)

            for kt in range(NB):
                normalise(0, kt, x[:, kt, :])
                staged(2 * kt)
                next_cols(2 * kt)
                staged(2 * kt + 1)
                turn_hi(0, kt)
                next_cols(2 * kt + 1)
                if kt:
                    act.wait_ge(y_done, kt)
                    copy(y[:, kt - 1, :], bank[4 + (kt - 1) % 2][:, :], y_kept)
            act.wait_ge(y_done, NB)
            copy(y[:, NB - 1, :], bank[4 + (NB - 1) % 2][:, :], y_kept)
            act.wait_ge(y_kept, NB)
            for m in range(NB):
                act.wait_ge(dinv0_ready, m + 1)
                copy(y_hi[:, m, :], y[:, m, :], y_hi_ready, scale=degs[:, DINV0, m:m + 1])

            def expert_hi(k, e, i, e_half):
                act.wait_ge(raw_ld[k][i], 16 * (e_half + 1))
                copy(w_hi[i][k][:, :, :], w_raw[i][k][:, :, :], whi_done[k])

            for k in range(2):
                expert_hi(k, 0, 0, 0)
            for m in range(NB + 1):
                if m < NB:
                    normalise(1, m, x[:, m, :])
                if m:
                    turn_hi(1, m - 1)

            def hidden(e, i, j):
                n = 4 * e + j
                act.wait_ge(h_done, n + 1)
                if not (isinstance(n, int) and n < 2):
                    act.wait_ge(hlo_done, n - 1)
                f = j % FB
                nc.scalar.activation(hrelu[:, j % 2, :], bank[j][:, :], ACT.Relu, bias=b1cur[:, i, f:f + 1]).then_inc(relu_done, 1)

            def hidden_bias(e, i):
                copy(b1cur[:, i, :], b1T[:, bass.ds(e * FB, FB)], b1_kept)
                act.wait_ge(b1_kept, e + 1)

            hidden_bias(0, 0)
            def gate_copy(half):
                act.wait_ge(gate_done, half + 1)
                copy(gate_rows[:, half * 512:half * 512 + 512], bank[2 + half][0:16, :], gate_kept)

            expert_hi(0, 1, 1, 0)
            gate_copy(0)
            hidden(0, 0, 0)
            hidden(0, 0, 1)
            gate_copy(1)
            expert_hi(1, 1, 1, 0)
            hidden(0, 0, 2)
            hidden(0, 0, 3)
            act.wait_ge(topdiff, 1)
            nc.scalar.activation(pair[:, 1, :], pair[:, 0, :], ACT.Exp).then_inc(topexp, 1)

            def moe_step(e, i, t, nxt=True, refill=True):
                if nxt:
                    hidden_bias(e + 1, 1 - i)
                    for j in range(4):
                        hidden(e + 1, 1 - i, j)
                    if isinstance(e, int) and e == 0:
                        act.wait_ge(comb_ready, 1)
                        act.wait_ge(small_zero, 2)
                        copy(comb_parts[:, :, 0:NE], comb[:, :, :], comb_parts_ready, scale=2.0)
                        copy(comb_parts[:, :, 32:32 + NE], comb[:, :, :], comb_parts_ready, scale=2.0)
                if refill:
                    act.wait_ge(h_done, 4 * (e + 1))
                    expert_hi(0, e + 2, i, t + 1)
                    act.wait_ge(moe_done, NB * (e + 1))
                    expert_hi(1, e + 2, i, t + 1)

            moe_step(0, 0, 0)
            act.wait_ge(b2_ld, 48)
            copy(b2_parts[0:CK, :], b2_raw[0:CK, :], b2_hi_done)
            with act.Fori(0, 3) as t:
                moe_step(2 * t + 1, 1, t)
                moe_step(2 * t + 2, 0, t + 1)
            for g in range(2):
                act.wait_ge(combT_done, g + 1)
                copy(combT[0:CK, g * 512:(g + 1) * 512], bank[6 + g][0:CK, :], combT_kept)
            moe_step(7, 1, 3, refill=False)

            def cheb_hi(s, i):
                act.wait_ge(wc_ld, 16 * (s + 1))
                if not isinstance(s, int) or s >= 2:
                    act.wait_ge(xw_done, NB * (s - 1))
                copy(wc_hi[i][:, :, :], wc_raw[:, :, :], wchi_done)

            cheb_hi(0, 0)
            for m in range(NB + 1):
                if m < NB:
                    normalise(2, m, x[:, m, :])
                if m == NB - 1:
                    for half in range(HALVES):
                        act.wait_ge(deg_rows, half + 1)
                        copy(deg_row[:, half * 512:half * 512 + 512], bank[2 + half][0:1, :], deg_rows_kept)
                if m:
                    turn_hi(2, m - 1)
                if m == NB - 2:
                    cheb_hi(1, 1)

            def scaled_hi(s, m, i):
                act.wait_ge(b_done, NB * s + m + 1)
                copy(c_hi[i][:, m, :], b[i][:, m, :], chi_done, scale=degs[:, DINV1, m:m + 1])

            act.wait_ge(dinv1_ready, 1)
            act.wait_ge(spilled, 16 * NB)
            for m in range(NB):
                scaled_hi(0, m, 0)
            with act.Fori(0, 3) as t:
                for j in range(2):
                    s = 2 * t + 1 + j
                    for m in range(NB):
                        scaled_hi(s, m, 1 - j)
                        if m == 0:
                            cheb_hi(s + 1, j)
            for m in range(NB + 1):
                if m < NB:
                    act.wait_ge(b_done, NB * (KC - 1) + m + 1)
                    normalise(3, m, b[1][:, m, :])
                if m:
                    act.wait_ge(ln_turned[3], m)
                    copy(xhT[:, :, (m - 1) * P:m * P],
                         bank[6 + (m - 1) % 2][:, :].rearrange("p (k n) -> p k n", k=KD), xT_kept)
                if m == 0:
                    act.wait_ge(wscale_ready, 1)
                    for k in range(KD):
                        copy(wc_raw[:, k, :], wc_raw[:, k, :], w_scaled, scale=w_scale)
            act.wait_ge(xscale_ready, 1)
            act.wait_ge(xT_kept, NB)
            for c in range(4):
                part = xhT[:, :, c * 2 * P:(c + 1) * 2 * P]
                copy(part, part, x_scaled, scale=x_scale)
            act.wait_ge(xscale_ready, 2)
            for m in range(4):
                act.wait_ge(fp8_done, m + 1)
                copy(scaled_out[:, m, :], bank[m][:, :], fp8_scaled, scale=out_scale)

        @block.vector
        def _(dve):
            chain = [0, 0]

            def new_chain():
                chain[:] = [chain[0] + 1, 0]

            def link(ins):
                chain[1] += 1
                ins.then_inc(dve_step[chain[0]], 1)
                dve.wait_ge(dve_step[chain[0]], chain[1])

            def ln_stats(i, m, rows):
                link(nc.vector.bn_stats(stats[:, m, :], rows))
                nc.vector.bn_aggr(meanvar[:, i, m, :], stats[:, m, :]).then_inc(ln_var[i], 1)

            def turn_lo(i, m):
                dve.wait_ge(ln_hi[i], m + 1)
                cols = slice(m * P, (m + 1) * P)
                nc.vector.tensor_tensor(xT_lo[:, :, cols], bank[6 + m % 2][:, :].rearrange("p (k n) -> p k n", k=KD),
                                        xT_hi[:, :, cols].bitcast(F32), ALU.subtract).then_inc(ln_lo[i], 1)

            dve.wait_ge(edges_in, 32)
            halves = dst_i[:, :].rearrange("p (h n) -> p h n", h=2)
            nc.vector.tensor_reduce(tilemm_i[:, 0, :], halves, AX_X, ALU.min)
            nc.vector.tensor_scalar(shi_i[:, :], src_i[:, :], SL.bit_length() - 1, None, ALU.logical_shift_right)
            nc.vector.tensor_scalar(slo_i[:, :], src_i[:, :], SL - 1, None, ALU.bitwise_and)
            link(nc.vector.tensor_reduce(tilemm_i[:, 1, :], halves, AX_X, ALU.max))
            nc.vector.scalar_tensor_tensor(joint[:, :], dst_i[:, :], float(SH), shi_i[:, :], ALU.mult, ALU.add).then_inc(idx_rows, 1)
            nc.vector.tensor_copy(slo[:, :], slo_i[:, :]).then_inc(idx_rows, 1)
            link(nc.vector.tensor_scalar(tilewin[:, :, :], tilemm_i[:, :, :], N - WD, None, ALU.bitwise_and))
            dve.wait_ge(consts, 11)
            link(nc.vector.scalar_tensor_tensor(tilemm[:, :, :], tilewin[:, :, :], float(TPW) / WD, tileno[:, :, :],
                                                ALU.mult, ALU.subtract))
            nc.vector.tensor_reduce(off[:, 0:1], tilemm[:, 1, :], AX_X, ALU.max)
            link(nc.vector.tensor_reduce(off[:, 1:2], tilemm[:, 0, :], AX_X, ALU.min))
            nc.vector.tensor_scalar(off[:, 2:3], off[:, 0:1], float(BEFORE), None, ALU.subtract)
            link(nc.vector.tensor_scalar(off[:, 3:4], off[:, 1:2], -1.0, -float(VIS - 1 - BEFORE), ALU.mult, ALU.add))
            nc.vector.tensor_tensor(off[:, 0:1], off[:, 2:3], off[:, 3:4], ALU.max).then_inc(off_ready, 1)
            dve.wait_ge(idx_turned, 1)
            turned = bank[2][:, :].rearrange("p (c h t) -> p c t h", c=2, h=2)
            nc.vector.tensor_copy(jT[:, BEFORE:BEFORE + TILES].rearrange("p (t h) -> p t h", h=2), turned[:, 0, :, :]).then_inc(idx_kept, 1)
            nc.vector.tensor_copy(sT[:, :].rearrange("p (t h) -> p t h", h=2), turned[:, 1, :, :]).then_inc(idx_kept, 1)
            nc.vector.tensor_scalar(neg_slo[:, :].rearrange("p (t h) -> p t h", h=2), turned[:, 1, :, :], -1.0, None, ALU.mult).then_inc(idx_kept, 1)
            dve.wait_ge(off_row, 1)
            link(nc.vector.tensor_reduce(offall[:, :], bank[3][0:1, 0:P], AX_X, ALU.max))
            nc.vector.tensor_scalar(unsorted[:, :], offall[:, :], 0.0, None, ALU.is_gt).then_inc(path_ready, 1)
            dve.wait_ge(idx_kept, 3)

            def cols_of(c):
                own = CHUNK - (ACT_COLS if c >= ACT_FROM else 0)
                shape = [P, own // 2, SL, 2]
                idx = sT[:, c * CHUNK:c * CHUNK + own].rearrange("p (t o h) -> p t o h", o=1, h=2).broadcast_to(shape)
                j = jconst[:, 0:SL, :].rearrange("p (o n) h -> p o n h", o=1).broadcast_to(shape)
                return nc.vector.tensor_tensor(oh_cols[c % 5][:, 0:own // 2, :, :], idx, j, ALU.is_equal)

            def rows_of(g):
                shape = [P, WG * VIS // 2, P, 2]
                idx = rel[:, g * WG:(g + 1) * WG, :].rearrange("p w (t o h) -> p (w t) o h", o=1, h=2).broadcast_to(shape)
                j = jconst[:, :, :].rearrange("p (o n) h -> p o n h", o=1).broadcast_to(shape)
                return nc.vector.tensor_tensor(oh_rows[g % 2][:, :, :, :], idx, j, ALU.is_equal)

            for a in range(0, VIS, TPW):
                n = min(TPW, VIS - a)
                tiles = jT[:, a:a + TILES].rearrange("p (w f) -> p w f", f=TPW)[:, :, 0:n]
                base_w = wbase[:, :].rearrange("p (w o) -> p w o", o=1).broadcast_to([P, NW, n])
                last = nc.vector.tensor_tensor(rel[:, :, a:a + n], tiles, base_w, ALU.subtract)
            last.then_inc(rel_ready, 1)
            cols_of(0)
            cols_of(1)

            def sorted_path():
                dve.wait_ge(rel_ready, 1)
                for kt in range(NB):
                    for g in (2 * kt, 2 * kt + 1):
                        if g >= 2:
                            dve.wait_ge(win_done, g - 1)
                        if 2 <= g + 1 < NG:
                            cols_of(g + 1)
                        rows_of(g).then_inc(oh_ready, 1)
                        if g == 0:
                            first_stats(0)
                        if g == 2 * kt and kt + 1 < NB:
                            first_stats(kt + 1)
                    if kt:
                        turn_lo(0, kt - 1)

            def first_stats(kt):
                dve.wait_ge(x_ld[kt], 16)
                ln_stats(0, kt, x[:, kt, :])

            def general_path():
                dve.wait_ge(slow_consts, 8)
                nc.vector.tensor_copy(sF[:, :], sT[:, :])
                nc.vector.tensor_reduce(pairmm[:, 0:1], dst_i[:, :], AX_X, ALU.min)
                link(nc.vector.tensor_reduce(pairmm[:, 1:2], dst_i[:, :], AX_X, ALU.max))
                for c in range(2):
                    nc.vector.tensor_scalar(diag[:, c, :], ident[:, :], pairmm[:, c:c + 1], None, ALU.mult).then_inc(diag_ready, 1)
                dve.wait_ge(pair_rows, 1)
                link(nc.vector.tensor_scalar(wmask[:, 0, :], bank[3][0:NW, 0:PAIRS], wstart[:, 1:2], None, ALU.is_lt))
                link(nc.vector.scalar_tensor_tensor(wmask[:, 1, :], bank[3][0:NW, PAIRS:2 * PAIRS], wstart[:, 0:1],
                                                    wmask[:, 0, :], ALU.is_ge, ALU.mult))
                nc.vector.scalar_tensor_tensor(wsel[:, 0, :], wmask[:, 1, :], -float(PAIRS), iotap[:, 0, :], ALU.mult, ALU.add)
                link(nc.vector.tensor_tensor(wsel[:, 1, :], wmask[:, 1, :], iotap[:, 1, :], ALU.mult))
                nc.vector.tensor_reduce(wcol[:, 0:1], wsel[:, 0, :], AX_X, ALU.min)
                link(nc.vector.tensor_reduce(wcol[:, 1:2], wsel[:, 1, :], AX_X, ALU.max))
                link(nc.vector.tensor_scalar(wcol[:, 2:3], wcol[:, 0:1], float(PAIRS - 1), None, ALU.min))
                link(nc.vector.tensor_tensor(wcol[:, 3:4], wcol[:, 1:2], wcol[:, 2:3], ALU.subtract))
                nc.vector.tensor_scalar(wcol[:, 3:4], wcol[:, 3:4], 1.0, None, ALU.max).then_inc(wcol_ready, 1)
                dve.wait_ge(tab_rows, 1)
                link(nc.vector.tensor_copy(tabf[:, :], bank[3][0:1, 0:NW + 1]))
                nc.vector.tensor_copy(tab[:, 0:NW + 1], tabf[:, :]).then_inc(tab_ready, 1)
                nc.vector.tensor_tensor(tab[:, NW + 1:2 * NW + 1], bank[3][0:1, P:P + NW], tabf[:, 0:NW], ALU.subtract).then_inc(tab_ready, 1)
                dve.wait_ge(tab_ready, 2)
                for kt in range(NB):
                    for w in range(2 * WG * kt, 2 * WG * (kt + 1)):
                        first = dve.value_load(tab[0:1, w:w + 1], min_val=0, max_val=NW * PAIRS)
                        after = dve.value_load(tab[0:1, w + 1:w + 2], min_val=1, max_val=NW * PAIRS)
                        shift = dve.value_load(tab[0:1, NW + 1 + w:NW + 2 + w])
                        with dve.Fori(first, after) as v:
                            dve.wait_ge(oh_used, v + 1)
                            slot = v & (RING - 1)
                            for h in range(2):
                                tile = (v + shift) * 2 + h
                                nc.vector.tensor_scalar(oh_row[:, bass.ds(slot, 1), h, :], iotab[:, :].rearrange("p (a n) -> p a n", a=1),
                                                        wbase[:, w:w + 1], jT[:, bass.ds(tile + BEFORE, 1)], ALU.add, ALU.is_equal)
                                last = nc.vector.tensor_scalar(oh_col[:, bass.ds(slot, 1), h, :], iotab[:, :].rearrange("p (a n) -> p a n", a=1),
                                                               sF[:, bass.ds(tile, 1)], None, ALU.is_equal)
                            last.then_inc(oh_ready, 1)
                    if kt == 0:
                        first_stats(0)
                    if kt + 1 < NB:
                        first_stats(kt + 1)
                    if kt:
                        turn_lo(0, kt - 1)

            dve.wait_ge(path_ready, 1)
            other = dve.value_load(unsorted[0:1, 0:1], min_val=0, max_val=1)
            with dve.If(other > 0):
                new_chain()
                general_path()
            with dve.Else():
                new_chain()
                sorted_path()
            new_chain()
            turn_lo(0, NB - 1)

            for g in (NG - 2, NG - 1):
                dve.wait_ge(win_placed[g % 4], 16 * WG * (g // 4 + 1))
            nc.vector.tensor_scalar(B[:, NB - 1, :], AT[:, NB - 1, :].bitcast(F32), 1.0, None, ALU.min).then_inc(b_ready, 1)

            dve.wait_ge(xb_ready, NB)
            for m in range(NB + 1):
                if m < NB:
                    dve.wait_ge(bt_done, m + 1)
                    nc.vector.scalar_tensor_tensor(S[:, m, :], B[:, m, :], 1.0, bank[BT_BANKS[m % 4]][:, :].bitcast(BF16), ALU.mult, ALU.max,
                                                   accum_out=degs[:, ROWSUM, m:m + 1]).then_inc(s_rows, 1)
                if m:
                    dve.wait_ge(y_hi_ready, m)
                    nc.vector.scalar_tensor_tensor(y_lo[:, m - 1, :], y[:, m - 1, :], degs[:, DINV0, m - 1:m], y_hi[:, m - 1, :].bitcast(F32),
                                                   ALU.mult, ALU.subtract).then_inc(y_lo_ready, 1)
            for m in range(NB + 2):
                if m < NB:
                    dve.wait_ge(gcn_done, m + 1)
                    dve.wait_ge(xb_ready, m + 1)
                    nc.vector.scalar_tensor_tensor(x[:, m, :], bank[GCN_BANKS[m % 4]][:, :], degs[:, DINV0, m:m + 1], x[:, m, :],
                                                   ALU.mult, ALU.add).then_inc(gcn_kept, 1)
                    dve.wait_ge(gcn_kept, m + 1)
                    ln_stats(1, m, x[:, m, :])
                if m >= 2:
                    turn_lo(1, m - 2)

            def hidden_hi(n, i, j):
                dve.wait_ge(relu_done, n + 1)
                f, half = j % FB, j // FB
                nc.vector.tensor_copy(h_hi[i][:, f, half * 512:half * 512 + 512], hrelu[:, j % 2, :]).then_inc(hhi_done, 1)

            for j in range(3):
                hidden_hi(j, 0, j)

            dve.wait_ge(gate_turned, 1)
            logits = bank[4][:, 0:16 * NB].rearrange("p (m c) -> p m c", m=NB)
            link(nc.vector.tensor_tensor(gate[:, :, :], logits[:, :, 0:8],
                                         bgb[:, :].rearrange("p (o n) -> p o n", o=1).broadcast_to([P, NB, 8]), ALU.add))
            last = nc.vector.tensor_tensor(gate[:, :, :], logits[:, :, 8:16], gate[:, :, :], ALU.add)
            link(last)
            for m in range(NB):
                last = nc.vector.max(top8[:, m, :], gate[:, m, :])
            link(last)
            for m in range(NB):
                last = nc.vector.max_index(top8i[:, m, :], top8[:, m, :], gate[:, m, :])
            nc.vector.tensor_tensor(pair[:, 0, :], top8[:, :, 1], top8[:, :, 0], ALU.subtract).then_inc(topdiff, 1)
            link(nc.vector.engine_nop())
            nc.vector.tensor_copy(topi[:, :, :], top8i[:, :, 0:2])
            hidden_hi(3, 0, 3)
            dve.wait_ge(topexp, 1)
            link(nc.vector.tensor_scalar(pair[:, 2, :], pair[:, 1, :], 1.0, None, ALU.add))
            link(nc.vector.reciprocal(pair[:, 3, :], pair[:, 2, :]))
            link(nc.vector.tensor_tensor(pair[:, 4, :], pair[:, 1, :], pair[:, 3, :], ALU.mult))
            for m in range(NB):
                nc.vector.tensor_scalar(sel1[:, m, :], iota8[:, :], topi[:, m, 0:1], pair[:, 3, m:m + 1], ALU.is_equal, ALU.mult)
                last = nc.vector.tensor_scalar(sel2[:, m, :], iota8[:, :], topi[:, m, 1:2], pair[:, 4, m:m + 1], ALU.is_equal, ALU.mult)
            link(last)
            nc.vector.tensor_tensor(comb[:, :, 0:8], sel1[:, :, :], sel2[:, :, :], ALU.add).then_inc(comb_ready, 1)
            dve.wait_ge(comb_ready, 1)
            nc.vector.tensor_scalar(comb2[:, :, :], comb[:, :, :], 2.0, None, ALU.mult).then_inc(comb2_ready, 1)

            for j in range(4):
                hidden_hi(4 + j, 1, j)

            def expert_added(e, m):
                dve.wait_ge(moe_done, NB * e + m + 1)
                if isinstance(e, int):
                    weight = comb[:, m, e:e + 1]
                else:
                    weight = comb[:, m, bass.ds(e, 1)]
                nc.vector.scalar_tensor_tensor(x[:, m, :], bank[4 + m % 2][:, :], weight, x[:, m, :], ALU.mult, ALU.add).then_inc(moe_added, 1)

            def block_max(m):
                return nc.vector.tensor_reduce(block_maxs[:, m:m + 1], AT[:, m, :].bitcast(F32), AX_X, ALU.max)

            def moe_step(e, i, max_of_AT=False):
                for j in range(4):
                    hidden_hi(4 * (e + 1) + j, 1 - i, j)
                    if max_of_AT:
                        for n in ((0, 1), (2, 3), (4,), (5,))[j]:
                            block_max(n)
                for m in range(NB):
                    expert_added(e, m)
                    if max_of_AT and m == 3:
                        block_max(6)
                    if max_of_AT and m == 5:
                        link(block_max(7))
                        nc.vector.tensor_reduce(mult_max, block_maxs, AX_X, ALU.max).then_inc(degmax_ready, 1)

            for m in range(NB):
                expert_added(0, m)
            with dve.Fori(0, 3) as t:
                moe_step(2 * t + 1, 1)
                moe_step(2 * t + 2, 0)
            moe_step(7, 1, max_of_AT=True)
            for m in range(NB + 2):
                if m < NB:
                    expert_added(NE - 1, m)
                    dve.wait_ge(moe_added, (NE - 1) * NB + m + 1)
                    ln_stats(2, m, x[:, m, :])
                if m == 3:
                    dve.wait_ge(big_all, 1)
                    nc.vector.tensor_scalar(bigflag[0:1, 0:1], mult_max_all[0:1, :], float(EXACT), None, ALU.is_gt).then_inc(big_ready, 1)
                if m >= 2:
                    turn_lo(2, m - 2)

            def take_xw(s, m, i):
                dve.wait_ge(xw_done, NB * s + m + 1)
                nc.vector.tensor_tensor(b[i][:, m, :], bank[m % 4][:, :], b[i][:, m, :], ALU.subtract).then_inc(xw_taken, 1)

            def propagate(s, m, i, factor, banks=4):
                dve.wait_ge(prop_done, NB * (s - 1) + m + 1)
                dve.wait_ge(xw_taken, NB * s + m + 1)
                return nc.vector.scalar_tensor_tensor(b[i][:, m, :], bank[4 + m % banks][:, :], degs[:, factor, m:m + 1], b[i][:, m, :],
                                                      ALU.mult, ALU.add).then_inc(b_done, 1)

            def scaled_lo(s, m, i):
                dve.wait_ge(chi_done, NB * s + m + 1)
                nc.vector.scalar_tensor_tensor(c_lo[i][:, m, :], b[i][:, m, :], degs[:, DINV1, m:m + 1], c_hi[i][:, m, :].bitcast(F32),
                                               ALU.mult, ALU.subtract).then_inc(clo_done, 1)

            dve.wait_ge(deg1_done, 1)
            nc.vector.tensor_scalar(degs[:, DEG_POS, :], bank[4][:, 0:NB], 0.0, None, ALU.is_gt)
            nc.vector.tensor_scalar(degs[:, DEG1, :], bank[4][:, 0:NB], 1e-30, None, ALU.max).then_inc(deg1_kept, 1)
            dve.wait_ge(deg1_pow, 1)
            link(nc.vector.tensor_tensor(degs[:, DINV1, :], degs[:, DINV1, :], degs[:, DEG_POS, :], ALU.mult))
            nc.vector.tensor_scalar(degs[:, M2_DINV1, :], degs[:, DINV1, :], -2.0, None, ALU.mult)
            nc.vector.tensor_scalar(degs[:, NEG_DINV1, :], degs[:, DINV1, :], -1.0, None, ALU.mult).then_inc(dinv1_ready, 1)
            dve.wait_ge(dinv1_ready, 1)
            for m in range(NB + 1):
                if m < NB:
                    dve.wait_ge(xw_done, m + 1)
                    nc.vector.tensor_copy(b[0][:, m, :], bank[m % 4][:, :]).then_inc(b_done, 1)
                    dve.wait_ge(b_done, m + 1)
                    nc.vector.engine_nop().then_inc(xw_taken, 1)
                if m:
                    scaled_lo(0, m - 1, 0)

            def cheb_step(s, i):
                take_xw(s, 0, i)
                take_xw(s, 1, i)
                for m in range(NB):
                    propagate(s, m, i, M2_DINV1)
                    if m + 2 < NB:
                        take_xw(s, m + 2, i)
                    if m:
                        scaled_lo(s, m - 1, i)
                scaled_lo(s, NB - 1, i)

            dve.wait_ge(b_zero, 1)
            with dve.Fori(0, 3) as t:
                for j in range(2):
                    cheb_step(2 * t + 1 + j, 1 - j)

            def round_pair(pair_no, stages, outs, values, tmp, done, ready, ready_count):
                for stage_no in stages:
                    for c in range(2):
                        v, (exps, mags, sums) = values[c], tmp[c]
                        if stage_no == 0:
                            dve.wait_ge(ready, ready_count + c)
                            if pair_no:
                                dve.wait_ge(round_step, 6 * pair_no)
                            op = nc.vector.tensor_scalar(exps[:, :, :].bitcast(I32), v.bitcast(I32), 0x7F800000, None, ALU.bitwise_and)
                        else:
                            dve.wait_ge(round_step, 6 * pair_no + 2 * (stage_no - 1) + c + 1)
                        if stage_no == 1:
                            op = nc.vector.tensor_scalar(mags[:, :, :], exps[:, :, :], 2.0 ** -6, MAGIC, ALU.max, ALU.mult)
                        if stage_no == 2:
                            op = nc.vector.scalar_tensor_tensor(sums[:, :, :], v, -FP8_MAX, mags[:, :, :], ALU.max, ALU.add)
                        if stage_no == 3:
                            op = nc.vector.scalar_tensor_tensor(outs[c], sums[:, :, :], 256.0 * MAGIC + FP8_MAX, mags[:, :, :],
                                                                ALU.min, ALU.subtract)
                        op.then_inc(done if stage_no == 3 else round_step, 1)

            def scale_of(amax_all, scale, guarded):
                link(nc.vector.tensor_scalar(guarded, amax_all, 1e-12, None, ALU.max))
                link(nc.vector.reciprocal(scale, guarded))
                return nc.vector.tensor_scalar(scale, scale, FP8_MAX, None, ALU.mult)

            def round_weights(n, stages):
                ks = [slice(2 * n + c, 2 * n + c + 1) for c in range(2)]
                if n and stages[0] == 0:
                    dve.wait_ge(wq_ready, 2)
                round_pair(n, stages, [wq[:, k, :] for k in ks], [wc_raw[:, k, :] for k in ks], qtmp_w, wq_ready, w_scaled, 2 * n + 1)

            def round_x(half):
                cols = [slice(c * 2 * P, (c + 1) * 2 * P) for c in (2 * half, 2 * half + 1)]
                dve.wait_ge(wq_ready, KD)
                if half:
                    dve.wait_ge(xq_ready, 2)
                round_pair(2 + half, range(4), [xq[:, :, c] for c in cols], [xhT[:, :, c] for c in cols], qtmp_x, xq_ready, x_scaled,
                           2 * half + 1)

            S7 = KC - 1

            def add_x(m):
                dve.wait_ge(xw_taken, NB * S7 + m + 1)
                dve.wait_ge(xr_ready, m + 1)
                nc.vector.tensor_tensor(b[1][:, m, :], b[1][:, m, :], xr[:, m, :], ALU.add).then_inc(x_added, 1)

            take_xw(S7, 0, 1)
            take_xw(S7, 1, 1)
            add_x(0)
            add_x(1)
            dve.wait_ge(wc_ld, 16 * (KC + 1))
            nc.vector.tensor_reduce(w_amax, wc_raw[:, :, :].rearrange("p k n -> p (k n)"), AX_X, ALU.max,
                                    apply_absolute_value=True).then_inc(wamax, 1)
            for m in range(NB + 1):
                if m < NB:
                    dve.wait_ge(x_added, m + 1)
                    propagate(S7, m, 1, NEG_DINV1, banks=2)
                    dve.wait_ge(b_done, NB * S7 + m + 1)
                    ln_stats(3, m, b[1][:, m, :])
                    if m + 2 < NB:
                        take_xw(S7, m + 2, 1)
                        add_x(m + 2)
                if m == 0:
                    dve.wait_ge(wamax_all, 1)
                    scale_of(w_amax_all, w_scale, w_unscale).then_inc(wscale_ready, 1)
                if m:
                    dve.wait_ge(ln_norm[3], m)
                    nc.vector.tensor_reduce(block_maxs[:, m - 1:m], xh[:, (m - 1) % 2, :], AX_X, ALU.max,
                                            apply_absolute_value=True).then_inc(block_amax, 1)
                if 1 <= m < 5:
                    round_weights((m - 1) // 2, (range(2), range(2, 4))[(m - 1) % 2])
            dve.wait_ge(block_amax, NB)
            nc.vector.tensor_reduce(x_amax, block_maxs, AX_X, ALU.max).then_inc(xamax, 1)
            link(nc.vector.reciprocal(w_unscale, w_scale))
            dve.wait_ge(xamax_all, 1)
            scale_of(x_amax_all, x_scale, x_unscale).then_inc(xscale_ready, 1)
            dve.wait_ge(xscale_ready, 1)
            link(nc.vector.reciprocal(x_unscale, x_scale))
            nc.vector.tensor_tensor(out_scale, x_unscale, w_unscale, ALU.mult).then_inc(xscale_ready, 1)
            for half in range(HALVES):
                round_x(half)
            dve.wait_ge(xscale_ready, 2)
            for m in range(4, NB):
                dve.wait_ge(fp8_done, m + 1)
                nc.vector.scalar_tensor_tensor(b[1][:, m, :], bank[m][:, :], out_scale, b[1][:, m, :],
                                               ALU.mult, ALU.add).then_inc(out_ready, 1)

        @block.tensor
        def _(pe):
            def mm(out_ap, lhsT, rhs, start, stop):
                return nc.tensor.matmul(out_ap, lhsT, rhs, start=start, stop=stop)

            def product(out_ap, terms):
                for n, (a, c) in enumerate(terms):
                    last = mm(out_ap, a, c, n == 0, n == len(terms) - 1)
                return last

            def turn(i, m):
                pe.wait_ge(ln_norm[i], m + 1)
                if m >= 2:
                    pe.wait_ge(ln_lo[i] if i < 3 else xT_kept, m - 1)
                for k in range(KD):
                    last = nc.tensor.transpose(bank[6 + m % 2][:, k * P:(k + 1) * P], xh[:, m % 2, k * P:(k + 1) * P], ident[:, :])
                last.then_inc(ln_turned[i], 1)

            def x_times(w_hi_ap, w_lo_ap, m):
                rows = slice(m * P, (m + 1) * P)
                t = []
                for k in range(KD):
                    t.append((xT_hi[:, k, rows], w_hi_ap[:, k, :]))
                    t.append((xT_hi[:, k, rows], w_lo_ap[:, k, :]))
                    t.append((xT_lo[:, k, rows], w_hi_ap[:, k, :]))
                return t

            pe.wait_ge(consts, 11)
            pe.wait_ge(idx_rows, 2)
            for c, rows in enumerate((joint, slo)):
                for h in range(2):
                    last = nc.tensor.transpose(bank[2][:, (2 * c + h) * P:(2 * c + h + 1) * P], rows[:, h * P:(h + 1) * P], ident[:, :])
            last.then_inc(idx_turned, 1)
            pe.wait_ge(off_ready, 1)
            nc.tensor.transpose(bank[3][0:1, 0:P], off[:, 0:1], ident[:, :]).then_inc(off_row, 1)

            def y_block(m):
                pe.wait_ge(ln_lo[0], m + 1)
                pe.wait_ge(ln_hi[0], m + 1)
                if m == 0:
                    pe.wait_ge(w0_split, 2)
                if m >= 2:
                    pe.wait_ge(y_kept, m - 1)
                product(bank[4 + m % 2][:, :], x_times(w0_hi, w0_lo, m)).then_inc(y_done, 1)

            def between(kt):
                turn(0, kt)
                if kt:
                    y_block(kt - 1)

            def sorted_path():
                for kt in range(NB):
                    for g in (2 * kt, 2 * kt + 1):
                        if g >= 4:
                            pe.wait_ge(win_staged, g - 3)
                        pe.wait_ge(oh_ready, g + 1)
                        if g + 1 >= ACT_FROM:
                            pe.wait_ge(act_cols, min(g + 1, NG - 1) - ACT_FROM + 1)
                        for q in range(WG):
                            w = g * WG + q
                            t = []
                            for i in range(VIS):
                                tile = TPW * w - BEFORE + i
                                if 0 <= tile < TILES:
                                    c, n = tile // CHUNK, tile % CHUNK
                                    t.append((oh_rows[g % 2][:, (q * VIS + i) // 2, :, i % 2],
                                              oh_cols[c % 5][:, n // 2, :, n % 2]))
                            last = product(bank[g % 4][:, q * SL:(q + 1) * SL], t)
                        last.then_inc(win_done, 1)
                    between(kt)

            def general_path():
                pe.wait_ge(slow_consts, 8)
                pe.wait_ge(diag_ready, 2)
                mm(bank[3][0:NW, 0:2 * PAIRS], ones_w[:, :], diag[:, :, :], True, True).then_inc(pair_rows, 1)
                pe.wait_ge(wcol_ready, 1)
                mm(bank[3][0:1, 0:NW + 1], wcol[:, 3:4], tri[:, :], True, True)
                mm(bank[3][0:1, P:P + NW], wcol[:, 2:3], ident[0:NW, 0:NW], True, True).then_inc(tab_rows, 1)
                pe.wait_ge(tab_ready, 2)
                for kt in range(NB):
                    for g in (2 * kt, 2 * kt + 1):
                        if g >= 4:
                            pe.wait_ge(win_staged, g - 3)
                        for q in range(WG):
                            w = g * WG + q
                            sums = bank[g % 4][:, q * SL:(q + 1) * SL]
                            mm(sums, zerob[:, :], iotab[:, :], True, False)
                            first = pe.value_load(tab[0:1, w:w + 1], min_val=0, max_val=NW * PAIRS)
                            after = pe.value_load(tab[0:1, w + 1:w + 2], min_val=1, max_val=NW * PAIRS)
                            with pe.Fori(first, after) as v:
                                pe.wait_ge(oh_ready, v + 1)
                                slot = v & (RING - 1)
                                for h in range(2):
                                    last = mm(sums, oh_row[:, bass.ds(slot, 1), h, :], oh_col[:, bass.ds(slot, 1), h, :], False, False)
                                last.then_inc(oh_used, 1)
                            last = mm(sums, zerob[:, :], iotab[:, :], False, True)
                        last.then_inc(win_done, 1)
                    between(kt)

            pe.wait_ge(idx_kept, 3)
            pe.wait_ge(path_ready, 1)
            other = pe.value_load(unsorted[0:1, 0:1], min_val=0, max_val=1)
            with pe.If(other > 0):
                general_path()
            with pe.Else():
                sorted_path()
            y_block(NB - 1)

            pe.wait_ge(b_ready, NB)
            pe.wait_ge(win_staged, NG)

            def turn_B(m):
                if m >= 4:
                    pe.wait_ge(s_rows, m - 3)
                for j in range(NB):
                    last = nc.tensor.transpose(bank[BT_BANKS[m % 4]][:, :].bitcast(BF16)[:, j * P:(j + 1) * P], B[:, j, m * P:(m + 1) * P], identb[:, :])
                last.then_inc(bt_done, 1)

            def gcn_terms(k, m):
                rows, sums = slice(m * P, (m + 1) * P), bank[GCN_BANKS[m % 4]][:, :]
                mm(sums, S[:, k, rows], y_hi[:, k, :], k == 0, False)
                return mm(sums, S[:, k, rows], y_lo[:, k, :], False, k == NB - 1)

            pe.wait_ge(ln_lo[0], NB)
            for m in range(4):
                turn_B(m)
            pe.wait_ge(y_kept, NB)
            for k in range(NB):
                pe.wait_ge(s_ready, k + 1)
                pe.wait_ge(y_hi_ready, k + 1)
                pe.wait_ge(y_lo_ready, k + 1)
                for m in range(4):
                    last = gcn_terms(k, m)
                    if k == NB - 1:
                        last.then_inc(gcn_done, 1)
                if k + 4 < NB:
                    turn_B(k + 4)
            for m in range(4, NB):
                pe.wait_ge(gcn_kept, m - 3)
                for k in range(NB):
                    last = gcn_terms(k, m)
                last.then_inc(gcn_done, 1)
                turn(1, m - 4)

            def hidden_part(i, j):
                f, half = j % FB, j // FB
                cols, fs = slice(half * 512, half * 512 + 512), slice(f * P, (f + 1) * P)
                t = []
                for k in range(KD):
                    t.append((w_hi[i][0][:, k, fs], xT_hi[:, k, cols]))
                    t.append((w_hi[i][0][:, k, fs], xT_lo[:, k, cols]))
                    t.append((w_lo[i][0][:, k, fs], xT_hi[:, k, cols]))
                product(bank[j][:, :], t).then_inc(h_done, 1)

            def hidden(e, i):
                pe.wait_ge(whi_done[0], e + 1)
                pe.wait_ge(wlo_done[0], e + 1)
                for j in range(4):
                    pe.wait_ge(relu_done, 4 * (e - 1) + j + 1)
                    hidden_part(i, j)

            def gate_logits(half):
                cols = slice(half * 512, half * 512 + 512)
                for k in range(KD):
                    mm(bank[2 + half][0:16, :], wg_hilo[:, k, :], xT_hi[:, k, cols], k == 0, False)
                    last = mm(bank[2 + half][0:8, :], wg_hilo[:, k, 0:8], xT_lo[:, k, cols], False, k == KD - 1)
                last.then_inc(gate_done, 1)

            def expert_out(e, i, last=False):
                pe.wait_ge(whi_done[1], e + 1)
                pe.wait_ge(wlo_done[1], e + 1)
                for m in range(NB):
                    if m % 4 == 0:
                        pe.wait_ge(hlo_done, 4 * e + 2 + m // 2)
                    if isinstance(e, int) and e == 0:
                        if m == 0:
                            pe.wait_ge(comb_ready, 1)
                        if m >= 2:
                            pe.wait_ge(moe_added, m - 1)
                    else:
                        pe.wait_ge(moe_added, NB * e + m - 1)
                    rows = slice(m * P, (m + 1) * P)
                    t = []
                    for f in range(FB):
                        t.append((h_hi[i][:, f, rows], w_hi[i][1][:, f, :]))
                        t.append((h_hi[i][:, f, rows], w_lo[i][1][:, f, :]))
                        t.append((h_lo[i][:, f, rows], w_hi[i][1][:, f, :]))
                    if last:
                        t.append((combT[0:CK, rows], b2_parts[0:CK, :]))
                    product(bank[4 + m % 2][:, :], t).then_inc(moe_done, 1)
                    if last and m >= 2:
                        turn(2, m - 2)

            turn(1, 4)
            pe.wait_ge(wg_split, 1)
            pe.wait_ge(ln_lo[1], 4)
            gate_logits(0)
            turn(1, 5)
            pe.wait_ge(whi_done[0], 1)
            pe.wait_ge(wlo_done[0], 1)
            pe.wait_ge(gcn_kept, 5)
            hidden_part(0, 0)
            turn(1, 6)
            turn(1, 7)
            pe.wait_ge(gcn_kept, 6)
            hidden_part(0, 1)
            pe.wait_ge(ln_lo[1], NB)
            gate_logits(1)
            pe.wait_ge(gate_kept, 1)
            hidden_part(0, 2)
            pe.wait_ge(gate_kept, 2)
            pe.wait_ge(gcn_kept, NB)
            for m in range(NB):
                last = nc.tensor.transpose(bank[4][:, 16 * m:16 * m + 16], gate_rows[:, m * P:(m + 1) * P], ident[0:16, 0:16])
            last.then_inc(gate_turned, 1)
            hidden_part(0, 3)
            hidden(1, 1)
            expert_out(0, 0)
            with pe.Fori(0, 3) as t:
                hidden(2 * t + 2, 0)
                expert_out(2 * t + 1, 1)
                hidden(2 * t + 3, 1)
                expert_out(2 * t + 2, 0)
            pe.wait_ge(comb_parts_ready, 3)
            for g in range(2):
                for m in range(4 * g, 4 * g + 4):
                    last = nc.tensor.transpose(bank[6 + g][0:CK, (m % 4) * P:(m % 4 + 1) * P], comb_parts[:, m, :].bitcast(F32), ident[:, :])
                last.then_inc(combT_done, 1)
            hidden(8, 0)
            expert_out(7, 1)
            pe.wait_ge(combT_kept, 2)
            pe.wait_ge(b2_ready, 1)
            expert_out(8, 0, last=True)

            def xw(s, m, i):
                if m == 0:
                    pe.wait_ge(wchi_done, s + 1)
                    pe.wait_ge(wclo_done, s + 1)
                if isinstance(s, int) and s == 0:
                    pe.wait_ge(ln_lo[2], m + 1)
                    if m >= 4:
                        pe.wait_ge(b_done, m - 3)
                else:
                    pe.wait_ge(xw_taken, NB * s + m - 3)
                product(bank[m % 4][:, :], x_times(wc_hi[i], wc_lo[i], m)).then_inc(xw_done, 1)

            def prop(s, m, i, cast, banks):
                pe.wait_ge(clo_done, NB * s)
                if m >= banks:
                    pe.wait_ge(b_done, NB * s + m - banks + 1)
                rows = slice(m * P, (m + 1) * P)
                t = [(cast(AT[:, k, rows]), cast(part[:, k, :])) for k in range(NB) for part in (c_hi[i], c_lo[i])]
                product(bank[4 + m % banks][:, :], t).then_inc(prop_done, 1)

            def cheb(cast):
                for half in range(HALVES):
                    product(bank[2 + half][0:2, :], [(cast(onecol[:, :]), cast(AT[:, k, half * 512:half * 512 + 512])) for k in range(NB)])\
                        .then_inc(deg_rows, 1)
                turn(2, NB - 2)
                turn(2, NB - 1)
                xw(0, 0, 0)
                pe.wait_ge(deg_rows_kept, 2)
                pe.wait_ge(moe_added, NE * NB)
                for m in range(NB):
                    last = nc.tensor.transpose(bank[4][:, m:m + 1], deg_row[:, m * P:(m + 1) * P], ident[0:1, 0:1])
                last.then_inc(deg1_done, 1)
                for m in range(1, NB):
                    xw(0, m, 0)
                pe.wait_ge(deg1_kept, 1)

                def step(s, i, final=False):
                    xw(s, 0, i)
                    xw(s, 1, i)
                    for m in range(NB):
                        prop(s, m, 1 - i, cast, 2 if final else 4)
                        if m + 2 < NB:
                            xw(s, m + 2, i)
                        if final and m >= 2:
                            turn(3, m - 2)

                with pe.Fori(0, 3) as t:
                    for j in range(2):
                        step(2 * t + 1 + j, 1 - j)
                step(KC - 1, 1, final=True)

            pe.wait_ge(big_ready, 1)
            big = pe.value_load(bigflag[0:1, 0:1], min_val=0, max_val=1)
            with pe.If(big > 0):
                cheb(lambda ap: ap.bitcast(F32))
            with pe.Else():
                cheb(lambda ap: ap)

            turn(3, NB - 2)
            turn(3, NB - 1)
            pe.wait_ge(wq_ready, KD)
            for m in range(NB):
                pe.wait_ge(xq_ready, m // 2 + 1)
                product(bank[m][:, :], [(xq[:, k, m * P:(m + 1) * P], wq[:, k, :]) for k in range(KD)]).then_inc(fp8_done, 1)


def kernel(x, src, dst, L0_gnn_weight, L0_gnn_bias, L0_ffn_Wg, L0_ffn_bg, L0_ffn_W1, L0_ffn_b1,
           L0_ffn_W2, L0_ffn_b2, L0_ffn_Ws1, L0_ffn_bs1, L0_ffn_Ws2, L0_ffn_bs2,
           L1_gnn_weight, L1_gnn_bias, L1_ffn_weight):
    import numpy as np
    import concourse.bacc as bacc
    from concourse.bass_utils import run_bass_kernel_spmd

    rows = lambda a: np.asarray(a)
    arrays = {
        "x_in": rows(x),
        "src_in": rows(src).reshape(PAIRS, 2 * P),
        "dst_in": rows(dst).reshape(PAIRS, 2 * P),
        "w0_in": rows(L0_gnn_weight),
        "bias0_in": rows(L0_gnn_bias),
        "wg_in": rows(L0_ffn_Wg),
        "bg_in": rows(L0_ffn_bg),
        "w1_in": np.concatenate([rows(L0_ffn_W1), rows(L0_ffn_Ws1)[None]]),
        "b1_in": np.concatenate([rows(L0_ffn_b1), rows(L0_ffn_bs1)[None]]).reshape(NE * FB, P).T,
        "w2_in": np.concatenate([rows(L0_ffn_W2), rows(L0_ffn_Ws2)[None]]),
        "b2_in": np.concatenate([rows(L0_ffn_b2), rows(L0_ffn_bs2)[None]]),
        "wc_in": rows(L1_gnn_weight)[::-1],
        "bias1_in": rows(L1_gnn_bias),
        "wf_in": rows(L1_ffn_weight),
    }
    arrays = {n: np.ascontiguousarray(a) for n, a in arrays.items()}
    nc = bacc.Bacc("TRN2", target_bir_lowering=False, num_devices=1)
    aps = [nc.dram_tensor(n, a.shape, mybir.dt.from_np(a.dtype), kind="ExternalInput").ap() for n, a in arrays.items()]
    out = nc.dram_tensor("out", [N, D], F32, kind="ExternalOutput").ap()
    build(nc, *aps, out)
    r = run_bass_kernel_spmd(nc, [arrays], core_ids=[0])
    return r.results[0]["out"]
```
